# Optimizing a Trainium2 kernel written in Bass

```python
import numpy as np
import jax
import jax.numpy as jnp

def _softmax(x, axis=-1):
    return jax.nn.softmax(x, axis=axis)

def _gelu(x):
    return jax.nn.gelu(x, approximate=True)

def _silu(x):
    return jax.nn.silu(x)

def _sigmoid(x):
    return jax.nn.sigmoid(x)

def _layernorm(x, axis=-1, eps=1e-05):
    m = jnp.mean(x, axis=axis, keepdims=True)
    v = jnp.var(x, axis=axis, keepdims=True)
    return (x - m) / jnp.sqrt(v + eps)

def _scatter_add(tgt, idx, src, axis=0):
    return tgt.at[idx].add(src)

def _segment_sum(src, seg, n):
    return jax.ops.segment_sum(src, seg, n)
kernel_name = 'mk_recurrent_d2_jaxref_r4_9104bf'

def setup_inputs(seed: int=0):
    np.random.seed(seed)
    _w = jnp.asarray

    def _L0_attn_setup():
        import jax, jax.numpy as jnp
        import numpy as np
        B, L, D, H = (2, 512, 256, 16)
        Dh = D // H
        key = jax.random.key(seed)
        kx, kq, kk, kv, ko = jax.random.split(key, 5)
        scale = 1.0 / np.sqrt(D)
        return {'x': jax.random.normal(kx, (B, L, D), dtype=jnp.float32), 'Wq': jax.random.normal(kq, (D, H, Dh), dtype=jnp.float32) * scale, 'Wk': jax.random.normal(kk, (D, H, Dh), dtype=jnp.float32) * scale, 'Wv': jax.random.normal(kv, (D, H, Dh), dtype=jnp.float32) * scale, 'Wout': jax.random.normal(ko, (H, Dh, D), dtype=jnp.float32) * (1.0 / np.sqrt(D))}
    _L0_attn_in = _L0_attn_setup()

    def _L0_ffn_setup():
        import jax, jax.numpy as jnp
        import numpy as np
        E = 8
        K = 2
        CF = 1.25
        key = jax.random.key(seed)
        kx, kr, kg, ku, kd = jax.random.split(key, 5)
        D, F = (256, 1024)
        x = jax.random.normal(kx, (4, 512, D), dtype=jnp.float32)
        router_w = 0.02 * jax.random.normal(kr, (E, D), dtype=jnp.float32)
        wg = jax.random.normal(kg, (E, D, F), dtype=jnp.float32) / np.sqrt(D)
        wu = jax.random.normal(ku, (E, D, F), dtype=jnp.float32) / np.sqrt(D)
        wd = jax.random.normal(kd, (E, F, D), dtype=jnp.float32) / np.sqrt(F)
        return {'x': x, 'router_w': router_w, 'wg': wg, 'wu': wu, 'wd': wd}
    _L0_ffn_in = _L0_ffn_setup()

    def _L1_attn_setup():
        import jax, jax.numpy as jnp
        import numpy as np
        key = jax.random.key(seed)
        ks = jax.random.split(key, 5)
        Bsz, T, d = (8, 512, 256)
        x = jax.random.normal(ks[0], (Bsz, T, d), dtype=jnp.float32)
        W_in = jax.random.normal(ks[1], (d, d), dtype=jnp.float32) * (1.0 / np.sqrt(d))
        b_in = jnp.zeros((d,), dtype=jnp.float32)
        log_A = -jnp.ones((d,), dtype=jnp.float32)
        B_vec = jax.random.normal(ks[2], (d,), dtype=jnp.float32) * 0.05
        C = jax.random.normal(ks[3], (d, d), dtype=jnp.float32) * 0.05
        D = jnp.zeros((d,), dtype=jnp.float32)
        return {'x': x, 'W_in': W_in, 'b_in': b_in, 'log_A': log_A, 'B_vec': B_vec, 'C': C, 'D': D}
    _L1_attn_in = _L1_attn_setup()

    def _L1_ffn_setup():
        import jax, jax.numpy as jnp
        import numpy as np
        DIM = 256
        HIDDEN = 768
        SCALE = 1.0 / 127.0

        def _dequant(w_int, dtype):
            return w_int.astype(dtype) * jnp.asarray(SCALE, dtype)
        key = jax.random.key(seed)
        k_x, k_g, k_u, k_d = jax.random.split(key, 4)
        x = jax.random.normal(k_x, (4, 512, DIM), dtype=jnp.float32)
        w_gate = jax.random.randint(k_g, (HIDDEN, DIM), -127, 128, dtype=jnp.int32)
        w_up = jax.random.randint(k_u, (HIDDEN, DIM), -127, 128, dtype=jnp.int32)
        w_down = jax.random.randint(k_d, (DIM, HIDDEN), -127, 128, dtype=jnp.int32)
        return {'x': x, 'w_gate': w_gate, 'w_up': w_up, 'w_down': w_down}
    _L1_ffn_in = _L1_ffn_setup()
    _d = {'L0_attn_x': _L0_attn_in['x'], 'L0_attn_Wq': _L0_attn_in['Wq'], 'L0_attn_Wk': _L0_attn_in['Wk'], 'L0_attn_Wv': _L0_attn_in['Wv'], 'L0_attn_Wout': _L0_attn_in['Wout'], 'L0_ffn_router_w': _L0_ffn_in['router_w'], 'L0_ffn_wg': _L0_ffn_in['wg'], 'L0_ffn_wu': _L0_ffn_in['wu'], 'L0_ffn_wd': _L0_ffn_in['wd'], 'L1_attn_W_in': _L1_attn_in['W_in'], 'L1_attn_b_in': _L1_attn_in['b_in'], 'L1_attn_log_A': _L1_attn_in['log_A'], 'L1_attn_B_vec': _L1_attn_in['B_vec'], 'L1_attn_C': _L1_attn_in['C'], 'L1_attn_D': _L1_attn_in['D'], 'L1_ffn_w_gate': _L1_ffn_in['w_gate'], 'L1_ffn_w_up': _L1_ffn_in['w_up'], 'L1_ffn_w_down': _L1_ffn_in['w_down']}
    _x0 = _d['L0_attn_x']
    _d['L0_attn_x'] = jax.random.normal(jax.random.fold_in(jax.random.key(seed), 1), (4, 1024, 256), dtype=_x0.dtype)
    del _x0
    return _d

def reference(L0_attn_x, L0_attn_Wq, L0_attn_Wk, L0_attn_Wv, L0_attn_Wout, L0_ffn_router_w, L0_ffn_wg, L0_ffn_wu, L0_ffn_wd, L1_attn_W_in, L1_attn_b_in, L1_attn_log_A, L1_attn_B_vec, L1_attn_C, L1_attn_D, L1_ffn_w_gate, L1_ffn_w_up, L1_ffn_w_down):

    def _L0_attn_ref(x, Wq, Wk, Wv, Wout):
        import jax, jax.numpy as jnp
        import numpy as np
        B, L, D, H = (2, 512, 256, 16)
        Dh = D // H
        q = jnp.einsum('bld,dhe->blhe', x, Wq)
        k = jnp.einsum('bld,dhe->blhe', x, Wk)
        v = jnp.einsum('bld,dhe->blhe', x, Wv)
        a = jnp.einsum('bqhd,bkhd->bhqk', q, k) / Dh ** 0.5
        Lq = x.shape[1]
        mask = jnp.tril(jnp.ones((1, 1, Lq, Lq), dtype=jnp.bool_))
        NEG_INF = jnp.finfo(jnp.float32).min
        a = jnp.where(mask, a, NEG_INF)
        a = jax.nn.softmax(a, axis=-1)
        o = jnp.einsum('bhqk,bkhd->bqhd', a, v)
        return jnp.einsum('blhe,hed->bld', o, Wout)

    def _L0_ffn_ref(x, router_w, wg, wu, wd):
        import jax, jax.numpy as jnp
        import numpy as np
        E = 8
        K = 2
        CF = 1.25
        B, L, D = x.shape
        xf = x.reshape(-1, D)
        N = xf.shape[0]
        capacity = max(1, int(CF * N / E))
        logits = xf @ router_w.T
        probs = jax.nn.softmax(logits, axis=-1)
        topw, topi = jax.lax.top_k(probs, K)
        topw = topw / (topw.sum(-1, keepdims=True) + 1e-06)
        fe = topi.reshape(-1)
        fw = topw.reshape(-1)
        ft = jnp.repeat(jnp.arange(N), K)
        order = jnp.lexsort((-fw, fe))
        se, sw, st = (fe[order], fw[order], ft[order])
        counts = jax.ops.segment_sum(jnp.ones_like(se), se, num_segments=E)
        starts = jnp.cumsum(counts) - counts
        rank = jnp.arange(N * K) - starts[se]
        keep = rank < capacity
        pos = jnp.where(keep, rank, capacity)
        disp = jnp.zeros((E, capacity + 1, D), x.dtype).at[se, pos].set(xf[st])
        disp = disp[:, :capacity]
        g = jnp.einsum('ecd,edf->ecf', disp, wg)
        u = jnp.einsum('ecd,edf->ecf', disp, wu)
        eo = jnp.einsum('ecf,efd->ecd', jax.nn.silu(g) * u, wd)
        gathered = eo[se, jnp.minimum(pos, capacity - 1)]
        contrib = gathered * (sw * keep.astype(x.dtype))[:, None]
        out = jnp.zeros_like(xf).at[st].add(contrib)
        return out.reshape(B, L, D)

    def _L1_attn_ref(x, W_in, b_in, log_A, B_vec, C, D):
        import jax, jax.numpy as jnp
        import numpy as np
        u = jnp.einsum('btd,de->bte', x, W_in) + b_in
        A = -jnp.exp(log_A)
        b = u * B_vec
        a = jnp.broadcast_to(A, b.shape)

        def combine(e1, e2):
            a1, b1 = e1
            a2, b2 = e2
            return (a1 * a2, b1 * a2 + b2)
        _, h_seq = jax.lax.associative_scan(combine, (a, b), axis=1)
        y = jnp.einsum('bts,sd->btd', h_seq, C)
        return y + x * D

    def _L1_ffn_ref(x, w_gate, w_up, w_down):
        import jax, jax.numpy as jnp
        import numpy as np
        DIM = 256
        HIDDEN = 768
        SCALE = 1.0 / 127.0

        def _dequant(w_int, dtype):
            return w_int.astype(dtype) * jnp.asarray(SCALE, dtype)
        wg = _dequant(w_gate, x.dtype)
        wu = _dequant(w_up, x.dtype)
        wd = _dequant(w_down, x.dtype)
        gate = jnp.einsum('bsd,hd->bsh', x, wg)
        up = jnp.einsum('bsd,hd->bsh', x, wu)
        h = jax.nn.silu(gate) * up
        return jnp.einsum('bsh,dh->bsd', h, wd)
    x = L0_attn_x
    xn = _layernorm(x, axis=-1)
    s = _L0_attn_ref(xn, L0_attn_Wq, L0_attn_Wk, L0_attn_Wv, L0_attn_Wout)
    g = _silu(_L0_ffn_ref(xn, L0_ffn_router_w, L0_ffn_wg, L0_ffn_wu, L0_ffn_wd))
    x = x + s * g
    xn = _layernorm(x, axis=-1)
    s = _L1_attn_ref(xn, L1_attn_W_in, L1_attn_b_in, L1_attn_log_A, L1_attn_B_vec, L1_attn_C, L1_attn_D)
    g = _silu(_L1_ffn_ref(xn, L1_ffn_w_gate, L1_ffn_w_up, L1_ffn_w_down))
    x = x + s * g
    return x

_drawn_inputs = setup_inputs


def setup_inputs(seed=0):
    import zlib

    import numpy as np

    out = dict(_drawn_inputs(seed))
    spreads = {'L1_attn_b_in': (0.0, 0.279), 'L1_attn_log_A': (-1.0, 0.2), 'L1_attn_D': (0.0, 0.1)}
    factors = {}
    for name, (base, spread) in spreads.items():
        noise = np.random.default_rng([zlib.crc32(name.encode()), seed]).standard_normal(out[name].shape)
        drawn = base * np.exp(spread * noise) if base else spread * noise
        out[name] = jnp.asarray(drawn.astype(out[name].dtype))
    for name, factor in factors.items():
        out[name] = (out[name] * factor).astype(out[name].dtype)
    return out
```

```python
from contextlib import ExitStack

import concourse.bass as bass
from concourse import mybir

F32 = mybir.dt.float32
F32R = mybir.dt.float32r
BF16 = mybir.dt.bfloat16
I32 = mybir.dt.int32
U32 = mybir.dt.uint32
ALU = mybir.AluOpType
ACT = mybir.ActivationFunctionType
AX = mybir.AxisListType

P = 128
BANK = 512
B, L, D = 4, 1024, 256
H, DH = 16, 16
N = B * L
NT = N // P
KC = D // P
CHUNK = 512
TPC = CHUNK // P
QUADS = H // 4
QT = L // P
PARTS = 3
VW = DH + 1
E, F = 8, 1024
FC = F // P
TOPK = 2
CAP = int(1.25 * N / E)
CT = CAP // P
EPS = 1e-5
MASKED = -1e38
TERMS = [(0, 0), (0, 1), (1, 0), (1, 1), (0, 2), (2, 0)]
STACK = len(TERMS) * DH
MAXROWS = PARTS


PRIME = 16


def prime(engine, semaphores):
    for s in semaphores:
        engine.sem_inc(s, PRIME)


class Shared:
    pass


def build_constants(nc, ctx, g):
    def sb(name, shape, dt):
        return ctx.enter_context(nc.sbuf_tensor(name, shape, dt))

    g.ident = sb("ident", [P, P], F32)
    g.identb = sb("identb", [P, P], BF16)
    g.maskneg = sb("maskneg", [P, P], BF16)
    filled = ctx.enter_context(nc.semaphore("filled"))
    cut = ctx.enter_context(nc.semaphore("cut"))
    with nc.Block() as block:
        @block.gpsimd
        def _(pool):
            nc.gpsimd.memset(g.ident[:, :], 0.0).then_inc(filled, 1)
            nc.gpsimd.memset(g.identb[:, :], 0.0).then_inc(filled, 1)
            nc.gpsimd.memset(g.maskneg[:, :], 0.0).then_inc(filled, 1)
            pool.wait_ge(filled, 3)
            for t in (g.ident, g.identb):
                nc.gpsimd.affine_select(out=t[:, :], in_=t[:, :], compare_op=ALU.not_equal, fill=1.0,
                                        base=0, pattern=[[-1, P]], channel_multiplier=1).then_inc(cut, 1)
            nc.gpsimd.affine_select(out=g.maskneg[:, :], in_=g.maskneg[:, :], compare_op=ALU.is_ge,
                                    fill=MASKED, base=0, pattern=[[-1, P]],
                                    channel_multiplier=1).then_inc(cut, 1)
            pool.wait_ge(cut, 3)


def build_project(nc, g, x, Wq, Wk, Wv, router_w):
    MC = 2 * KC
    with ExitStack() as ctx:
        def sb(name, shape, dt):
            return ctx.enter_context(nc.sbuf_tensor(name, shape, dt))

        def psum(name, shape):
            return ctx.enter_context(nc.psum_tensor(name, shape, F32))

        primed = []

        def sem(name):
            primed.append(ctx.enter_context(nc.semaphore(name)))
            return primed[-1]

        wqkv = sb("wqkv", [P, 3, KC, D], F32)
        rw = sb("rw", [E, D], F32)
        rwT = sb("rwT", [P, KC, E], F32)
        eps = sb("eps", [P, 1], F32)
        zeros = sb("zeros", [P, 4 * D], F32)
        xin = [sb(f"xin{s}", [P, TPC, D], F32) for s in range(2)]
        stats = [sb(f"stats{s}", [P, TPC, 6], F32) for s in range(2)]
        mv = [sb(f"mv{s}", [P, TPC, 2], F32) for s in range(2)]
        std = [sb(f"std{s}", [P, TPC], F32) for s in range(2)]
        rstd = [sb(f"rstd{s}", [P, TPC], F32) for s in range(2)]
        newt = [sb(f"newt{s}", [P, TPC], F32) for s in range(2)]
        xn = [sb(f"xn{s}", [P, TPC, D], F32) for s in range(2)]
        xnT = [sb(f"xnT{s}", [P, KC, CHUNK], F32) for s in range(2)]
        rest = [sb(f"rest{m}", [P, CHUNK], F32) for m in range(2)]
        parts = [sb(f"parts{s}", [P, MC, PARTS, CHUNK], BF16) for s in range(2)]
        vrow = [sb(f"vrow{s}", [P, TPC, H, VW], F32) for s in range(2)]
        turned = psum("turned", [P, KC, CHUNK])
        qk = [psum(f"qk{m}", [P, CHUNK]) for m in range(2)]
        vps = psum("vps", [P, TPC, D])
        lps = psum("lps", [P, TPC, E])

        weights_in = sem("weights_in")
        x_in = [sem(f"x_in{s}") for s in range(2)]
        tally = sem("p_tally")
        stats_done = sem("stats_done")
        var_done = sem("var_done")
        std_done = sem("std_done")
        rstd_step = sem("rstd_step")
        xn_done = sem("xn_done")
        xn_kept = sem("xn_kept")
        turned_done = sem("turned_done")
        xnT_done = sem("xnT_done")
        qk_done = sem("qk_done")
        hi_done = sem("hi_done")
        rest_done = sem("rest_done")
        mid_done = sem("mid_done")
        lo_done = sem("lo_done")
        v_done = sem("v_done")
        logits_done = sem("logits_done")
        v_kept = sem("v_kept")
        logits_kept = sem("logits_kept")
        stored = [sem(f"stored{s}") for s in range(2)]
        filled = sem("p_filled")
        rw_turned = sem("rw_turned")
        rw_done = sem("rw_done")
        zeroed = sem("zeroed")
        zeros_out = sem("zeros_out")
        NEWTON = 4

        with nc.Block() as block:
            @block.sync
            def _(sp):
                for n, w in enumerate((Wq, Wk, Wv)):
                    sp.dma_start(wqkv[:, n, :, :], w.rearrange("(c p) h e -> p c (h e)", p=P)).then_inc(weights_in, 16)
                sp.dma_start(rw[:, :], router_w).then_inc(weights_in, 16)

                def load(i, s):
                    sp.dma_start(xin[s][:, :, :], x[bass.ds(i * L + s * CHUNK, CHUNK), :].rearrange(
                        "(t p) d -> p t d", p=P)).then_inc(x_in[s], 16)

                def store(i, s):
                    sp.wait_ge(lo_done, PRIME + i * 2 * MC + (s + 1) * MC)
                    for m in range(MC):
                        sp.dma_start(g.qk_parts[m // KC, :, (m % KC) * P:(m % KC + 1) * P,
                                                bass.ds(i * L + s * CHUNK, CHUNK)].rearrange("r p t -> p r t"),
                                     parts[s][:, m, :, :]).then_inc(stored[s], 16)
                    sp.wait_ge(v_kept, PRIME + i * 2 + s + 1)
                    for q in range(QUADS):
                        sp.dma_start(g.v_rows[bass.ds(i * QUADS + q, 1), :, s * TPC:(s + 1) * TPC, :].rearrange(
                            "o p t c -> p (o t) c"),
                            vrow[s][:, :, 4 * q:4 * q + 4, :].rearrange("p t h c -> p t (h c)")).then_inc(stored[s], 16)

                load(0, 0)
                load(0, 1)
                sp.wait_ge(zeroed, PRIME + 1)
                for r in range(0, E * CAP, 4 * P):
                    sp.dma_start(g.queues[r:r + 4 * P, :].rearrange("(p c) d -> p (c d)", c=4), zeros[:, :]).then_inc(zeros_out, 16)
                sp.dma_start(g.answers[E * CAP:E * CAP + P, :], zeros[:, 0:D]).then_inc(zeros_out, 16)
                with sp.Fori(0, B - 1) as i:
                    for s in range(2):
                        store(i, s)
                        sp.wait_ge(xn_done, PRIME + (i * 2 + s + 1) * TPC)
                        load(i + 1, s)
                for s in range(2):
                    store(B - 1, s)
                for s in range(2):
                    sp.wait_ge(stored[s], PRIME + 16 * B * (MC + QUADS))
                sp.wait_ge(zeros_out, PRIME + 16 * (E * CT // 4 + 1))

            @block.gpsimd
            def _(pool):
                prime(pool, primed)
                nc.gpsimd.memset(zeros[:, :], 0.0).then_inc(zeroed, 1)
                nc.gpsimd.memset(eps[:, :], EPS).then_inc(filled, 1)
                for s in range(2):
                    nc.gpsimd.memset(vrow[s][:, :, :, DH:VW], 1.0).then_inc(filled, 1)
                with pool.Fori(0, B) as i:
                    for s in range(2):
                        for m in range(MC):
                            pool.wait_ge(mid_done, PRIME + i * 2 * MC + s * MC + m + 1)
                            nc.gpsimd.tensor_tensor(parts[s][:, m, 2, :], rest[m % 2][:, :], parts[s][:, m, 1, :],
                                                    ALU.subtract).then_inc(lo_done, 1)

            @block.tensor
            def _(pe):
                pe.wait_ge(weights_in, PRIME + 64)
                for c in range(KC):
                    nc.tensor.transpose(turned[:, 0, c * E:(c + 1) * E], rw[:, c * P:(c + 1) * P],
                                        g.ident[0:E, 0:E]).then_inc(rw_turned, 1)
                pe.wait_ge(rw_done, PRIME + 1)
                with pe.Fori(0, B) as i:
                    for s in range(2):
                        n = i * 2 + s
                        pe.wait_ge(xn_done, PRIME + (n + 1) * TPC)
                        pe.wait_ge(xnT_done, PRIME + n)
                        for t in range(TPC):
                            for c in range(KC):
                                mm = nc.tensor.transpose(turned[:, c, t * P:(t + 1) * P],
                                                         xn[s][:, t, c * P:(c + 1) * P], g.ident[:, :])
                        mm.then_inc(turned_done, 1)
                        pe.wait_ge(xnT_done, PRIME + n + 1)
                        for m in range(MC):
                            pe.wait_ge(rest_done, PRIME + n * MC + m - 1)
                            for c in range(KC):
                                mm = nc.tensor.matmul(qk[m % 2][:, :],
                                                      wqkv[:, m // KC, c, (m % KC) * P:(m % KC + 1) * P],
                                                      xnT[s][:, c, :], start=c == 0, stop=c == KC - 1)
                            mm.then_inc(qk_done, 1)
                        pe.wait_ge(v_kept, PRIME + n)
                        pe.wait_ge(logits_kept, PRIME + n)
                        for t in range(TPC):
                            for c in range(KC):
                                mm = nc.tensor.matmul(vps[:, t, :], xnT[s][:, c, t * P:(t + 1) * P],
                                                      wqkv[:, 2, c, :], start=c == 0, stop=c == KC - 1)
                        mm.then_inc(v_done, 1)
                        for t in range(TPC):
                            for c in range(KC):
                                mm = nc.tensor.matmul(lps[:, t, :], xnT[s][:, c, t * P:(t + 1) * P],
                                                      rwT[:, c, :], start=c == 0, stop=c == KC - 1)
                        mm.then_inc(logits_done, 1)

            @block.scalar
            def _(act):
                def mid(n, s, m):
                    act.wait_ge(rest_done, PRIME + n * MC + m + 1)
                    nc.scalar.copy(parts[s][:, m, 1, :], rest[m % 2][:, :]).then_inc(mid_done, 1)

                act.wait_ge(filled, PRIME + 3)
                with act.Fori(0, B) as i:
                    for s in range(2):
                        n = i * 2 + s
                        act.wait_ge(var_done, PRIME + (n + 1) * TPC)
                        nc.scalar.activation(std[s][:, :], mv[s][:, :, 1], ACT.Sqrt,
                                             bias=eps[:, 0:1]).then_inc(std_done, 1)
                        act.wait_ge(turned_done, PRIME + n + 1)
                        act.wait_ge(logits_done, PRIME + n - 1)
                        nc.scalar.copy(xnT[s][:, :, :], turned[:, :, :]).then_inc(xnT_done, 1)
                        nc.scalar.copy(g.xn_all[:, bass.ds(i * QT + s * TPC, TPC), :], xn[s][:, :, :]).then_inc(xn_kept, 1)
                        act.wait_ge(stored[s], PRIME + i * (16 * (MC + QUADS)))
                        for m in range(MC):
                            act.wait_ge(qk_done, PRIME + n * MC + m + 1)
                            nc.scalar.mul(parts[s][:, m, 0, :], qk[m % 2][:, :], DH ** -0.5 if m < KC else 1.0).then_inc(hi_done, 1)
                            if m:
                                mid(n, s, m - 1)
                        mid(n, s, MC - 1)
                        act.wait_ge(v_done, PRIME + n + 1)
                        nc.scalar.copy(vrow[s][:, :, :, 0:DH], vps[:, :, :].rearrange("p t (h e) -> p (t h) e", e=DH).rearrange(
                            "p (t h) e -> p t h e", t=TPC)).then_inc(v_kept, 1)

            @block.vector
            def _(dve):
                def layernorm(n, i, s):
                    dve.wait_ge(x_in[s], PRIME + i * 16 + 16)
                    for t in range(TPC):
                        nc.vector.bn_stats(stats[s][:, t, :], xin[s][:, t, :]).then_inc(stats_done, 1)
                    dve.wait_ge(stats_done, PRIME + (n + 1) * TPC)
                    dve.sem_inc(tally, 1)
                    for t in range(TPC):
                        nc.vector.bn_aggr(mv[s][:, t, :], stats[s][:, t, :]).then_inc(var_done, 1)
                    dve.wait_ge(var_done, PRIME + (n + 1) * TPC)
                    dve.wait_ge(std_done, PRIME + n + 1)
                    nc.vector.reciprocal(rstd[s][:, :], std[s][:, :]).then_inc(rstd_step, 1)
                    base = n * (NEWTON + 1)
                    dve.wait_ge(rstd_step, PRIME + base + 1)
                    nc.vector.tensor_tensor(newt[s][:, :], rstd[s][:, :], rstd[s][:, :], ALU.mult).then_inc(rstd_step, 1)
                    dve.wait_ge(rstd_step, PRIME + base + 2)
                    nc.vector.scalar_tensor_tensor(out=newt[s][:, :], in0=mv[s][:, :, 1], scalar=EPS, in1=newt[s][:, :],
                                                   op0=ALU.add, op1=ALU.mult).then_inc(rstd_step, 1)
                    dve.wait_ge(rstd_step, PRIME + base + 3)
                    nc.vector.tensor_scalar(newt[s][:, :], newt[s][:, :], -0.5, 1.5, ALU.mult, ALU.add).then_inc(rstd_step, 1)
                    dve.wait_ge(rstd_step, PRIME + base + 4)
                    nc.vector.tensor_tensor(rstd[s][:, :], rstd[s][:, :], newt[s][:, :], ALU.mult).then_inc(rstd_step, 1)
                    dve.wait_ge(rstd_step, PRIME + base + 5)

                def normalise(n, s):
                    for t in range(TPC):
                        nc.vector.tensor_scalar(xn[s][:, t, :], xin[s][:, t, :], mv[s][:, t, 0:1], rstd[s][:, t:t + 1],
                                                ALU.subtract, ALU.mult).then_inc(xn_done, 1)

                dve.wait_ge(rw_turned, PRIME + KC)
                nc.vector.tensor_copy(rwT[:, :, :], turned[:, 0, 0:KC * E].rearrange("p (c e) -> p c e", c=KC)).then_inc(rw_done, 1)
                with dve.Fori(0, B) as i:
                    for s in range(2):
                        n = i * 2 + s
                        layernorm(n, i, s)
                        dve.wait_ge(xn_kept, PRIME + n - 1)
                        normalise(n, s)
                        for m in range(MC):
                            dve.wait_ge(hi_done, PRIME + n * MC + m + 1)
                            dve.wait_ge(lo_done, PRIME + n * MC + m - 1)
                            nc.vector.scalar_tensor_tensor(out=rest[m % 2][:, :], in0=qk[m % 2][:, :],
                                                           scalar=DH ** -0.5 if m < KC else 1.0,
                                                           in1=parts[s][:, m, 0, :], op0=ALU.mult,
                                                           op1=ALU.subtract).then_inc(rest_done, 1)
                        dve.wait_ge(logits_done, PRIME + n + 1)
                        nc.vector.tensor_copy(g.logits[:, bass.ds(i * QT + s * TPC, TPC), :], lps[:, :, :]).then_inc(logits_kept, 1)


STEPS = [(qc, j) for qc in range(L // BANK) for j in range((qc + 1) * TPC)]
NS = len(STEPS)
MASKED_STEPS = [s for s, (qc, j) in enumerate(STEPS) if j >= qc * TPC]
TILES = [(h, qt) for h in range(4) for qt in range(QT)]
NTILE = len(TILES)
TILE_STEPS = 10
TURN_FIRST = 6
TURN_MAX = 10


def tiles_beside(s):
    if s >= TILE_STEPS:
        return [], []
    mine = list(range(NTILE * s // TILE_STEPS, NTILE * (s + 1) // TILE_STEPS))
    return mine[:len(mine) // 2], mine[len(mine) // 2:]


def build_attend(nc, g):
    with ExitStack() as ctx:
        def sb(name, shape, dt):
            return ctx.enter_context(nc.sbuf_tensor(name, shape, dt))

        def psum(name, shape):
            return ctx.enter_context(nc.psum_tensor(name, shape, F32))

        primed = []

        def sem(name):
            primed.append(ctx.enter_context(nc.semaphore(name)))
            return primed[-1]

        qst = [sb(f"qst{q}", [STACK + MAXROWS, 4, L], BF16) for q in range(QUADS)]
        kst = [sb(f"kst{q}", [STACK + MAXROWS, 4, L], BF16) for q in range(QUADS)]
        vst = [sb(f"vst{q}", [P, QT, 4 * VW], F32) for q in range(QUADS)]
        probs = [sb(f"probs{n}", [P, 4, BANK], F32) for n in range(3)]
        rowmax = sb("rowmax", [P, 4, QT], F32)
        maxrest = sb("maxrest", [P, 4, QT], F32)
        maxparts = sb("maxparts", [P, MAXROWS, 4, QT], BF16)
        maxturned = sb("maxturned", [MAXROWS * 4 * QT, P], BF16)
        outT = [sb(f"outT{n}", [P, BANK], F32) for n in range(2)]
        recip = sb("recip", [P, TPC, 4], F32)
        heads = [sb(f"heads{n}", [P, TPC, 4 * DH], F32) for n in range(2)]
        score = [psum(f"score{n}", [P, L]) for n in range(2)]
        scoreT = [psum(f"scoreT{n}", [P, BANK]) for n in range(2)]
        outps = psum("outps", [P, BANK])
        small = psum("small", [P, TPC, P])
        smallb = small[:, 0, :].bitcast(BF16)

        tally = sem("a_tally")
        ones_set = sem("ones_set")
        stack_in = [sem(f"stack_in{q}") for q in range(QUADS)]
        max_in = [sem(f"max_in{q}") for q in range(QUADS)]
        score_done = sem("score_done")
        max_done = sem("max_done")
        max_step = sem("max_step")
        max_turned = sem("max_turned")
        max_copied = sem("max_copied")
        scoreT_done = sem("scoreT_done")
        exp_done = sem("exp_done")
        mask_done = sem("mask_done")
        pv_done = sem("pv_done")
        out_copied = sem("out_copied")
        out_turned = sem("out_turned")
        heads_step = sem("heads_step")
        heads_out = [sem(f"heads_out{n}") for n in range(2)]
        LOADS = 2 * len(TERMS) + 1
        MAXSTEPS = 5

        def units(eng, first, phase):
            first()
            with eng.Fori(0, B - 1) as i:
                for q in range(QUADS):
                    phase(i, q, True)
            for q in range(QUADS):
                phase(B - 1, q, q < QUADS - 1)

        with nc.Block() as block:
            @block.sync
            def _(sp):
                def load(i, q):
                    for n, (a, c) in enumerate(TERMS):
                        for st, side, part in ((qst, 0, a), (kst, 1, c)):
                            sp.dma_start(st[q][n * DH:(n + 1) * DH, :, :],
                                         g.qk_parts[side, part, 4 * DH * q:4 * DH * (q + 1), bass.ds(i * L, L)].rearrange(
                                             "(h d) t -> d h t", d=DH)).then_inc(stack_in[q], 16)
                    sp.dma_start(vst[q][:, :, :], g.v_rows[bass.ds(i * QUADS + q, 1), :, :, :].rearrange(
                        "o p t c -> p (o t) c")).then_inc(stack_in[q], 16)

                def max_rows(u, q):
                    sp.wait_ge(max_copied, PRIME + u + 1)
                    for r in range(MAXROWS):
                        sp.dma_start(qst[q][STACK + r:STACK + r + 1, :, :].rearrange("o h t -> o (h t)"),
                                     maxturned[r * 4 * QT:(r + 1) * 4 * QT, :]).then_inc(max_in[q], 16)

                def store(i, q, qc):
                    sp.wait_ge(heads_step, PRIME + ((i * QUADS + q) * 2 + qc + 1) * 2)
                    sp.dma_start(g.attn_rows[bass.ds(i * L + qc * BANK, BANK), 4 * DH * q:4 * DH * (q + 1)].rearrange(
                        "(t p) c -> p t c", p=P), heads[qc][:, :, :]).then_inc(heads_out[qc], 16)

                def phase(i, q, ahead):
                    u = i * QUADS + q
                    store(i, q, 0)
                    if ahead:
                        max_rows(u + 1, (q + 1) % QUADS)
                    store(i, q, 1)
                    if not isinstance(i, int):
                        sp.wait_ge(scoreT_done, PRIME + (u + 1) * 4 * NS)
                        sp.wait_ge(pv_done, PRIME + (u + 1) * NS)
                        load(i + 1, q)

                sp.wait_ge(ones_set, PRIME + 2)
                for q in range(QUADS):
                    load(0, q)
                units(sp, lambda: max_rows(0, 0), phase)
                for qc in range(2):
                    sp.wait_ge(heads_out[qc], PRIME + 16 * B * QUADS)

            @block.gpsimd
            def _(pool):
                prime(pool, primed)
                for q in range(QUADS):
                    one = nc.gpsimd.memset(kst[q][STACK:STACK + MAXROWS, :, :], 1.0)
                one.then_inc(ones_set, 1)

                def phase(i, q, ahead):
                    u = i * QUADS + q
                    for n, s in enumerate(MASKED_STEPS):
                        qc, j = STEPS[s]
                        off = (j - qc * TPC) * P
                        pool.wait_ge(exp_done, PRIME + u * 4 * NS + 4 * (s + 1))
                        pool.sem_inc(tally, 1)
                        tile = probs[s % 3][:, :, off:off + P]
                        nc.gpsimd.affine_select(out=tile, in_=tile, compare_op=ALU.is_ge, fill=0.0, base=0,
                                                pattern=[[0, 4], [1, P]], channel_multiplier=-1).then_inc(mask_done, 1)

                units(pool, lambda: None, phase)

            @block.tensor
            def _(pe):
                def row_tiles(i, u, q, tiles):
                    for t in tiles:
                        h, qt = TILES[t]
                        if t == 0:
                            pe.wait_ge(stack_in[q], PRIME + 16 * LOADS * (i + 1))
                        pe.wait_ge(max_done, PRIME + u * NTILE + t - 1)
                        width = (qt + 1) * P
                        for k0 in range(0, width, BANK):
                            k1 = min(width, k0 + BANK)
                            last = k1 == width
                            mm = nc.tensor.matmul(score[t % 2][:, k0:k1], qst[q][0:STACK, h, qt * P:(qt + 1) * P],
                                                  kst[q][0:STACK, h, k0:k1], start=True, stop=not last)
                        mm = nc.tensor.matmul(score[t % 2][:, width - P:width], g.identb[:, :], g.maskneg[:, :],
                                              start=False, stop=True)
                        mm.then_inc(score_done, 1)

                def turn_max(u):
                    pe.wait_ge(max_step, PRIME + (u + 1) * MAXSTEPS)
                    pe.wait_ge(heads_step, PRIME + (2 * u - 1) * 2)
                    nc.tensor.transpose(smallb[0:MAXROWS * 4 * QT, 0:P],
                                        maxparts[:, :, :, :].rearrange("p r h t -> p (r h t)"),
                                        g.identb[:, :]).then_inc(max_turned, 1)

                def turn_out(u, qc, behind):
                    pe.wait_ge(out_copied, PRIME + 2 * u + qc + 1)
                    pe.wait_ge(heads_step, PRIME + (2 * u + qc) * 2)
                    if behind is not None:
                        pe.wait_ge(max_copied, PRIME + behind)
                    for t in range(TPC):
                        mm = nc.tensor.transpose(small[:, t, :], outT[qc][:, t * P:(t + 1) * P], g.ident[:, :])
                    mm.then_inc(out_turned, 1)

                def values(u, q, s):
                    qc, j = STEPS[s]
                    off = max(0, (j - qc * TPC) * P)
                    pe.wait_ge(exp_done, PRIME + u * 4 * NS + 4 * (s + 1))
                    if s in MASKED_STEPS:
                        pe.wait_ge(mask_done, PRIME + u * len(MASKED_STEPS) + MASKED_STEPS.index(s) + 1)
                    if j == 0:
                        pe.wait_ge(out_copied, PRIME + 2 * u + qc)
                    for h in range(4):
                        mm = nc.tensor.matmul(outps[32 * h:32 * h + VW, off:BANK], vst[q][:, j, h * VW:(h + 1) * VW],
                                              probs[s % 3][:, h, off:BANK], start=j == 0,
                                              stop=j == (qc + 1) * TPC - 1)
                    mm.then_inc(pv_done, 1)

                def phase(i, q, ahead):
                    u = i * QUADS + q
                    nq = (q + 1) % QUADS
                    ni = i + 1 if nq == 0 else i
                    pe.wait_ge(max_in[q], PRIME + 16 * MAXROWS * (i + 1))
                    for s, (qc, j) in enumerate(STEPS):
                        off = max(0, (j - qc * TPC) * P)
                        beside = tiles_beside(s) if ahead else ([], [])
                        for h in range(4):
                            m = 4 * s + h
                            pe.wait_ge(exp_done, PRIME + u * 4 * NS + m - 1)
                            nc.tensor.matmul(scoreT[m % 2][:, off:BANK], kst[q][:, h, j * P:(j + 1) * P],
                                             qst[q][:, h, qc * BANK + off:(qc + 1) * BANK],
                                             start=True, stop=True).then_inc(scoreT_done, 1)
                            if h % 2:
                                row_tiles(ni, u + 1, nq, beside[h // 2])
                        if s:
                            values(u, q, s - 1)
                        if s == TURN_FIRST:
                            turn_out(u, 0, None)
                        if s == TURN_MAX and ahead:
                            turn_max(u + 1)
                    values(u, q, NS - 1)
                    turn_out(u, 1, u + 2 if ahead else None)

                pe.wait_ge(ones_set, PRIME + 2)

                def first():
                    row_tiles(0, 0, 0, range(NTILE))
                    turn_max(0)

                units(pe, first, phase)

            @block.scalar
            def _(act):
                def copy_max(u):
                    act.wait_ge(max_turned, PRIME + u + 1)
                    nc.scalar.copy(maxturned[:, :], smallb[0:MAXROWS * 4 * QT, 0:P]).then_inc(max_copied, 1)

                def copy_out(u, qc):
                    act.wait_ge(pv_done, PRIME + u * NS + (TPC if qc == 0 else NS))
                    nc.scalar.copy(outT[qc][:, :], outps[:, :]).then_inc(out_copied, 1)

                def phase(i, q, ahead):
                    u = i * QUADS + q
                    for s, (qc, j) in enumerate(STEPS):
                        off = max(0, (j - qc * TPC) * P)
                        act.wait_ge(pv_done, PRIME + u * NS + s - 2)
                        for h in range(4):
                            m = 4 * s + h
                            act.wait_ge(scoreT_done, PRIME + u * 4 * NS + m + 1)
                            nc.scalar.activation(probs[s % 3][:, h, off:BANK], scoreT[m % 2][:, off:BANK],
                                                 ACT.Exp).then_inc(exp_done, 1)
                        if s == TPC:
                            copy_out(u, 0)
                        if s == TURN_MAX and ahead:
                            act.wait_ge(max_in[q], PRIME + 16 * MAXROWS * (i + 1))
                            copy_max(u + 1)
                    copy_out(u, 1)

                units(act, lambda: copy_max(0), phase)

            @block.vector
            def _(dve):
                def row_tiles(u, tiles):
                    for t in tiles:
                        h, qt = TILES[t]
                        dve.wait_ge(score_done, PRIME + u * NTILE + t + 1)
                        if t == 0:
                            dve.wait_ge(max_step, PRIME + u * MAXSTEPS)
                        nc.vector.tensor_reduce(rowmax[:, h, qt:qt + 1], score[t % 2][:, 0:(qt + 1) * P],
                                                AX.X, ALU.max).then_inc(max_done, 1)

                def split_max(u):
                    dve.wait_ge(max_done, PRIME + (u + 1) * NTILE)
                    dve.wait_ge(max_turned, PRIME + u)
                    base = u * MAXSTEPS
                    nc.vector.tensor_scalar(maxparts[:, 0, :, :], rowmax[:, :, :], -1.0, None, ALU.mult).then_inc(max_step, 1)
                    dve.wait_ge(max_step, PRIME + base + 1)
                    nc.vector.scalar_tensor_tensor(out=maxrest[:, :, :], in0=rowmax[:, :, :], scalar=-1.0,
                                                   in1=maxparts[:, 0, :, :], op0=ALU.mult,
                                                   op1=ALU.subtract).then_inc(max_step, 1)
                    dve.wait_ge(max_step, PRIME + base + 2)
                    nc.vector.tensor_copy(maxparts[:, 1, :, :], maxrest[:, :, :]).then_inc(max_step, 1)
                    dve.wait_ge(max_step, PRIME + base + 3)
                    nc.vector.tensor_tensor(maxrest[:, :, :], maxrest[:, :, :], maxparts[:, 1, :, :],
                                            ALU.subtract).then_inc(max_step, 1)
                    dve.wait_ge(max_step, PRIME + base + 4)
                    nc.vector.tensor_copy(maxparts[:, 2, :, :], maxrest[:, :, :]).then_inc(max_step, 1)

                def normalise(u, qc):
                    turned = small[:, :, :].rearrange("p t (h c) -> p (t h) c", h=4)
                    dve.wait_ge(out_turned, PRIME + 2 * u + qc + 1)
                    nc.vector.reciprocal(recip[:, :, :].rearrange("p t h -> p (t h)"), turned[:, :, DH]).then_inc(heads_step, 1)
                    dve.wait_ge(heads_step, PRIME + (2 * u + qc) * 2 + 1)
                    dve.wait_ge(heads_out[qc], PRIME + u * 16)
                    nc.vector.tensor_tensor(heads[qc][:, :, :].rearrange("p t (h c) -> p (t h) c", h=4),
                                            turned[:, :, 0:DH],
                                            recip[:, :, :].rearrange("p t h -> p (t h)").unsqueeze(2).broadcast_to([P, TPC * 4, DH]),
                                            ALU.mult).then_inc(heads_step, 1)

                def phase(i, q, ahead):
                    u = i * QUADS + q
                    for s in range(NS):
                        beside = tiles_beside(s) if ahead else ([], [])
                        row_tiles(u + 1, beside[0] + beside[1])
                        if s == TILE_STEPS - 1 and ahead:
                            split_max(u + 1)
                        if s == TURN_FIRST:
                            normalise(u, 0)
                    normalise(u, 1)

                def first():
                    nc.vector.memset(outps[:, :], 0.0).then_inc(ones_set, 1)
                    row_tiles(0, range(NTILE))
                    split_max(0)

                units(dve, first, phase)


def build_route(nc, g):
    with ExitStack() as ctx:
        def sb(name, shape, dt=F32):
            return ctx.enter_context(nc.sbuf_tensor(name, shape, dt))

        def sem(name):
            return ctx.enter_context(nc.semaphore(name))

        prob = sb("prob", [P, NT, E])
        left = sb("left", [P, NT, E])
        pick = sb("pick", [P, NT, E])
        hot = [sb(f"hot{k}", [P, NT, E]) for k in range(TOPK)]
        gate = sb("gate", [P, NT, E])
        back = sb("back", [P, 1, E])
        row = sb("row", [P, NT])
        top = [sb(f"top{k}", [P, NT]) for k in range(TOPK)]
        total = sb("total", [P, NT])
        bits = sb("bits", [P, E], I32)
        trial = sb("trial", [P, E], I32)
        bit = sb("bit", [P, E], I32)
        over = sb("over", [P, E, NT], BF16)
        count = sb("count", [P, E], BF16)
        above = sb("above", [P, E, NT])
        ties = sb("ties", [P, E, NT], BF16)
        need = sb("need", [P, E])
        kept = sb("kept", [P, E, NT], BF16)
        start = sb("start", [P, E, NT])
        resets = sb("resets", [P, E, NT])
        slot = sb("slot", [P, E, NT])
        base = sb("base", [P, E, 1])
        ones = sb("ones", [P, P], BF16)
        before = sb("before", [P, P], BF16)
        counted = ctx.enter_context(nc.psum_tensor("counted", [P, BANK], F32))
        ranked = ctx.enter_context(nc.psum_tensor("ranked", [P, E, NT], F32))
        tiles = ctx.enter_context(nc.psum_tensor("tiles", [P, E, NT], F32))

        filled = sem("r_filled")
        cut = sem("r_cut")
        shifted = sem("shifted")
        exp_done = sem("r_exp_done")
        step = sem("r_step")
        trial_done = sem("trial_done")
        count_done = sem("count_done")
        prefix_in = sem("prefix_in")
        prefix_done = sem("prefix_done")
        slots_done = sem("slots_done")
        sent = sem("sent")
        BITS = 30

        def by_expert(t):
            return t[:, :, :].rearrange("p t e -> p e t")

        with nc.Block() as block:
            @block.gpsimd
            def _(pool):
                nc.gpsimd.memset(ones[:, :], 1.0).then_inc(filled, 1)
                pool.wait_ge(filled, 1)
                nc.gpsimd.affine_select(out=before[:, :], in_=ones[:, :], compare_op=ALU.is_gt, fill=0.0,
                                        base=0, pattern=[[1, P]], channel_multiplier=-1).then_inc(cut, 1)
                nc.gpsimd.memset(bits[:, :], 0).then_inc(filled, 1)
                nc.gpsimd.memset(resets[:, :, :], 1.0).then_inc(filled, 1)
                pool.wait_ge(filled, 3)
                nc.gpsimd.memset(resets[:, :, 0:1], 0.0).then_inc(filled, 1)
                for e in range(E):
                    nc.gpsimd.memset(back[:, 0, e:e + 1], float(E - e)).then_inc(filled, 1)
                    nc.gpsimd.memset(base[:, e, :], float(e * CAP - E * CAP)).then_inc(filled, 1)
                pool.wait_ge(slots_done, TOPK)
                for t in range(NT):
                    for k in range(TOPK):
                        nc.gpsimd.indirect_dma_start(
                            g.queues, bass.IndirectOffsetOnAxis(ap=g.slots[:, k, t:t + 1], axis=0),
                            g.xn_all[:, t, :], None, bounds_check=E * CAP - 1, oob_is_err=False).then_inc(sent, 16)
                pool.wait_ge(sent, 16 * NT * TOPK)

            @block.scalar
            def _(act):
                act.wait_ge(shifted, 1)
                nc.scalar.activation(prob[:, :, :], left[:, :, :], ACT.Exp).then_inc(exp_done, 1)

            @block.tensor
            def _(pe):
                pe.wait_ge(filled, 4 + 2 * E)
                pe.wait_ge(cut, 1)
                for n in range(BITS + 1):
                    pe.wait_ge(trial_done, n + 1)
                    nc.tensor.matmul(counted[:, 0:E], ones[:, :], count[:, :], start=True, stop=True).then_inc(count_done, 1)
                for n, rows in enumerate((ties, kept)):
                    pe.wait_ge(prefix_in, n + 1)
                    flat = rows[:, :, :].rearrange("p e t -> p (e t)")
                    nc.tensor.matmul(ranked[:, :, :].rearrange("p e t -> p (e t)"), before[:, :], flat, start=True, stop=True)
                    nc.tensor.matmul(tiles[:, :, :].rearrange("p e t -> p (e t)"), ones[:, :], flat,
                                     start=True, stop=True).then_inc(prefix_done, 1)

            @block.vector
            def _(dve):
                chain = [0]

                def link(ins):
                    chain[0] += 1
                    ins.then_inc(step, 1)
                    dve.wait_ge(step, chain[0])

                def over_experts(t):
                    return t[:, :].unsqueeze(2).broadcast_to([P, NT, E])

                def over_tiles(t):
                    return t[:, :].unsqueeze(2).broadcast_to([P, E, NT])

                link(nc.vector.tensor_reduce(row[:, :], g.logits[:, :, :], AX.X, ALU.max))
                nc.vector.tensor_tensor(left[:, :, :], g.logits[:, :, :], over_experts(row), ALU.subtract).then_inc(shifted, 1)
                dve.wait_ge(exp_done, 1)
                link(nc.vector.tensor_reduce(total[:, :], prob[:, :, :], AX.X, ALU.add))
                link(nc.vector.reciprocal(row[:, :], total[:, :]))
                link(nc.vector.tensor_tensor(prob[:, :, :], prob[:, :, :], over_experts(row), ALU.mult))
                dve.wait_ge(filled, 4 + 2 * E)
                backwards = back[:, :, :].broadcast_to([P, NT, E])
                now = prob
                for k in range(TOPK):
                    link(nc.vector.tensor_reduce(top[k][:, :], now[:, :, :], AX.X, ALU.max))
                    link(nc.vector.tensor_tensor(pick[:, :, :], now[:, :, :], over_experts(top[k]), ALU.is_equal))
                    link(nc.vector.tensor_tensor(pick[:, :, :], pick[:, :, :], backwards, ALU.mult))
                    link(nc.vector.tensor_reduce(row[:, :], pick[:, :, :], AX.X, ALU.max))
                    link(nc.vector.tensor_tensor(hot[k][:, :, :], backwards, over_experts(row), ALU.is_equal))
                    if k == 0:
                        link(nc.vector.scalar_tensor_tensor(out=left[:, :, :], in0=hot[0][:, :, :], scalar=-2.0,
                                                            in1=prob[:, :, :], op0=ALU.mult, op1=ALU.add))
                        now = left
                link(nc.vector.tensor_tensor(total[:, :], top[0][:, :], top[1][:, :], ALU.add))
                link(nc.vector.tensor_scalar(total[:, :], total[:, :], 1e-6, None, ALU.add))
                link(nc.vector.reciprocal(row[:, :], total[:, :]))
                for k in range(TOPK):
                    link(nc.vector.tensor_tensor(g.weights[:, k, :], top[k][:, :], row[:, :], ALU.mult))
                link(nc.vector.tensor_tensor(gate[:, :, :], hot[0][:, :, :], over_experts(g.weights[:, 0, :]), ALU.mult))
                link(nc.vector.tensor_tensor(pick[:, :, :], hot[1][:, :, :], over_experts(g.weights[:, 1, :]), ALU.mult))
                link(nc.vector.tensor_tensor(gate[:, :, :], gate[:, :, :], pick[:, :, :], ALU.add))
                link(nc.vector.scalar_tensor_tensor(out=pick[:, :, :], in0=hot[0][:, :, :], scalar=-1.0,
                                                    in1=hot[1][:, :, :], op0=ALU.add, op1=ALU.add))
                link(nc.vector.tensor_tensor(gate[:, :, :], gate[:, :, :], pick[:, :, :], ALU.add))
                for n in range(BITS):
                    b = BITS - 1 - n
                    link(nc.vector.tensor_scalar(trial[:, :], bits[:, :], 1 << b, None, ALU.bitwise_or))
                    link(nc.vector.tensor_tensor(over[:, :, :], by_expert(gate), over_tiles(trial[:, :].bitcast(F32)), ALU.is_ge))
                    with nc.allow_low_precision("counts of at most NT are exact in bfloat16"):
                        nc.vector.tensor_reduce(count[:, :], over[:, :, :], AX.X, ALU.add).then_inc(trial_done, 1)
                    dve.wait_ge(count_done, n + 1)
                    link(nc.vector.tensor_scalar(bit[:, :], counted[:, 0:E], float(CAP), float(1 << b), ALU.is_ge, ALU.mult))
                    link(nc.vector.tensor_tensor(bits[:, :], bits[:, :], bit[:, :], ALU.bitwise_or))
                limit = over_tiles(bits[:, :].bitcast(F32))
                link(nc.vector.tensor_tensor(above[:, :, :], by_expert(gate), limit, ALU.is_gt))
                with nc.allow_low_precision("counts of at most NT are exact in bfloat16"):
                    nc.vector.tensor_reduce(count[:, :], above[:, :, :], AX.X, ALU.add).then_inc(trial_done, 1)
                nc.vector.tensor_tensor(ties[:, :, :], by_expert(gate), limit, ALU.is_equal).then_inc(prefix_in, 1)
                dve.wait_ge(count_done, BITS + 1)
                link(nc.vector.tensor_scalar(need[:, :], counted[:, 0:E], -1.0, float(CAP), ALU.mult, ALU.add))

                def ranks(n):
                    dve.wait_ge(prefix_done, n + 1)
                    link(nc.vector.tensor_copy(slot[:, :, :], tiles[:, :, :]))
                    link(nc.vector.tensor_tensor_scan(
                        start[:, :, :].rearrange("p e t -> p (e t)"), resets[:, :, :].rearrange("p e t -> p (e t)"),
                        slot[:, :, :].rearrange("p e t -> p (e t)"), 0.0, ALU.mult, ALU.add))
                    link(nc.vector.tensor_tensor(start[:, :, :], start[:, :, :], slot[:, :, :], ALU.subtract))
                    link(nc.vector.tensor_tensor(slot[:, :, :], ranked[:, :, :], start[:, :, :], ALU.add))

                ranks(0)
                link(nc.vector.tensor_tensor(slot[:, :, :], slot[:, :, :], over_tiles(need), ALU.is_lt))
                link(nc.vector.tensor_tensor(slot[:, :, :], slot[:, :, :], ties[:, :, :], ALU.mult))
                nc.vector.tensor_tensor(kept[:, :, :], above[:, :, :], slot[:, :, :], ALU.add).then_inc(prefix_in, 1)
                ranks(1)
                link(nc.vector.tensor_tensor(slot[:, :, :], slot[:, :, :], base[:, :, :].broadcast_to([P, E, NT]), ALU.add))
                link(nc.vector.tensor_tensor(slot[:, :, :], slot[:, :, :], kept[:, :, :], ALU.mult))
                for k in range(TOPK):
                    link(nc.vector.tensor_tensor(pick[:, :, :], hot[k][:, :, :], slot[:, :, :].rearrange("p e t -> p t e"), ALU.mult))
                    link(nc.vector.tensor_reduce(row[:, :], pick[:, :, :], AX.X, ALU.add))
                    nc.vector.tensor_scalar(g.slots[:, k, :], row[:, :], float(E * CAP), None, ALU.add).then_inc(slots_done, 1)


HALF = CAP // 2
NHALF = 2
GU = FC * NHALF


def split_product(nc, out, left, right, first, last):
    nc.tensor.matmul(out, left[0], right[0], start=first, stop=False)
    nc.tensor.matmul(out, left[1], right[0], start=False, stop=False)
    return nc.tensor.matmul(out, left[0], right[1], start=False, stop=last)


def build_experts(nc, g, wg, wu, wd):
    with ExitStack() as ctx:
        def sb(name, shape, dt=F32):
            return ctx.enter_context(nc.sbuf_tensor(name, shape, dt))

        def psum(name, shape):
            return ctx.enter_context(nc.psum_tensor(name, shape, F32))

        primed = []

        def sem(name):
            primed.append(ctx.enter_context(nc.semaphore(name)))
            return primed[-1]

        MATS = 3
        WCOLS = KC * F
        raw = [sb(f"raw{m}", [P, WCOLS]) for m in range(MATS)]
        whi = [[sb(f"whi{s}{m}", [P, WCOLS], F32R) for m in range(MATS)] for s in range(2)]
        wlo = [[sb(f"wlo{s}{m}", [P, WCOLS], F32R) for m in range(MATS)] for s in range(2)]
        queue = sb("queue", [P, CT, D])
        qhi = sb("qhi", [P, KC, CAP], F32R)
        qlo = sb("qlo", [P, KC, CAP], F32R)
        act_out = [sb(f"act_out{n}", [P, HALF]) for n in range(2)]
        hidden = [sb(f"hidden{n}", [P, HALF]) for n in range(2)]
        hhi = sb("hhi", [P, FC, CAP], F32R)
        hlo = sb("hlo", [P, FC, CAP], F32R)
        rows = [sb(f"rows{n}", [P, D]) for n in range(2)]
        gps = [psum(f"gps{n}", [P, BANK]) for n in range(2)]
        ups = [psum(f"ups{n}", [P, BANK]) for n in range(2)]
        dps = [psum(f"dps{n}", [P, BANK]) for n in range(2)]
        tps = [psum(f"tps{n}", [P, KC, P]) for n in range(2)]

        raw_in = [sem(f"raw_in{m}") for m in range(MATS)]
        queue_in = sem("queue_in")
        whi_done = [sem(f"whi_done{m}") for m in range(MATS)]
        wlo_done = [sem(f"wlo_done{m}") for m in range(MATS)]
        queue_turned = sem("queue_turned")
        qhi_done = sem("qhi_done")
        qlo_done = sem("qlo_done")
        gate_done = sem("gate_done")
        up_done = sem("up_done")
        silu_done = sem("silu_done")
        hidden_done = sem("hidden_done")
        hhi_done = sem("hhi_done")
        hlo_done = sem("hlo_done")
        down_done = sem("down_done")
        rows_done = sem("rows_done")
        rows_out = [sem(f"rows_out{n}") for n in range(2)]
        weights = (wg, wu, wd)

        def hi_lo(pair, *index):
            return [t[index] for t in pair]

        def pairs(eng, first, body):
            first()
            with eng.Fori(0, E // 2 - 1) as i:
                for s in range(2):
                    body(i * 2 + s, s, i, True)
            for s in range(2):
                body(E - 2 + s, s, E // 2 - 1, s == 0)

        with nc.Block() as block:
            @block.sync
            def _(sp):
                def load_weights(e):
                    for m in range(MATS):
                        sp.wait_ge(wlo_done[m], PRIME + e)
                        sp.dma_start(raw[m][:, :].rearrange("p (c f) -> p c f", c=KC if m < 2 else FC),
                                     weights[m][bass.ds(e, 1), :, :].rearrange("o (c p) f -> p (o c) f", p=P)).then_inc(raw_in[m], 16)

                def load_queue(e):
                    sp.wait_ge(queue_turned, PRIME + e * CT)
                    sp.dma_start(queue[:, :, :], g.queues[bass.ds(e * CAP, CAP), :].rearrange(
                        "(t p) d -> p t d", p=P)).then_inc(queue_in, 16)

                def store(e, t, n):
                    sp.wait_ge(rows_done, PRIME + e * CT + t + 1)
                    sp.dma_start(g.answers[bass.ds(e * CAP + t * P, P), :], rows[n][:, :]).then_inc(rows_out[n], 16)

                def body(e, s, i, more):
                    if more:
                        load_queue(e + 1)
                        load_weights(e + 1)
                    for t in range(CT):
                        store(e, t, (s + t) % 2)

                def first():
                    load_queue(0)
                    load_weights(0)

                pairs(sp, first, body)
                for n in range(2):
                    sp.wait_ge(rows_out[n], PRIME + 16 * E * CT // 2)

            @block.gpsimd
            def _(pool):
                prime(pool, primed)

            @block.tensor
            def _(pe):
                def turn_queue(e):
                    pe.wait_ge(queue_in, PRIME + 16 * (e + 1))
                    for t in range(CT):
                        pe.wait_ge(qlo_done, PRIME + e * CT + t - 1)
                        for c in range(KC):
                            mm = nc.tensor.transpose(tps[t % 2][:, c, :], queue[:, t, c * P:(c + 1) * P], g.ident[:, :])
                        mm.then_inc(queue_turned, 1)

                def gate_up(e, s):
                    for m in range(2):
                        pe.wait_ge(wlo_done[m], PRIME + e + 1)
                    pe.wait_ge(qlo_done, PRIME + (e + 1) * CT)
                    for n in range(GU):
                        f, half = n // NHALF, n % NHALF
                        cols = slice(half * HALF, (half + 1) * HALF)
                        pe.wait_ge(hidden_done, PRIME + e * GU + n - 1)
                        for m, (ps, done) in enumerate(((gps, gate_done), (ups, up_done))):
                            for c in range(KC):
                                w = slice(c * F + f * P, c * F + (f + 1) * P)
                                mm = split_product(nc, ps[n % 2][:, 0:HALF],
                                                   (whi[s][m][:, w], wlo[s][m][:, w]),
                                                   (qhi[:, c, cols], qlo[:, c, cols]), c == 0, c == KC - 1)
                            mm.then_inc(done, 1)

                def down(e, s):
                    pe.wait_ge(wlo_done[2], PRIME + e + 1)
                    pe.wait_ge(hlo_done, PRIME + (e + 1) * GU)
                    for t in range(CT):
                        pe.wait_ge(rows_done, PRIME + e * CT + t - 1)
                        for f in range(FC):
                            w, h = slice(f * D, (f + 1) * D), slice(t * P, (t + 1) * P)
                            mm = split_product(nc, dps[(s + t) % 2][:, 0:D], (hhi[:, f, h], hlo[:, f, h]),
                                               (whi[s][2][:, w], wlo[s][2][:, w]), f == 0, f == FC - 1)
                        mm.then_inc(down_done, 1)

                def body(e, s, i, more):
                    gate_up(e, s)
                    if more:
                        turn_queue(e + 1)
                    down(e, s)

                pairs(pe, lambda: turn_queue(0), body)

            @block.scalar
            def _(act):
                def split_weights(e, s):
                    for m in range(MATS):
                        act.wait_ge(raw_in[m], PRIME + 16 * (e + 1))
                        act.wait_ge(down_done, PRIME + (e - 1) * CT)
                        nc.scalar.copy(whi[s][m][:, :], raw[m][:, :]).then_inc(whi_done[m], 1)

                def split_queue(e):
                    for t in range(CT):
                        act.wait_ge(queue_turned, PRIME + e * CT + t + 1)
                        if t == 0:
                            act.wait_ge(up_done, PRIME + e * GU)
                        nc.scalar.copy(qhi[:, :, t * P:(t + 1) * P], tps[t % 2][:, :, :]).then_inc(qhi_done, 1)

                def body(e, s, i, more):
                    for n in range(GU):
                        f, half = n // NHALF, n % NHALF
                        cols = slice(half * HALF, (half + 1) * HALF)
                        act.wait_ge(gate_done, PRIME + e * GU + n + 1)
                        act.wait_ge(hidden_done, PRIME + e * GU + n - 1)
                        nc.scalar.activation(act_out[n % 2][:, :], gps[n % 2][:, 0:HALF], ACT.Silu).then_inc(silu_done, 1)
                        act.wait_ge(hidden_done, PRIME + e * GU + n + 1)
                        if n == 0:
                            act.wait_ge(down_done, PRIME + e * CT)
                        nc.scalar.copy(hhi[:, f, cols], hidden[n % 2][:, :]).then_inc(hhi_done, 1)
                    if more:
                        split_queue(e + 1)
                        split_weights(e + 1, 1 - s)
                    for t in range(CT):
                        act.wait_ge(down_done, PRIME + e * CT + t + 1)
                        act.wait_ge(rows_out[(s + t) % 2], PRIME + 16 * ROWS_OUT(e, s, t, i))
                        nc.scalar.copy(rows[(s + t) % 2][:, :], dps[(s + t) % 2][:, 0:D]).then_inc(rows_done, 1)

                def ROWS_OUT(e, s, t, i):
                    n = (s + t) % 2
                    return i * CT + sum(1 for ss in range(s + 1) for tt in range(CT if ss < s else t) if (ss + tt) % 2 == n)

                def first():
                    split_weights(0, 0)
                    split_queue(0)

                pairs(act, first, body)

            @block.vector
            def _(dve):
                def split_weights(e, s):
                    for m in range(MATS):
                        dve.wait_ge(whi_done[m], PRIME + e + 1)
                        nc.vector.tensor_tensor(wlo[s][m][:, :], raw[m][:, :], whi[s][m][:, :].bitcast(F32),
                                                ALU.subtract).then_inc(wlo_done[m], 1)

                def split_queue(e):
                    for t in range(CT):
                        dve.wait_ge(qhi_done, PRIME + e * CT + t + 1)
                        nc.vector.tensor_tensor(qlo[:, :, t * P:(t + 1) * P], tps[t % 2][:, :, :],
                                                qhi[:, :, t * P:(t + 1) * P].bitcast(F32), ALU.subtract).then_inc(qlo_done, 1)

                def body(e, s, i, more):
                    for n in range(GU):
                        f, half = n // NHALF, n % NHALF
                        cols = slice(half * HALF, (half + 1) * HALF)
                        dve.wait_ge(silu_done, PRIME + e * GU + n + 1)
                        dve.wait_ge(up_done, PRIME + e * GU + n + 1)
                        dve.wait_ge(hlo_done, PRIME + e * GU + n - 1)
                        nc.vector.tensor_tensor(hidden[n % 2][:, :], act_out[n % 2][:, :], ups[n % 2][:, 0:HALF],
                                                ALU.mult).then_inc(hidden_done, 1)
                        dve.wait_ge(hidden_done, PRIME + e * GU + n + 1)
                        dve.wait_ge(hhi_done, PRIME + e * GU + n + 1)
                        nc.vector.tensor_tensor(hlo[:, f, cols], hidden[n % 2][:, :], hhi[:, f, cols].bitcast(F32),
                                                ALU.subtract).then_inc(hlo_done, 1)
                    if more:
                        split_queue(e + 1)
                        split_weights(e + 1, 1 - s)

                def first():
                    split_weights(0, 0)
                    split_queue(0)

                pairs(dve, first, body)


HID = 768
HC = HID // P
SCALE = 1.0 / 127.0


def build_ffn_weights(nc, ctx, g, Wout, W_in, C, w_gate, w_up, w_down):
    def keep(name, shape):
        return [ctx.enter_context(nc.sbuf_tensor(f"{name}_{part}", shape, F32R)) for part in ("hi", "lo")]

    g.wout, g.win, g.cmat = keep("wout", [P, KC, D]), keep("win", [P, KC, D]), keep("cmat", [P, KC, D])
    g.gateT, g.upT, g.downT = keep("gateT", [P, KC, HID]), keep("upT", [P, KC, HID]), keep("downT", [P, HC, D])
    with ExitStack() as own:
        def sb(name, shape, dt=F32):
            return own.enter_context(nc.sbuf_tensor(name, shape, dt))

        def sem(name):
            return own.enter_context(nc.semaphore(name))

        square = [sb(f"square{n}", [P, KC, D]) for n in range(3)]
        whole = [sb("gate_int", [P, HC, D], I32), sb("up_int", [P, HC, D], I32), sb("down_int", [P, KC, HID], I32)]
        scaled = [sb("gate_f", [P, HC, D]), sb("up_f", [P, HC, D]), sb("down_f", [P, KC, HID])]
        tps = [own.enter_context(nc.psum_tensor(f"ftps{n}", [P, D], F32)) for n in range(2)]
        square_in = sem("square_in")
        whole_in = sem("whole_in")
        square_hi = sem("square_hi")
        square_lo = sem("square_lo")
        scaled_done = sem("scaled_done")
        turned = sem("f_turned")
        hi_done = sem("f_hi_done")
        lo_done = sem("f_lo_done")
        groups = []
        for m, parts in enumerate((g.gateT, g.upT)):
            for c in range(KC):
                for f in range(0, HC, 2):
                    groups.append((m, [(f, c), (f + 1, c)], [t[:, c, f * P:(f + 2) * P] for t in parts]))
        for f in range(HC):
            groups.append((2, [(0, f), (1, f)], [t[:, f, :] for t in g.downT]))
        squares = (g.wout, g.win, g.cmat)

        with nc.Block() as block:
            @block.sync
            def _(sp):
                for t, w in zip(whole, (w_gate, w_up, w_down)):
                    sp.dma_start(t[:, :, :], w.rearrange("(c p) d -> p c d", p=P)).then_inc(whole_in, 16)
                sp.dma_start(square[0][:, :, :], Wout.rearrange("h e d -> (h e) d").rearrange("(c p) d -> p c d", p=P)).then_inc(square_in, 16)
                for t, w in zip(square[1:], (W_in, C)):
                    sp.dma_start(t[:, :, :], w.rearrange("(c p) d -> p c d", p=P)).then_inc(square_in, 16)

            @block.tensor
            def _(pe):
                for n, (m, blocks, _) in enumerate(groups):
                    pe.wait_ge(scaled_done, m + 1)
                    if n >= 2:
                        pe.wait_ge(lo_done, n - 1)
                    for k, (r, c) in enumerate(blocks):
                        mm = nc.tensor.transpose(tps[n % 2][:, k * P:(k + 1) * P], scaled[m][:, r, c * P:(c + 1) * P], g.ident[:, :])
                    mm.then_inc(turned, 1)

            @block.scalar
            def _(act):
                for n, (_, _, parts) in enumerate(groups):
                    act.wait_ge(turned, n + 1)
                    nc.scalar.copy(parts[0], tps[n % 2][:, :]).then_inc(hi_done, 1)
                act.wait_ge(square_in, 48)
                for t, parts in zip(square, squares):
                    nc.scalar.copy(parts[0][:, :, :], t[:, :, :]).then_inc(square_hi, 1)

            @block.vector
            def _(dve):
                dve.wait_ge(whole_in, 48)
                for m in range(3):
                    nc.vector.tensor_scalar(scaled[m][:, :, :], whole[m][:, :, :], SCALE, None, ALU.mult).then_inc(scaled_done, 1)
                for n, (_, _, parts) in enumerate(groups):
                    dve.wait_ge(hi_done, n + 1)
                    nc.vector.tensor_tensor(parts[1], tps[n % 2][:, :], parts[0].bitcast(F32), ALU.subtract).then_inc(lo_done, 1)
                dve.wait_ge(square_in, 48)
                for n, (t, parts) in enumerate(zip(square, squares)):
                    dve.wait_ge(square_hi, n + 1)
                    nc.vector.tensor_tensor(parts[1][:, :, :], t[:, :, :], parts[0][:, :, :].bitcast(F32), ALU.subtract).then_inc(square_lo, 1)
                dve.wait_ge(lo_done, len(groups))
                dve.wait_ge(square_lo, 3)


def build_finish(nc, g, x, b_in, log_A, B_vec, Dv, out):
    with ExitStack() as ctx:
        def sb(name, shape, dt=F32):
            return ctx.enter_context(nc.sbuf_tensor(name, shape, dt))

        def psum(name, shape):
            return ctx.enter_context(nc.psum_tensor(name, shape, F32))

        primed = []

        def sem(name):
            primed.append(ctx.enter_context(nc.semaphore(name)))
            return primed[-1]

        def two(name, shape, dt=F32):
            return [sb(f"{name}{s}", shape, dt) for s in range(2)]

        vecs = sb("vecs", [P, 3, KC])
        decay = sb("decay", [P, KC])
        dmat = sb("dmat", [P, 1, D])
        attn = two("attn", [P, TPC, D])
        x1 = two("x1", [P, TPC, D])
        answer = [two(f"answer{k}", [P, TPC, D]) for k in range(TOPK)]
        index = two("index", [P, TOPK, TPC], U32)
        share = two("share", [P, TOPK, TPC])
        gate1 = sb("gate1", [P, TPC, D])
        gate2 = sb("gate2", [P, TPC, D])
        stats = sb("fstats", [P, TPC, 6])
        mv = sb("fmv", [P, TPC, 2])
        var = sb("fvar", [P, TPC])
        power = sb("power", [P, TPC])
        rstd_power = sb("rstd_power", [P, TPC])
        rstd = sb("frstd", [P, TPC])
        newt = sb("fnewt", [P, TPC])
        xn = two("fxn", [P, TPC, D])
        side = two("side", [P, TPC, D])
        ahi, alo = sb("ahi", [P, KC, CHUNK], F32R), sb("alo", [P, KC, CHUNK], F32R)
        xhi, xlo = two("xhi", [P, KC, CHUNK], F32R), two("xlo", [P, KC, CHUNK], F32R)
        drive = sb("drive", [P, KC, CHUNK])
        state = two("state", [P, KC, CHUNK])
        shi, slo = sb("shi", [P, KC, CHUNK], F32R), sb("slo", [P, KC, CHUNK], F32R)
        act_out = two("fact_out", [P, CHUNK])
        hidden = two("fhidden", [P, CHUNK])
        hhi, hlo = sb("fhhi", [P, HC, CHUNK], F32R), sb("fhlo", [P, HC, CHUNK], F32R)
        tps = psum("ftps", [P, KC, CHUNK])
        yps = psum("yps", [P, TPC, D])
        gps = [psum(f"fgps{n}", [P, CHUNK]) for n in range(2)]
        ups = [psum(f"fups{n}", [P, CHUNK]) for n in range(2)]

        tally = sem("f_tally")
        vecs_in = sem("vecs_in")
        decay_step = sem("decay_step")
        rows_in = [sem(f"rows_in{s}") for s in range(2)]
        index_set = sem("index_set")
        index_tally = sem("index_tally")
        answers_in = [ctx.enter_context(nc.semaphore(f"answers_in{s}")) for s in range(2)]
        share_set = sem("share_set")
        mix_step = sem("mix_step")
        gate1_done = sem("gate1_done")
        attn_turned = sem("attn_turned")
        ahi_done = sem("ahi_done")
        alo_done = sem("alo_done")
        proj_done = sem("proj_done")
        x1_step = sem("x1_step")
        ln_step = sem("ln_step")
        power_set = sem("power_set")
        power_done = sem("power_done")
        xn_done = sem("fxn_done")
        xn_turned = sem("xn_turned")
        xhi_done = sem("xhi_done")
        xlo_done = sem("xlo_done")
        side_done = sem("side_done")
        drive_in = sem("drive_in")
        drive_done = sem("drive_done")
        state_done = sem("state_done")
        shi_done = sem("shi_done")
        slo_done = sem("slo_done")
        recur_done = sem("recur_done")
        recur_kept = sem("recur_kept")
        gate_done = sem("fgate_done")
        up_done = sem("fup_done")
        silu_done = sem("fsilu_done")
        hidden_done = sem("fhidden_done")
        hhi_done = sem("fhhi_done")
        hlo_done = sem("fhlo_done")
        ffn_done = sem("ffn_done")
        gate2_done = sem("gate2_done")
        out_step = sem("out_step")
        out_stored = [sem(f"out_stored{s}") for s in range(2)]
        LN = 7

        def steps(eng, first, body):
            first()
            with eng.Fori(0, B - 1) as i:
                for s in range(2):
                    body(i * 2 + s, s, i, True)
            for s in range(2):
                body((B - 1) * 2 + s, s, B - 1, s == 0)

        def turn(s, i):
            return i if s == 0 else i + 1

        with nc.Block() as block:
            @block.sync
            def _(sp):
                def load(n, s, i):
                    sp.wait_ge(attn_turned, PRIME + n - 1)
                    sp.wait_ge(out_step, PRIME + (n - 1) * 2)
                    tokens = bass.ds(n * CHUNK, CHUNK)
                    sp.dma_start(attn[s][:, :, :], g.attn_rows[tokens, :].rearrange("(t p) d -> p t d", p=P)).then_inc(rows_in[s], 16)
                    sp.dma_start(x1[s][:, :, :], x[tokens, :].rearrange("(t p) d -> p t d", p=P)).then_inc(rows_in[s], 16)

                def body(n, s, i, more):
                    sp.wait_ge(out_step, PRIME + (n + 1) * 2)
                    sp.dma_start(out[bass.ds(n * CHUNK, CHUNK), :].rearrange("(t p) d -> p t d", p=P), side[s][:, :, :]).then_inc(out_stored[s], 16)
                    if not (isinstance(i, int) and i == B - 1):
                        load(n + 2, s, i + 1)

                def first():
                    for n, v in enumerate((b_in, B_vec, log_A)):
                        sp.dma_start(vecs[:, n, :], v.rearrange("(c p) -> p c", p=P),
                                     allow_slow_non_contiguous=True).then_inc(vecs_in, 16)
                    sp.dma_start(dmat[:, 0, :], Dv.unsqueeze(0).broadcast_to([P, D])).then_inc(vecs_in, 16)
                    load(0, 0, 0)
                    load(1, 1, 0)

                steps(sp, first, body)
                for s in range(2):
                    sp.wait_ge(out_stored[s], PRIME + 16 * B)

            @block.gpsimd
            def _(pool):
                prime(pool, primed)

                def gather(n, s, i):
                    pool.wait_ge(gate1_done, PRIME + n - 1)
                    if not (isinstance(i, int) and i == 0):
                        pool.wait_ge(answers_in[s], 16 * TOPK * TPC * i)
                    nc.gpsimd.tensor_copy(index[s][:, :, :], g.slots[:, :, bass.ds(n * TPC, TPC)]).then_inc(index_set, 1)
                    pool.wait_ge(index_set, PRIME + n + 1)
                    pool.sem_inc(index_tally, 1)
                    for k in range(TOPK):
                        for t in range(TPC):
                            nc.gpsimd.indirect_dma_start(
                                answer[k][s][:, t, :], None, g.answers,
                                bass.IndirectOffsetOnAxis(ap=index[s][:, k, t:t + 1], axis=0)).then_inc(answers_in[s], 16)

                def front(n, s, i):
                    pool.wait_ge(ln_step, PRIME + n * LN + 3)
                    nc.gpsimd.tensor_tensor(power[:, :], var[:, :], rstd_power[:, :], ALU.pow).then_inc(power_done, 1)
                    pool.wait_ge(xn_done, PRIME + (n + 1) * TPC)
                    pool.wait_ge(out_stored[s], PRIME + 16 * i)
                    nc.gpsimd.tensor_tensor(side[s][:, :, :], xn[s][:, :, :], dmat[:, :, :].broadcast_to([P, TPC, D]),
                                            ALU.mult).then_inc(side_done, 1)

                def body(n, s, i, more):
                    if more:
                        front(n + 1, 1 - s, turn(s, i))
                        if not (isinstance(i, int) and i == B - 1):
                            gather(n + 2, s, i + 1)

                def first():
                    nc.gpsimd.memset(rstd_power[:, :], -0.5).then_inc(power_set, 1)
                    pool.wait_ge(power_set, PRIME + 1)
                    pool.wait_ge(vecs_in, PRIME + 64)
                    gather(0, 0, 0)
                    gather(1, 1, 0)
                    front(0, 0, 0)

                steps(pool, first, body)

            @block.tensor
            def _(pe):
                def turn_attn(n, s, i):
                    pe.wait_ge(rows_in[s], PRIME + 32 * (i + 1))
                    pe.wait_ge(drive_done, PRIME + n * KC)
                    for t in range(TPC):
                        for c in range(KC):
                            mm = nc.tensor.transpose(tps[:, c, t * P:(t + 1) * P], attn[s][:, t, c * P:(c + 1) * P], g.ident[:, :])
                    mm.then_inc(attn_turned, 1)

                def rows_product(hi, lo, w, chunks):
                    for t in range(TPC):
                        for c in range(chunks):
                            cols = slice(t * P, (t + 1) * P)
                            mm = split_product(nc, yps[:, t, :], (hi[:, c, cols], lo[:, c, cols]),
                                               (w[0][:, c, :], w[1][:, c, :]), c == 0, c == chunks - 1)
                    return mm

                def project(n):
                    pe.wait_ge(alo_done, PRIME + n + 1)
                    pe.wait_ge(recur_kept, PRIME + n)
                    rows_product(ahi, alo, g.wout, KC).then_inc(proj_done, 1)

                def turn_xn(n, s):
                    pe.wait_ge(xn_done, PRIME + (n + 1) * TPC)
                    pe.wait_ge(alo_done, PRIME + n + 1)
                    for t in range(TPC):
                        for c in range(KC):
                            mm = nc.tensor.transpose(tps[:, c, t * P:(t + 1) * P], xn[s][:, t, c * P:(c + 1) * P], g.ident[:, :])
                    mm.then_inc(xn_turned, 1)

                def recurrence_input(n, s):
                    pe.wait_ge(xlo_done, PRIME + n + 1)
                    for e in range(KC):
                        for c in range(KC):
                            mm = split_product(nc, tps[:, e, :], (g.win[0][:, c, e * P:(e + 1) * P], g.win[1][:, c, e * P:(e + 1) * P]),
                                               (xhi[s][:, c, :], xlo[s][:, c, :]), c == 0, c == KC - 1)
                    mm.then_inc(drive_in, 1)

                def recurrence_output(n):
                    pe.wait_ge(slo_done, PRIME + n + 1)
                    pe.wait_ge(gate2_done, PRIME + n)
                    rows_product(shi, slo, g.cmat, KC).then_inc(recur_done, 1)

                def gate_up(n, s, f):
                    pe.wait_ge(hidden_done, PRIME + n * HC + f - 1)
                    for ps, w, done in ((gps, g.gateT, gate_done), (ups, g.upT, up_done)):
                        for c in range(KC):
                            cols = slice(f * P, (f + 1) * P)
                            mm = split_product(nc, ps[f % 2][:, :], (w[0][:, c, cols], w[1][:, c, cols]),
                                               (xhi[s][:, c, :], xlo[s][:, c, :]), c == 0, c == KC - 1)
                        mm.then_inc(done, 1)

                def down(n, more):
                    pe.wait_ge(hlo_done, PRIME + (n + 1) * HC)
                    if more:
                        pe.wait_ge(x1_step, PRIME + (n + 2) * 2)
                    else:
                        pe.wait_ge(recur_kept, PRIME + n + 1)
                    rows_product(hhi, hlo, g.downT, HC).then_inc(ffn_done, 1)

                def body(n, s, i, more):
                    gate_up(n, s, 0)
                    gate_up(n, s, 1)
                    recurrence_output(n)
                    gate_up(n, s, 2)
                    if more:
                        turn_attn(n + 1, 1 - s, turn(s, i))
                        gate_up(n, s, 3)
                        project(n + 1)
                    else:
                        gate_up(n, s, 3)
                    gate_up(n, s, 4)
                    gate_up(n, s, 5)
                    if more:
                        turn_xn(n + 1, 1 - s)
                    down(n, more)
                    if more:
                        recurrence_input(n + 1, 1 - s)

                def first():
                    turn_attn(0, 0, 0)
                    project(0)
                    turn_xn(0, 0)
                    recurrence_input(0, 0)

                steps(pe, first, body)

            @block.scalar
            def _(act):
                def gate_first(n, s):
                    act.wait_ge(mix_step, PRIME + (n + 1) * 2 * TPC)
                    act.wait_ge(x1_step, PRIME + n * 2)
                    nc.scalar.activation(gate1[:, :, :], answer[0][s][:, :, :], ACT.Silu).then_inc(gate1_done, 1)

                def attn_hi(n):
                    act.wait_ge(attn_turned, PRIME + n + 1)
                    act.wait_ge(proj_done, PRIME + n)
                    nc.scalar.copy(ahi[:, :, :], tps[:, :, :]).then_inc(ahi_done, 1)

                def xn_hi(n, s):
                    act.wait_ge(xn_turned, PRIME + n + 1)
                    act.wait_ge(up_done, PRIME + (n - 1) * HC)
                    nc.scalar.copy(xhi[s][:, :, :], tps[:, :, :]).then_inc(xhi_done, 1)

                def state_hi(n, s):
                    act.wait_ge(state_done, PRIME + (n + 1) * KC)
                    act.wait_ge(recur_done, PRIME + n)
                    nc.scalar.copy(shi[:, :, :], state[s][:, :, :]).then_inc(shi_done, 1)

                def silu(n, f):
                    act.wait_ge(gate_done, PRIME + n * HC + f + 1)
                    act.wait_ge(hidden_done, PRIME + n * HC + f - 1)
                    nc.scalar.activation(act_out[f % 2][:, :], gps[f % 2][:, :], ACT.Silu).then_inc(silu_done, 1)
                    act.wait_ge(hidden_done, PRIME + n * HC + f + 1)
                    if f == 0:
                        act.wait_ge(ffn_done, PRIME + n)
                    nc.scalar.copy(hhi[:, f, :], hidden[f % 2][:, :]).then_inc(hhi_done, 1)

                def gate_second(n):
                    act.wait_ge(ffn_done, PRIME + n + 1)
                    act.wait_ge(out_step, PRIME + n * 2)
                    nc.scalar.activation(gate2[:, :, :], yps[:, :, :], ACT.Silu).then_inc(gate2_done, 1)

                def body(n, s, i, more):
                    silu(n, 0)
                    silu(n, 1)
                    silu(n, 2)
                    if more:
                        attn_hi(n + 1)
                        gate_first(n + 1, 1 - s)
                    silu(n, 3)
                    silu(n, 4)
                    silu(n, 5)
                    if more:
                        xn_hi(n + 1, 1 - s)
                    gate_second(n)
                    if more:
                        state_hi(n + 1, 1 - s)

                def first():
                    act.wait_ge(vecs_in, PRIME + 64)
                    nc.scalar.activation(decay[:, :], vecs[:, 2, :], ACT.Exp).then_inc(decay_step, 1)
                    attn_hi(0)
                    gate_first(0, 0)
                    xn_hi(0, 0)
                    state_hi(0, 0)

                steps(act, first, body)

            @block.vector
            def _(dve):
                def mix(n, s, i):
                    nc.vector.tensor_copy(share[s][:, :, :], g.weights[:, :, bass.ds(n * TPC, TPC)]).then_inc(share_set, 1)
                    dve.wait_ge(share_set, PRIME + n + 1)
                    dve.wait_ge(answers_in[s], 16 * TOPK * TPC * (i + 1))
                    for t in range(TPC):
                        nc.vector.tensor_scalar(answer[0][s][:, t, :], answer[0][s][:, t, :], share[s][:, 0, t:t + 1], None,
                                                ALU.mult).then_inc(mix_step, 1)
                    for t in range(TPC):
                        dve.wait_ge(mix_step, PRIME + n * 2 * TPC + TPC + t)
                        nc.vector.scalar_tensor_tensor(out=answer[0][s][:, t, :], in0=answer[1][s][:, t, :],
                                                       scalar=share[s][:, 1, t:t + 1], in1=answer[0][s][:, t, :],
                                                       op0=ALU.mult, op1=ALU.add).then_inc(mix_step, 1)

                def attn_lo(n):
                    dve.wait_ge(ahi_done, PRIME + n + 1)
                    nc.vector.tensor_tensor(alo[:, :, :], tps[:, :, :], ahi[:, :, :].bitcast(F32), ALU.subtract).then_inc(alo_done, 1)

                def add_first(n, s, i):
                    dve.wait_ge(proj_done, PRIME + n + 1)
                    dve.wait_ge(gate1_done, PRIME + n + 1)
                    dve.wait_ge(rows_in[s], PRIME + 32 * (i + 1))
                    nc.vector.tensor_tensor(attn[s][:, :, :], yps[:, :, :], gate1[:, :, :], ALU.mult).then_inc(x1_step, 1)
                    dve.wait_ge(x1_step, PRIME + 2 * n + 1)
                    nc.vector.tensor_tensor(x1[s][:, :, :], x1[s][:, :, :], attn[s][:, :, :], ALU.add).then_inc(x1_step, 1)

                def layernorm(n, s):
                    base = n * LN
                    dve.wait_ge(x1_step, PRIME + 2 * n + 2)
                    for t in range(TPC):
                        last = nc.vector.bn_stats(stats[:, t, :], x1[s][:, t, :])
                    last.then_inc(ln_step, 1)
                    dve.wait_ge(ln_step, PRIME + base + 1)
                    dve.sem_inc(tally, 1)
                    for t in range(TPC):
                        last = nc.vector.bn_aggr(mv[:, t, :], stats[:, t, :])
                    last.then_inc(ln_step, 1)
                    dve.wait_ge(ln_step, PRIME + base + 2)
                    nc.vector.tensor_scalar(var[:, :], mv[:, :, 1], EPS, None, ALU.add).then_inc(ln_step, 1)
                    dve.wait_ge(power_done, PRIME + n + 1)
                    nc.vector.tensor_tensor(newt[:, :], power[:, :], power[:, :], ALU.mult).then_inc(ln_step, 1)
                    dve.wait_ge(ln_step, PRIME + base + 4)
                    nc.vector.tensor_tensor(newt[:, :], newt[:, :], var[:, :], ALU.mult).then_inc(ln_step, 1)
                    dve.wait_ge(ln_step, PRIME + base + 5)
                    nc.vector.tensor_scalar(newt[:, :], newt[:, :], -0.5, 1.5, ALU.mult, ALU.add).then_inc(ln_step, 1)
                    dve.wait_ge(ln_step, PRIME + base + 6)
                    nc.vector.tensor_tensor(rstd[:, :], power[:, :], newt[:, :], ALU.mult).then_inc(ln_step, 1)
                    dve.wait_ge(ln_step, PRIME + base + 7)
                    dve.wait_ge(xn_turned, PRIME + n - 1)
                    dve.wait_ge(side_done, PRIME + n - 1)
                    for t in range(TPC):
                        nc.vector.tensor_scalar(xn[s][:, t, :], x1[s][:, t, :], mv[:, t, 0:1], rstd[:, t:t + 1],
                                                ALU.subtract, ALU.mult).then_inc(xn_done, 1)

                def xn_lo(n, s):
                    dve.wait_ge(xhi_done, PRIME + n + 1)
                    nc.vector.tensor_tensor(xlo[s][:, :, :], tps[:, :, :], xhi[s][:, :, :].bitcast(F32), ALU.subtract).then_inc(xlo_done, 1)

                def recur(n, s):
                    dve.wait_ge(drive_in, PRIME + n + 1)
                    for e in range(KC):
                        nc.vector.tensor_scalar(drive[:, e, :], tps[:, e, :], vecs[:, 0, e:e + 1], vecs[:, 1, e:e + 1],
                                                ALU.add, ALU.mult).then_inc(drive_done, 1)
                    for e in range(KC):
                        dve.wait_ge(drive_done, PRIME + n * KC + e + 1)
                        nc.vector.tensor_tensor_scan(state[s][:, e, :], decay[:, e:e + 1].broadcast_to([P, CHUNK]), drive[:, e, :],
                                                     0.0 if s == 0 else state[0][:, e, CHUNK - 1:CHUNK],
                                                     ALU.mult, ALU.add).then_inc(state_done, 1)
                    dve.wait_ge(shi_done, PRIME + n + 1)
                    nc.vector.tensor_tensor(slo[:, :, :], state[s][:, :, :], shi[:, :, :].bitcast(F32), ALU.subtract).then_inc(slo_done, 1)

                def keep_recurrence(n, s):
                    dve.wait_ge(recur_done, PRIME + n + 1)
                    dve.wait_ge(side_done, PRIME + n + 1)
                    nc.vector.tensor_tensor(side[s][:, :, :], yps[:, :, :], side[s][:, :, :], ALU.add).then_inc(recur_kept, 1)

                def multiply(n, f):
                    dve.wait_ge(silu_done, PRIME + n * HC + f + 1)
                    dve.wait_ge(up_done, PRIME + n * HC + f + 1)
                    dve.wait_ge(hlo_done, PRIME + n * HC + f - 1)
                    nc.vector.tensor_tensor(hidden[f % 2][:, :], act_out[f % 2][:, :], ups[f % 2][:, :], ALU.mult).then_inc(hidden_done, 1)
                    dve.wait_ge(hidden_done, PRIME + n * HC + f + 1)
                    dve.wait_ge(hhi_done, PRIME + n * HC + f + 1)
                    nc.vector.tensor_tensor(hlo[:, f, :], hidden[f % 2][:, :], hhi[:, f, :].bitcast(F32), ALU.subtract).then_inc(hlo_done, 1)

                def add_second(n, s):
                    dve.wait_ge(gate2_done, PRIME + n + 1)
                    dve.wait_ge(recur_kept, PRIME + n + 1)
                    nc.vector.tensor_tensor(side[s][:, :, :], side[s][:, :, :], gate2[:, :, :], ALU.mult).then_inc(out_step, 1)
                    dve.wait_ge(out_step, PRIME + 2 * n + 1)
                    nc.vector.tensor_tensor(side[s][:, :, :], side[s][:, :, :], x1[s][:, :, :], ALU.add).then_inc(out_step, 1)

                def body(n, s, i, more):
                    if more:
                        mix(n + 1, 1 - s, turn(s, i))
                    multiply(n, 0)
                    multiply(n, 1)
                    keep_recurrence(n, s)
                    multiply(n, 2)
                    if more:
                        attn_lo(n + 1)
                    multiply(n, 3)
                    if more:
                        add_first(n + 1, 1 - s, turn(s, i))
                    multiply(n, 4)
                    if more:
                        layernorm(n + 1, 1 - s)
                    multiply(n, 5)
                    if more:
                        xn_lo(n + 1, 1 - s)
                    add_second(n, s)
                    if more:
                        recur(n + 1, 1 - s)

                def first():
                    dve.wait_ge(decay_step, PRIME + 1)
                    nc.vector.tensor_scalar(decay[:, :], decay[:, :], -1.0, None, ALU.mult).then_inc(decay_step, 1)
                    dve.wait_ge(decay_step, PRIME + 2)
                    mix(0, 0, 0)
                    attn_lo(0)
                    add_first(0, 0, 0)
                    layernorm(0, 0)
                    xn_lo(0, 0)
                    recur(0, 0)

                steps(dve, first, body)


def build(nc, ins, out):
    g = Shared()
    (x, Wq, Wk, Wv, Wout, router_w, wg, wu, wd, W_in, b_in, log_A, B_vec, C, Dv, w_gate, w_up, w_down) = ins
    x = x.rearrange("b l d -> (b l) d")
    out = out.rearrange("b l d -> (b l) d")
    g.qk_parts = nc.dram_tensor("qk_parts", [2, PARTS, H * DH, N], BF16, kind="Internal").ap()
    g.v_rows = nc.dram_tensor("v_rows", [B * QUADS, P, QT, 4 * VW], F32, kind="Internal").ap()
    g.queues = nc.dram_tensor("queues", [E * CAP, D], F32, kind="Internal").ap()
    g.answers = nc.dram_tensor("answers", [E * CAP + P, D], F32, kind="Internal").ap()
    g.attn_rows = nc.dram_tensor("attn_rows", [N, D], F32, kind="Internal").ap()
    with ExitStack() as ctx:
        g.logits = ctx.enter_context(nc.sbuf_tensor("logits", [P, NT, E], F32))
        g.weights = ctx.enter_context(nc.sbuf_tensor("weights", [P, TOPK, NT], F32))
        g.slots = ctx.enter_context(nc.sbuf_tensor("slots", [P, TOPK, NT], U32))
        build_constants(nc, ctx, g)
        with nc.sbuf_tensor("xn_all", [P, NT, D], F32) as g.xn_all:
            build_project(nc, g, x, Wq, Wk, Wv, router_w)
            build_attend(nc, g)
            build_route(nc, g)
        build_experts(nc, g, wg, wu, wd)
        build_ffn_weights(nc, ctx, g, Wout, W_in, C, w_gate, w_up, w_down)
        build_finish(nc, g, x, b_in, log_A, B_vec, Dv, out)
    return g


_INS = ["L0_attn_x", "L0_attn_Wq", "L0_attn_Wk", "L0_attn_Wv", "L0_attn_Wout", "L0_ffn_router_w", "L0_ffn_wg",
        "L0_ffn_wu", "L0_ffn_wd", "L1_attn_W_in", "L1_attn_b_in", "L1_attn_log_A", "L1_attn_B_vec", "L1_attn_C",
        "L1_attn_D", "L1_ffn_w_gate", "L1_ffn_w_up", "L1_ffn_w_down"]


def kernel(**inputs):
    import numpy as _np
    import concourse.bacc as _bacc
    from concourse import mybir as _mybir
    from concourse.bass_utils import run_bass_kernel_spmd as _run

    nc = _bacc.Bacc("TRN2", target_bir_lowering=False, num_devices=1)
    arrays, args = {}, []
    for name in _INS:
        a = _np.ascontiguousarray(inputs[name])
        arrays[f"in_{name}"] = a
        args.append(nc.dram_tensor(f"in_{name}", a.shape, _mybir.dt.from_np(a.dtype), kind="ExternalInput").ap())
    out = nc.dram_tensor("out", (B, L, D), F32, kind="ExternalOutput").ap()
    build(nc, args, out)
    r = _run(nc, [arrays], core_ids=[0])
    return r.results[0]["out"]
```

```python
from contextlib import ExitStack

import concourse.bass as bass
from concourse import mybir

F32 = mybir.dt.float32
F32R = mybir.dt.float32r
BF16 = mybir.dt.bfloat16
I32 = mybir.dt.int32
U32 = mybir.dt.uint32
ALU = mybir.AluOpType
ACT = mybir.ActivationFunctionType
AX = mybir.AxisListType

P = 128
BANK = 512
B, L, D = 4, 1024, 256
H, DH = 16, 16
N = B * L
NT = N // P
KC = D // P
CHUNK = 512
TPC = CHUNK // P
QUADS = H // 4
QT = L // P
PARTS = 3
VW = DH + 1
E, F = 8, 1024
FC = F // P
TOPK = 2
CAP = int(1.25 * N / E)
CT = CAP // P
EPS = 1e-5
MASKED = -1e38
TERMS = [(0, 0), (0, 1), (1, 0), (1, 1), (0, 2), (2, 0)]
WCOLS = KC * F
MATS = 3
STACK = len(TERMS) * DH
MAXROWS = PARTS


PRIME = 16


def prime(engine, semaphores):
    for s in semaphores:
        engine.sem_inc(s, PRIME)


class Shared:

    def raw(g, m):
        return g.fresh[:, m, :]

    def parts(g, m):
        return g.split[:, m, :], g.split[:, MATS + m, :]


def build_constants(nc, ctx, g):
    def sb(name, shape, dt):
        return ctx.enter_context(nc.sbuf_tensor(name, shape, dt))

    g.ident = sb("ident", [P, P], F32)
    g.identb = sb("identb", [P, P], BF16)
    g.maskneg = sb("maskneg", [P, P], BF16)
    filled = ctx.enter_context(nc.semaphore("filled"))
    cut = ctx.enter_context(nc.semaphore("cut"))
    with nc.Block() as block:
        @block.gpsimd
        def _(pool):
            nc.gpsimd.memset(g.ident[:, :], 0.0).then_inc(filled, 1)
            nc.gpsimd.memset(g.identb[:, :], 0.0).then_inc(filled, 1)
            nc.gpsimd.memset(g.maskneg[:, :], 0.0).then_inc(filled, 1)
            pool.wait_ge(filled, 3)
            for t in (g.ident, g.identb):
                nc.gpsimd.affine_select(out=t[:, :], in_=t[:, :], compare_op=ALU.not_equal, fill=1.0,
                                        base=0, pattern=[[-1, P]], channel_multiplier=1).then_inc(cut, 1)
            nc.gpsimd.affine_select(out=g.maskneg[:, :], in_=g.maskneg[:, :], compare_op=ALU.is_ge,
                                    fill=MASKED, base=0, pattern=[[-1, P]],
                                    channel_multiplier=1).then_inc(cut, 1)
            pool.wait_ge(cut, 3)


BITS = 30


def split_product(nc, out, left, right, first, last):
    nc.tensor.matmul(out, left[0], right[0], start=first, stop=False)
    nc.tensor.matmul(out, left[1], right[0], start=False, stop=False)
    return nc.tensor.matmul(out, left[0], right[1], start=False, stop=last)


def build_project(nc, g, x, Wq, Wk, Wv, router_w):
    MC = 2 * KC
    with ExitStack() as ctx:
        def sb(name, shape, dt=F32):
            return ctx.enter_context(nc.sbuf_tensor(name, shape, dt))

        def psum(name, shape):
            return ctx.enter_context(nc.psum_tensor(name, shape, F32))

        primed = []

        def sem(name):
            primed.append(ctx.enter_context(nc.semaphore(name)))
            return primed[-1]

        def two(name, shape, dt=F32):
            return [sb(f"{name}{s}", shape, dt) for s in range(2)]

        wqkv = sb("wqkv", [P, 3, KC, D])
        whi, wlo = [g.split[:, n, 0:3 * KC * D].rearrange("p (m c d) -> p m c d", m=3, c=KC) for n in range(2)]
        rw = sb("rw", [E, D])
        rwT = sb("rwT", [P, KC, E])
        eps = sb("eps", [P, 1])
        zeros = sb("zeros", [P, 4 * D])
        xin = [g.fresh[:, 0, s * TPC * D:(s + 1) * TPC * D].rearrange("p (t d) -> p t d", t=TPC) for s in range(2)]
        stats = two("stats", [P, TPC, 6])
        mv = two("mv", [P, TPC, 2])
        std = two("std", [P, TPC])
        rstd = two("rstd", [P, TPC])
        newt = two("newt", [P, TPC])
        xn = [g.fresh[:, 1, s * TPC * D:(s + 1) * TPC * D].rearrange("p (t d) -> p t d", t=TPC) for s in range(2)]
        xnT = two("xnT", [P, KC, CHUNK])
        turned_all = sb("turned_all", [P, KC, N])
        xhi, xlo = [[g.split[:, n, s * KC * CHUNK:(s + 1) * KC * CHUNK].rearrange("p (c t) -> p c t", c=KC)
                     for s in range(2)] for n in (2, 3)]
        rest = two("rest", [P, CHUNK])
        parts = two("parts", [P, MC, PARTS, CHUNK], BF16)
        vrow = two("vrow", [P, TPC, H, VW])
        logits = sb("logits", [P, NT, E])
        prob = sb("prob", [P, NT, E])
        left = sb("left", [P, NT, E])
        pick = sb("pick", [P, NT, E])
        hot = two("hot", [P, NT, E])
        gate = sb("gate", [P, NT, E])
        back = sb("back", [P, 1, E])
        row = sb("row", [P, NT])
        top = two("top", [P, NT])
        total = sb("total", [P, NT])
        limit = sb("limit", [P, E], I32)
        trial = sb("trial", [P, E], I32)
        bit = sb("bit", [P, E], I32)
        grow = sb("grow", [P, E], I32)
        over = sb("over", [P, E, NT], BF16)
        count = sb("count", [P, E], BF16)
        above = sb("above", [P, E, NT])
        ties = sb("ties", [P, E, NT], BF16)
        need = sb("need", [P, E])
        kept = sb("kept", [P, E, NT], BF16)
        start = sb("start", [P, E, NT])
        resets = sb("resets", [P, E, NT])
        slot = sb("slot", [P, E, NT])
        base = sb("base", [P, E, 1])
        ones = sb("ones", [P, P], BF16)
        before = sb("before", [P, P], BF16)
        turned = psum("turned", [P, KC, CHUNK])
        qk = [psum(f"qk{m}", [P, CHUNK]) for m in range(2)]
        vps = psum("vps", [P, TPC, D])
        lps = psum("lps", [P, TPC, E])
        counted = psum("counted", [P, E])
        ranked, tiles = qk[0][:, 0:E * NT], qk[1][:, 0:E * NT]

        weights_in = sem("weights_in")
        x_in = [sem(f"x_in{s}") for s in range(2)]
        tally = sem("p_tally")
        stats_done = sem("stats_done")
        var_done = sem("var_done")
        std_done = sem("std_done")
        rstd_step = sem("rstd_step")
        xn_done = sem("xn_done")
        xn_kept = sem("xn_kept")
        turned_done = sem("turned_done")
        xnT_done = sem("xnT_done")
        turned_kept = sem("turned_kept")
        logits_done = sem("logits_done")
        logits_kept = sem("logits_kept")
        whi_done = sem("pwhi_done")
        wlo_done = sem("pwlo_done")
        xhi_done = sem("pxhi_done")
        xlo_done = sem("pxlo_done")
        qk_done = sem("qk_done")
        hi_done = sem("hi_done")
        rest_done = sem("rest_done")
        mid_done = sem("mid_done")
        lo_done = sem("lo_done")
        v_done = sem("v_done")
        v_kept = sem("v_kept")
        stored = [sem(f"stored{s}") for s in range(2)]
        filled = sem("p_filled")
        cut = sem("p_cut")
        rw_turned = sem("rw_turned")
        rw_done = sem("rw_done")
        zeroed = sem("zeroed")
        zeros_out = sem("zeros_out")
        shifted = sem("shifted")
        exp_done = sem("r_exp_done")
        step = sem("r_step")
        trial_done = sem("trial_done")
        trial_step = sem("trial_step")
        count_done = sem("count_done")
        prefix_in = sem("prefix_in")
        prefix_done = sem("prefix_done")
        NEWTON = 4
        FILLS = 3 + 4 + 2 * E
        TRIALSTEPS = 5
        TRIALS = 2 * B * MC
        assert TRIALS >= BITS

        def chunk(i, s):
            return bass.ds(i * L + s * CHUNK, CHUNK)

        def rows(eng, body):
            with eng.Fori(0, B - 1) as i:
                for s in range(2):
                    body(i, s, True)
            for s in range(2):
                body(B - 1, s, s == 0)

        with nc.Block() as block:
            @block.sync
            def _(sp):
                def load(i, s):
                    sp.dma_start(xin[s][:, :, :], x[chunk(i, s), :].rearrange("(t p) d -> p t d", p=P)).then_inc(x_in[s], 16)

                load(0, 0)
                load(0, 1)
                sp.dma_start(rw[:, :], router_w).then_inc(weights_in, 16)
                for n, w in enumerate((Wq, Wk, Wv)):
                    sp.dma_start(wqkv[:, n, :, :], w.rearrange("(c p) h e -> p c (h e)", p=P)).then_inc(weights_in, 16)
                sp.wait_ge(zeroed, PRIME + 1)
                for r in range(0, E * CAP, 4 * P):
                    sp.dma_start(g.queues[r:r + 4 * P, :].rearrange("(p c) d -> p (c d)", c=4), zeros[:, :]).then_inc(zeros_out, 16)
                sp.dma_start(g.answers[E * CAP:E * CAP + P, :], zeros[:, 0:D]).then_inc(zeros_out, 16)
                with sp.Fori(0, B - 1) as i:
                    for s in range(2):
                        sp.wait_ge(xn_done, PRIME + (i * 2 + s + 1) * TPC)
                        load(i + 1, s)
                with sp.Fori(0, B) as i:
                    for s in range(2):
                        n = i * 2 + s
                        for m in range(MC):
                            sp.wait_ge(lo_done, PRIME + n * MC + m + 1)
                            sp.dma_start(g.qk_parts[m // KC, :, (m % KC) * P:(m % KC + 1) * P, chunk(i, s)].rearrange(
                                "r p t -> p r t"), parts[s][:, m, :, :]).then_inc(stored[s], 16)
                        sp.wait_ge(v_kept, PRIME + n + 1)
                        for q in range(QUADS):
                            sp.dma_start(g.v_rows[bass.ds(i * QUADS + q, 1), :, s * TPC:(s + 1) * TPC, :].rearrange(
                                "o p t c -> p (o t) c"),
                                vrow[s][:, :, 4 * q:4 * q + 4, :].rearrange("p t h c -> p t (h c)")).then_inc(stored[s], 16)
                for s in range(2):
                    sp.wait_ge(stored[s], PRIME + 16 * B * (MC + QUADS))
                sp.wait_ge(zeros_out, PRIME + 16 * (E * CT // 4 + 1))

            @block.gpsimd
            def _(pool):
                prime(pool, primed)
                nc.gpsimd.memset(zeros[:, :], 0.0).then_inc(zeroed, 1)
                nc.gpsimd.memset(eps[:, :], EPS).then_inc(filled, 1)
                for s in range(2):
                    nc.gpsimd.memset(vrow[s][:, :, :, DH:VW], 1.0).then_inc(filled, 1)
                nc.gpsimd.memset(ones[:, :], 1.0).then_inc(filled, 1)
                nc.gpsimd.memset(limit[:, :], 0).then_inc(filled, 1)
                nc.gpsimd.memset(bit[:, :], 1 << (BITS - 1)).then_inc(filled, 1)
                nc.gpsimd.memset(resets[:, :, :], 1.0).then_inc(filled, 1)
                pool.wait_ge(filled, PRIME + 7)
                nc.gpsimd.affine_select(out=before[:, :], in_=ones[:, :], compare_op=ALU.is_gt, fill=0.0,
                                        base=0, pattern=[[1, P]], channel_multiplier=-1).then_inc(cut, 1)
                nc.gpsimd.memset(resets[:, :, 0:1], 0.0).then_inc(cut, 1)
                for e in range(E):
                    nc.gpsimd.memset(back[:, 0, e:e + 1], float(E - e)).then_inc(filled, 1)
                    nc.gpsimd.memset(base[:, e, :], float(e * CAP - E * CAP)).then_inc(filled, 1)

                def low_rows(n, i, s):
                    pool.wait_ge(xhi_done, PRIME + n + 1)
                    nc.gpsimd.tensor_tensor(xlo[s][:, :, :], turned_all[:, :, chunk(i, s)], xhi[s][:, :, :].bitcast(F32),
                                            ALU.subtract).then_inc(xlo_done, 1)

                def body(i, s, more):
                    n = i * 2 + s
                    for m in range(MC):
                        if m == 2 and more:
                            low_rows(n + 1, i + s, 1 - s)
                        pool.wait_ge(mid_done, PRIME + n * MC + m + 1)
                        nc.gpsimd.tensor_tensor(parts[s][:, m, 2, :], rest[m % 2][:, :], parts[s][:, m, 1, :],
                                                ALU.subtract).then_inc(lo_done, 1)

                low_rows(0, 0, 0)
                rows(pool, body)

            @block.tensor
            def _(pe):
                pe.wait_ge(weights_in, PRIME + 64)
                for c in range(KC):
                    nc.tensor.transpose(turned[:, 0, c * E:(c + 1) * E], rw[:, c * P:(c + 1) * P],
                                        g.ident[0:E, 0:E]).then_inc(rw_turned, 1)
                pe.wait_ge(rw_done, PRIME + 1)
                with pe.Fori(0, B) as i:
                    for s in range(2):
                        n = i * 2 + s
                        pe.wait_ge(xn_done, PRIME + (n + 1) * TPC)
                        pe.wait_ge(xnT_done, PRIME + n)
                        for t in range(TPC):
                            for c in range(KC):
                                mm = nc.tensor.transpose(turned[:, c, t * P:(t + 1) * P],
                                                         xn[s][:, t, c * P:(c + 1) * P], g.ident[:, :])
                        mm.then_inc(turned_done, 1)
                        pe.wait_ge(xnT_done, PRIME + n + 1)
                        pe.wait_ge(logits_kept, PRIME + n)
                        for t in range(TPC):
                            for c in range(KC):
                                mm = nc.tensor.matmul(lps[:, t, :], xnT[s][:, c, t * P:(t + 1) * P],
                                                      rwT[:, c, :], start=c == 0, stop=c == KC - 1)
                        mm.then_inc(logits_done, 1)

                def query_key(n, s, m):
                    pe.wait_ge(rest_done, PRIME + n * MC + m - 1)
                    cols = slice((m % KC) * P, (m % KC + 1) * P)
                    for c in range(KC):
                        mm = split_product(nc, qk[m % 2][:, :], (whi[:, m // KC, c, cols], wlo[:, m // KC, c, cols]),
                                           (xhi[s][:, c, :], xlo[s][:, c, :]), c == 0, c == KC - 1)
                    mm.then_inc(qk_done, 1)

                def body(i, s, more):
                    n = i * 2 + s
                    pe.wait_ge(xlo_done, PRIME + n + 1)
                    query_key(n, s, 0)
                    for m in range(MC):
                        if m < MC - 1:
                            query_key(n, s, m + 1)
                        if m == 0:
                            pe.wait_ge(v_kept, PRIME + n)
                        for c in range(KC):
                            cols = slice(m * P, (m + 1) * P)
                            mm = split_product(nc, vps[:, m, :], (xhi[s][:, c, cols], xlo[s][:, c, cols]),
                                               (whi[:, 2, c, :], wlo[:, 2, c, :]), c == 0, c == KC - 1)
                        if m == MC - 1:
                            mm.then_inc(v_done, 1)
                        pe.wait_ge(trial_done, PRIME + n * MC + m + 1)
                        nc.tensor.matmul(counted[:, :], ones[:, :], count[:, :], start=True, stop=True).then_inc(count_done, 1)

                pe.wait_ge(wlo_done, PRIME + 3)
                pe.wait_ge(filled, PRIME + FILLS)
                pe.wait_ge(cut, PRIME + 2)
                rows(pe, body)
                pe.wait_ge(trial_done, PRIME + TRIALS + 1)
                nc.tensor.matmul(counted[:, :], ones[:, :], count[:, :], start=True, stop=True).then_inc(count_done, 1)
                pe.wait_ge(rest_done, PRIME + 2 * B * MC)
                for n, marks in enumerate((ties, kept)):
                    pe.wait_ge(prefix_in, PRIME + n + 1)
                    flat = marks[:, :, :].rearrange("p e t -> p (e t)")
                    nc.tensor.matmul(ranked, before[:, :], flat, start=True, stop=True)
                    nc.tensor.matmul(tiles, ones[:, :], flat, start=True, stop=True).then_inc(prefix_done, 1)

            @block.scalar
            def _(act):
                act.wait_ge(filled, PRIME + 3)
                with act.Fori(0, B) as i:
                    for s in range(2):
                        n = i * 2 + s
                        act.wait_ge(var_done, PRIME + (n + 1) * TPC)
                        nc.scalar.activation(std[s][:, :], mv[s][:, :, 1], ACT.Sqrt,
                                             bias=eps[:, 0:1]).then_inc(std_done, 1)
                        act.wait_ge(turned_done, PRIME + n + 1)
                        act.wait_ge(logits_done, PRIME + n - 1)
                        act.wait_ge(turned_kept, PRIME + n - 1)
                        nc.scalar.copy(xnT[s][:, :, :], turned[:, :, :]).then_inc(xnT_done, 1)
                        nc.scalar.copy(g.xn_all[:, bass.ds(i * QT + s * TPC, TPC), :], xn[s][:, :, :]).then_inc(xn_kept, 1)
                for m in range(3):
                    nc.scalar.copy(whi[:, m, :, :], wqkv[:, m, :, :]).then_inc(whi_done, 1)

                def high_rows(n, i, s):
                    act.wait_ge(turned_kept, PRIME + n + 1)
                    act.wait_ge(v_done, PRIME + n - 1)
                    nc.scalar.copy(xhi[s][:, :, :], turned_all[:, :, chunk(i, s)]).then_inc(xhi_done, 1)

                def mid(n, s, m):
                    act.wait_ge(rest_done, PRIME + n * MC + m + 1)
                    nc.scalar.copy(parts[s][:, m, 1, :], rest[m % 2][:, :]).then_inc(mid_done, 1)

                def body(i, s, more):
                    n = i * 2 + s
                    act.wait_ge(stored[s], PRIME + i * (16 * (MC + QUADS)))
                    for m in range(MC):
                        act.wait_ge(qk_done, PRIME + n * MC + m + 1)
                        nc.scalar.mul(parts[s][:, m, 0, :], qk[m % 2][:, :], DH ** -0.5 if m < KC else 1.0).then_inc(hi_done, 1)
                        if m:
                            mid(n, s, m - 1)
                        if m == 1 and more:
                            high_rows(n + 1, i + s, 1 - s)
                    mid(n, s, MC - 1)
                    act.wait_ge(v_done, PRIME + n + 1)
                    nc.scalar.copy(vrow[s][:, :, :, 0:DH], vps[:, :, :].rearrange("p t (h e) -> p t h e", e=DH)).then_inc(v_kept, 1)

                high_rows(0, 0, 0)
                act.wait_ge(shifted, PRIME + 1)
                nc.scalar.activation(prob[:, :, :], left[:, :, :], ACT.Exp).then_inc(exp_done, 1)
                rows(act, body)

            @block.vector
            def _(dve):
                def layernorm(n, i, s):
                    dve.wait_ge(x_in[s], PRIME + i * 16 + 16)
                    for t in range(TPC):
                        nc.vector.bn_stats(stats[s][:, t, :], xin[s][:, t, :]).then_inc(stats_done, 1)
                    dve.wait_ge(stats_done, PRIME + (n + 1) * TPC)
                    dve.sem_inc(tally, 1)
                    for t in range(TPC):
                        nc.vector.bn_aggr(mv[s][:, t, :], stats[s][:, t, :]).then_inc(var_done, 1)
                    dve.wait_ge(std_done, PRIME + n + 1)
                    nc.vector.reciprocal(rstd[s][:, :], std[s][:, :]).then_inc(rstd_step, 1)
                    first = n * (NEWTON + 1)
                    dve.wait_ge(rstd_step, PRIME + first + 1)
                    nc.vector.tensor_tensor(newt[s][:, :], rstd[s][:, :], rstd[s][:, :], ALU.mult).then_inc(rstd_step, 1)
                    dve.wait_ge(rstd_step, PRIME + first + 2)
                    nc.vector.scalar_tensor_tensor(out=newt[s][:, :], in0=mv[s][:, :, 1], scalar=EPS, in1=newt[s][:, :],
                                                   op0=ALU.add, op1=ALU.mult).then_inc(rstd_step, 1)
                    dve.wait_ge(rstd_step, PRIME + first + 3)
                    nc.vector.tensor_scalar(newt[s][:, :], newt[s][:, :], -0.5, 1.5, ALU.mult, ALU.add).then_inc(rstd_step, 1)
                    dve.wait_ge(rstd_step, PRIME + first + 4)
                    nc.vector.tensor_tensor(rstd[s][:, :], rstd[s][:, :], newt[s][:, :], ALU.mult).then_inc(rstd_step, 1)
                    dve.wait_ge(rstd_step, PRIME + first + 5)
                    dve.wait_ge(xn_kept, PRIME + n - 1)
                    dve.wait_ge(turned_done, PRIME + n - 1)
                    for t in range(TPC):
                        nc.vector.tensor_scalar(xn[s][:, t, :], xin[s][:, t, :], mv[s][:, t, 0:1], rstd[s][:, t:t + 1],
                                                ALU.subtract, ALU.mult).then_inc(xn_done, 1)

                def keep(n, i, s):
                    dve.wait_ge(xnT_done, PRIME + n + 1)
                    nc.vector.tensor_copy(turned_all[:, :, chunk(i, s)], xnT[s][:, :, :]).then_inc(turned_kept, 1)
                    dve.wait_ge(logits_done, PRIME + n + 1)
                    nc.vector.tensor_copy(logits[:, bass.ds(i * QT + s * TPC, TPC), :], lps[:, :, :]).then_inc(logits_kept, 1)

                dve.wait_ge(rw_turned, PRIME + KC)
                nc.vector.tensor_copy(rwT[:, :, :], turned[:, 0, 0:KC * E].rearrange("p (c e) -> p c e", c=KC)).then_inc(rw_done, 1)
                layernorm(0, 0, 0)
                with dve.Fori(0, B - 1) as i:
                    layernorm(i * 2 + 1, i, 1)
                    keep(i * 2, i, 0)
                    layernorm(i * 2 + 2, i + 1, 0)
                    keep(i * 2 + 1, i, 1)
                layernorm(2 * B - 1, B - 1, 1)
                keep(2 * B - 2, B - 1, 0)
                keep(2 * B - 1, B - 1, 1)
                for m in range(3):
                    dve.wait_ge(whi_done, PRIME + m + 1)
                    nc.vector.tensor_tensor(wlo[:, m, :, :], wqkv[:, m, :, :], whi[:, m, :, :].bitcast(F32),
                                            ALU.subtract).then_inc(wlo_done, 1)

                chain = [PRIME]

                def link(ins):
                    chain[0] += 1
                    ins.then_inc(step, 1)
                    dve.wait_ge(step, chain[0])

                def by_expert(t):
                    return t[:, :, :].rearrange("p t e -> p e t")

                def over_experts(t):
                    return t[:, :].unsqueeze(2).broadcast_to([P, NT, E])

                def over_tiles(t):
                    return t[:, :].unsqueeze(2).broadcast_to([P, E, NT])

                dve.wait_ge(logits_kept, PRIME + 2 * B)
                link(nc.vector.tensor_reduce(row[:, :], logits[:, :, :], AX.X, ALU.max))
                nc.vector.tensor_tensor(left[:, :, :], logits[:, :, :], over_experts(row), ALU.subtract).then_inc(shifted, 1)
                dve.wait_ge(exp_done, PRIME + 1)
                link(nc.vector.tensor_reduce(total[:, :], prob[:, :, :], AX.X, ALU.add))
                link(nc.vector.reciprocal(row[:, :], total[:, :]))
                link(nc.vector.tensor_tensor(prob[:, :, :], prob[:, :, :], over_experts(row), ALU.mult))
                dve.wait_ge(filled, PRIME + FILLS)
                dve.wait_ge(cut, PRIME + 2)
                backwards = back[:, :, :].broadcast_to([P, NT, E])
                now = prob
                for k in range(TOPK):
                    link(nc.vector.tensor_reduce(top[k][:, :], now[:, :, :], AX.X, ALU.max))
                    link(nc.vector.tensor_tensor(pick[:, :, :], now[:, :, :], over_experts(top[k]), ALU.is_equal))
                    link(nc.vector.tensor_tensor(pick[:, :, :], pick[:, :, :], backwards, ALU.mult))
                    link(nc.vector.tensor_reduce(row[:, :], pick[:, :, :], AX.X, ALU.max))
                    link(nc.vector.tensor_tensor(hot[k][:, :, :], backwards, over_experts(row), ALU.is_equal))
                    if k == 0:
                        link(nc.vector.scalar_tensor_tensor(out=left[:, :, :], in0=hot[0][:, :, :], scalar=-2.0,
                                                            in1=prob[:, :, :], op0=ALU.mult, op1=ALU.add))
                        now = left
                link(nc.vector.tensor_tensor(total[:, :], top[0][:, :], top[1][:, :], ALU.add))
                link(nc.vector.tensor_scalar(total[:, :], total[:, :], 1e-6, None, ALU.add))
                link(nc.vector.reciprocal(row[:, :], total[:, :]))
                for k in range(TOPK):
                    link(nc.vector.tensor_tensor(g.weights[:, k, :], top[k][:, :], row[:, :], ALU.mult))
                link(nc.vector.tensor_tensor(gate[:, :, :], hot[0][:, :, :], over_experts(g.weights[:, 0, :]), ALU.mult))
                link(nc.vector.tensor_tensor(pick[:, :, :], hot[1][:, :, :], over_experts(g.weights[:, 1, :]), ALU.mult))
                link(nc.vector.tensor_tensor(gate[:, :, :], gate[:, :, :], pick[:, :, :], ALU.add))
                link(nc.vector.scalar_tensor_tensor(out=pick[:, :, :], in0=hot[0][:, :, :], scalar=-1.0,
                                                    in1=hot[1][:, :, :], op0=ALU.add, op1=ALU.add))
                link(nc.vector.tensor_tensor(gate[:, :, :], gate[:, :, :], pick[:, :, :], ALU.add))

                def body(i, s, more):
                    n = i * 2 + s
                    for m in range(MC):
                        done = (n * MC + m) * TRIALSTEPS
                        dve.wait_ge(trial_step, PRIME + done)
                        nc.vector.tensor_tensor(trial[:, :], limit[:, :], bit[:, :], ALU.bitwise_or).then_inc(trial_step, 1)
                        dve.wait_ge(trial_step, PRIME + done + 1)
                        nc.vector.tensor_tensor(over[:, :, :], by_expert(gate), over_tiles(trial[:, :].bitcast(F32)),
                                                ALU.is_ge).then_inc(trial_step, 1)
                        dve.wait_ge(trial_step, PRIME + done + 2)
                        with nc.allow_low_precision("counts of at most NT are exact in bfloat16"):
                            nc.vector.tensor_reduce(count[:, :], over[:, :, :], AX.X, ALU.add).then_inc(trial_done, 1)
                        dve.wait_ge(hi_done, PRIME + n * MC + m + 1)
                        dve.wait_ge(lo_done, PRIME + n * MC + m - 1)
                        nc.vector.scalar_tensor_tensor(out=rest[m % 2][:, :], in0=qk[m % 2][:, :],
                                                       scalar=DH ** -0.5 if m < KC else 1.0,
                                                       in1=parts[s][:, m, 0, :], op0=ALU.mult,
                                                       op1=ALU.subtract).then_inc(rest_done, 1)
                        dve.wait_ge(count_done, PRIME + n * MC + m + 1)
                        nc.vector.scalar_tensor_tensor(out=grow[:, :], in0=counted[:, :], scalar=float(CAP), in1=bit[:, :],
                                                       op0=ALU.is_ge, op1=ALU.mult).then_inc(trial_step, 1)
                        dve.wait_ge(trial_step, PRIME + done + 3)
                        nc.vector.tensor_tensor(limit[:, :], limit[:, :], grow[:, :], ALU.bitwise_or).then_inc(trial_step, 1)
                        nc.vector.tensor_scalar(bit[:, :], bit[:, :], 1, None, ALU.logical_shift_right).then_inc(trial_step, 1)

                rows(dve, body)
                dve.wait_ge(trial_step, PRIME + TRIALS * TRIALSTEPS)
                bound = over_tiles(limit[:, :].bitcast(F32))
                link(nc.vector.tensor_tensor(above[:, :, :], by_expert(gate), bound, ALU.is_gt))
                with nc.allow_low_precision("counts of at most NT are exact in bfloat16"):
                    nc.vector.tensor_reduce(count[:, :], above[:, :, :], AX.X, ALU.add).then_inc(trial_done, 1)
                nc.vector.tensor_tensor(ties[:, :, :], by_expert(gate), bound, ALU.is_equal).then_inc(prefix_in, 1)
                dve.wait_ge(count_done, PRIME + TRIALS + 1)
                link(nc.vector.tensor_scalar(need[:, :], counted[:, :], -1.0, float(CAP), ALU.mult, ALU.add))

                def ranks(n):
                    dve.wait_ge(prefix_done, PRIME + n + 1)
                    link(nc.vector.tensor_copy(slot[:, :, :].rearrange("p e t -> p (e t)"), tiles))
                    link(nc.vector.tensor_tensor_scan(
                        start[:, :, :].rearrange("p e t -> p (e t)"), resets[:, :, :].rearrange("p e t -> p (e t)"),
                        slot[:, :, :].rearrange("p e t -> p (e t)"), 0.0, ALU.mult, ALU.add))
                    link(nc.vector.tensor_tensor(start[:, :, :], start[:, :, :], slot[:, :, :], ALU.subtract))
                    link(nc.vector.tensor_tensor(slot[:, :, :], ranked.rearrange("p (e t) -> p e t", e=E), start[:, :, :], ALU.add))

                ranks(0)
                link(nc.vector.tensor_tensor(slot[:, :, :], slot[:, :, :], over_tiles(need), ALU.is_lt))
                link(nc.vector.tensor_tensor(slot[:, :, :], slot[:, :, :], ties[:, :, :], ALU.mult))
                nc.vector.tensor_tensor(kept[:, :, :], above[:, :, :], slot[:, :, :], ALU.add).then_inc(prefix_in, 1)
                ranks(1)
                link(nc.vector.tensor_tensor(slot[:, :, :], slot[:, :, :], base[:, :, :].broadcast_to([P, E, NT]), ALU.add))
                link(nc.vector.tensor_tensor(slot[:, :, :], slot[:, :, :], kept[:, :, :], ALU.mult))
                for k in range(TOPK):
                    link(nc.vector.tensor_tensor(pick[:, :, :], hot[k][:, :, :], slot[:, :, :].rearrange("p e t -> p t e"), ALU.mult))
                    link(nc.vector.tensor_reduce(row[:, :], pick[:, :, :], AX.X, ALU.add))
                    link(nc.vector.tensor_scalar(g.slots[:, k, :], row[:, :], float(E * CAP), None, ALU.add))


STEPS = [(qc, j) for qc in range(L // BANK) for j in range((qc + 1) * TPC)]
NS = len(STEPS)
MASKED_STEPS = [s for s, (qc, j) in enumerate(STEPS) if j >= qc * TPC]
HALVES = [(3, 0), (0, 0), (7, 0), (6, 1), (4, 0), (1, 0), (5, 0), (5, 1), (7, 1), (2, 0), (6, 0), (4, 1)]
TILES = [(h, qt, half) for h in range(4) for qt, half in HALVES]
NTILE = len(TILES)
NSCORE = 3
NTURNED = 3
FIRST_TILES = 9
TURN_MAX = 9
COPY_OUT = {TPC + 1: 0, 1: 1}
TURN_OUT = {TPC + 2: 0, 2: 1}
NORMALISE = {TPC + 3: 0, 3: 1}
LOAD_NEXT = 1
TAIL = 4


def tiles_beside(s):
    ahead, n = (2, s - FIRST_TILES) if s >= FIRST_TILES else (1, s - FIRST_TILES + NS)
    return ahead, range(NTILE * n // NS, NTILE * (n + 1) // NS)


def exists(i, unit):
    return unit < 2 * QUADS if not isinstance(i, int) else 0 <= i * QUADS + unit < B * QUADS


PIECES = [(m, n) for m in range(2) for n in range(WCOLS // BANK)]
PIECE_AT = [TAIL + 1 + 2 * n for n in range(len(PIECES))]
EARLY = 12


def build_attend(nc, g, wg, wu):
    with ExitStack() as ctx:
        def sb(name, shape, dt):
            return ctx.enter_context(nc.sbuf_tensor(name, shape, dt))

        def psum(name, shape):
            return ctx.enter_context(nc.psum_tensor(name, shape, F32))

        primed = []

        def sem(name):
            primed.append(ctx.enter_context(nc.semaphore(name)))
            return primed[-1]

        qst = [sb(f"qst{q}", [STACK + MAXROWS, 4, L], BF16) for q in range(QUADS)]
        kst = [sb(f"kst{q}", [STACK + MAXROWS, 4, L], BF16) for q in range(QUADS)]
        vst = [sb(f"vst{q}", [P, QT, 4 * VW], F32) for q in range(QUADS)]
        probs = [sb(f"probs{n}", [P, 4, BANK], F32) for n in range(3)]
        rowmax = sb("rowmax", [P, 2, 4, QT], F32)
        maxrest = sb("maxrest", [P, 4, QT], F32)
        maxparts = sb("maxparts", [P, MAXROWS, 4, QT], BF16)
        maxturned = sb("maxturned", [MAXROWS * 4 * QT, P], BF16)
        outT = [sb(f"outT{n}", [P, BANK], F32) for n in range(2)]
        recip = sb("recip", [P, TPC, 4], F32)
        heads = [sb(f"heads{n}", [P, TPC, 4 * DH], F32) for n in range(2)]
        score = [psum(f"score{n}", [P, BANK]) for n in range(NSCORE)]
        scoreT = [psum(f"scoreT{n}", [P, BANK]) for n in range(NTURNED)]
        outps = psum("outps", [P, BANK])
        small = psum("small", [P, TPC, P])
        smallb = small[:, 0, :].bitcast(BF16)

        sent = ctx.enter_context(nc.semaphore("sent"))
        tally = sem("a_tally")
        expert_in = [ctx.enter_context(nc.semaphore(f"expert_in{m}")) for m in range(2)]
        expert_hi = ctx.enter_context(nc.semaphore("expert_hi"))
        expert_lo = ctx.enter_context(nc.semaphore("expert_lo"))
        ones_set = sem("ones_set")
        stack_in = [sem(f"stack_in{q}") for q in range(QUADS)]
        max_in = [sem(f"max_in{q}") for q in range(QUADS)]
        score_done = sem("score_done")
        max_done = sem("max_done")
        max_step = sem("max_step")
        max_turned = sem("max_turned")
        max_copied = sem("max_copied")
        scoreT_done = sem("scoreT_done")
        exp_done = sem("exp_done")
        mask_done = sem("mask_done")
        pv_done = sem("pv_done")
        out_copied = sem("out_copied")
        out_turned = sem("out_turned")
        heads_step = sem("heads_step")
        heads_out = [sem(f"heads_out{n}") for n in range(2)]
        LOADS = 2 * len(TERMS) + 1
        MAXSTEPS = 6

        def slots(eng, slot):
            for k in range(TAIL):
                slot(0, k)
            with eng.Fori(0, B - 1) as i:
                for k in range(TAIL, QUADS * NS + TAIL):
                    slot(i, k)
            for k in range(TAIL, QUADS * NS + TAIL):
                slot(B - 1, k)

        with nc.Block() as block:
            @block.sync
            def _(sp):
                def load(i, q):
                    for n, (a, c) in enumerate(TERMS):
                        for st, side, part in ((qst, 0, a), (kst, 1, c)):
                            sp.dma_start(st[q][n * DH:(n + 1) * DH, :, :],
                                         g.qk_parts[side, part, 4 * DH * q:4 * DH * (q + 1), bass.ds(i * L, L)].rearrange(
                                             "(h d) t -> d h t", d=DH)).then_inc(stack_in[q], 16)
                    sp.dma_start(vst[q][:, :, :], g.v_rows[bass.ds(i * QUADS + q, 1), :, :, :].rearrange(
                        "o p t c -> p (o t) c")).then_inc(stack_in[q], 16)

                def max_rows(u, q):
                    sp.wait_ge(max_copied, PRIME + u + 1)
                    for r in range(MAXROWS):
                        sp.dma_start(qst[q][STACK + r:STACK + r + 1, :, :].rearrange("o h t -> o (h t)"),
                                     maxturned[r * 4 * QT:(r + 1) * 4 * QT, :]).then_inc(max_in[q], 16)

                def slot(i, k):
                    unit, s = k // NS, k % NS
                    u = i * QUADS + unit
                    if s == LOAD_NEXT and exists(i, unit - 1) and exists(i, unit + 3):
                        sp.wait_ge(scoreT_done, PRIME + u * 4 * NS)
                        sp.wait_ge(pv_done, PRIME + u * NS)
                        load(i + (unit + 3) // QUADS, (unit + 3) % QUADS)
                    if s in NORMALISE:
                        qc = NORMALISE[s]
                        if exists(i, unit - qc):
                            done = unit - qc
                            sp.wait_ge(heads_step, PRIME + ((i * QUADS + done) * 2 + qc + 1) * 2)
                            row, q = i + done // QUADS, done % QUADS
                            sp.dma_start(g.attn_rows[bass.ds(row * L + qc * BANK, BANK), 4 * DH * q:4 * DH * (q + 1)].rearrange(
                                "(t p) c -> p t c", p=P), heads[qc][:, :, :]).then_inc(heads_out[qc], 16)
                    if s == TURN_MAX and exists(i, unit + 1):
                        max_rows(u + 1, (unit + 1) % QUADS)

                sp.wait_ge(ones_set, PRIME + 2)
                for q in range(QUADS):
                    load(0, q)
                max_rows(0, 0)
                for m, w in enumerate((wg, wu)):
                    sp.dma_start(g.raw(m).rearrange("p (c f) -> p c f", c=KC),
                                 w[0].rearrange("(c p) f -> p c f", p=P)).then_inc(expert_in[m], 16)
                slots(sp, slot)
                for qc in range(2):
                    sp.wait_ge(heads_out[qc], PRIME + 16 * B * QUADS)

            @block.gpsimd
            def _(pool):
                prime(pool, primed)
                for q in range(QUADS):
                    one = nc.gpsimd.memset(kst[q][STACK:STACK + MAXROWS, :, :], 1.0)
                one.then_inc(ones_set, 1)

                def send(n):
                    t, choice = n // TOPK, n % TOPK
                    nc.gpsimd.indirect_dma_start(
                        g.queues, bass.IndirectOffsetOnAxis(ap=g.slots[:, choice, t:t + 1], axis=0),
                        g.xn_all[:, t, :], None, bounds_check=E * CAP - 1, oob_is_err=False).then_inc(sent, 16)

                def slot(i, k):
                    unit, s = k // NS, k % NS
                    u = i * QUADS + unit
                    qc, j = STEPS[s]
                    last = isinstance(i, int) and i == B - 1
                    if last:
                        late, span = NT * TOPK - EARLY, QUADS * NS - TAIL
                        for n in range(late * (k - TAIL) // span, min(late, late * (k - TAIL + 1) // span)):
                            send(EARLY + n)
                    if s in MASKED_STEPS and exists(i, unit):
                        off = (j - qc * TPC) * P
                        pool.wait_ge(exp_done, PRIME + u * 4 * NS + 4 * (s + 1))
                        pool.sem_inc(tally, 1)
                        tile = probs[s % 3][:, :, off:off + P]
                        nc.gpsimd.affine_select(out=tile, in_=tile, compare_op=ALU.is_ge, fill=0.0, base=0,
                                                pattern=[[0, 4], [1, P]], channel_multiplier=-1).then_inc(mask_done, 1)
                    if last and k - 1 in PIECE_AT:
                        n = PIECE_AT.index(k - 1)
                        m, piece = PIECES[n]
                        cols = slice(piece * BANK, (piece + 1) * BANK)
                        pool.wait_ge(expert_hi, n + 1)
                        nc.gpsimd.tensor_tensor(g.parts(m)[1][:, cols], g.raw(m)[:, cols], g.parts(m)[0][:, cols].bitcast(F32),
                                                ALU.subtract).then_inc(expert_lo, 1)

                for n in range(EARLY):
                    send(n)
                slots(pool, slot)
                pool.wait_ge(expert_lo, len(PIECES))
                pool.wait_ge(sent, 16 * NT * TOPK)

            @block.tensor
            def _(pe):
                def row_tile(row, u, q, t):
                    h, qt, half = TILES[t]
                    if t == 0:
                        pe.wait_ge(stack_in[q], PRIME + 16 * LOADS * (row + 1))
                    pe.wait_ge(max_done, PRIME + u * NTILE + t - NSCORE + 1)
                    k0 = half * BANK
                    width = min(BANK, (qt + 1) * P - k0)
                    diagonal = k0 + width == (qt + 1) * P
                    bank = score[t % NSCORE]
                    mm = nc.tensor.matmul(bank[:, 0:width], qst[q][0:STACK, h, qt * P:(qt + 1) * P],
                                          kst[q][0:STACK, h, k0:k0 + width], start=True, stop=not diagonal)
                    if diagonal:
                        mm = nc.tensor.matmul(bank[:, width - P:width], g.identb[:, :], g.maskneg[:, :],
                                              start=False, stop=True)
                    mm.then_inc(score_done, 1)

                def turn_max(u):
                    pe.wait_ge(max_step, PRIME + (u + 1) * MAXSTEPS)
                    pe.wait_ge(heads_step, PRIME + (2 * u - 1) * 2)
                    nc.tensor.transpose(smallb[0:MAXROWS * 4 * QT, 0:P],
                                        maxparts[:, :, :, :].rearrange("p r h t -> p (r h t)"),
                                        g.identb[:, :]).then_inc(max_turned, 1)

                def turn_out(u, qc):
                    pe.wait_ge(out_copied, PRIME + 2 * u + qc + 1)
                    pe.wait_ge(heads_step, PRIME + (2 * u + qc) * 2)
                    for t in range(TPC):
                        mm = nc.tensor.transpose(small[:, t, :], outT[qc][:, t * P:(t + 1) * P], g.ident[:, :])
                    mm.then_inc(out_turned, 1)

                def values(u, q, s):
                    qc, j = STEPS[s]
                    off = max(0, (j - qc * TPC) * P)
                    pe.wait_ge(exp_done, PRIME + u * 4 * NS + 4 * (s + 1))
                    if s in MASKED_STEPS:
                        pe.wait_ge(mask_done, PRIME + u * len(MASKED_STEPS) + MASKED_STEPS.index(s) + 1)
                    if j == 0:
                        pe.wait_ge(out_copied, PRIME + 2 * u + qc)
                    for h in range(4):
                        mm = nc.tensor.matmul(outps[32 * h:32 * h + VW, off:BANK], vst[q][:, j, h * VW:(h + 1) * VW],
                                              probs[s % 3][:, h, off:BANK], start=j == 0,
                                              stop=j == (qc + 1) * TPC - 1)
                    mm.then_inc(pv_done, 1)

                def slot(i, k):
                    unit, s = k // NS, k % NS
                    u, q, row = i * QUADS + unit, unit % QUADS, i + unit // QUADS
                    qc, j = STEPS[s]
                    off = max(0, (j - qc * TPC) * P)
                    ahead, tiles = tiles_beside(s)
                    tiles = list(tiles) if exists(i, unit + ahead) else []
                    ahead += unit
                    if s == 0 and exists(i, unit):
                        pe.wait_ge(max_in[q], PRIME + 16 * MAXROWS * (row + 1))
                    for h in range(4):
                        m = 4 * s + h
                        if exists(i, unit):
                            pe.wait_ge(exp_done, PRIME + u * 4 * NS + m - NTURNED + 1)
                            nc.tensor.matmul(scoreT[m % NTURNED][:, off:BANK], kst[q][:, h, j * P:(j + 1) * P],
                                             qst[q][:, h, qc * BANK + off:(qc + 1) * BANK],
                                             start=True, stop=True).then_inc(scoreT_done, 1)
                        if tiles:
                            row_tile(i + ahead // QUADS, i * QUADS + ahead, ahead % QUADS, tiles.pop(0))
                        if h == 2 and s > 0 and exists(i, unit):
                            values(u, q, s - 1)
                        if h == 2 and s == 0 and exists(i, unit - 1):
                            values(u - 1, (unit - 1) % QUADS, NS - 1)
                    assert not tiles
                    if s in TURN_OUT and exists(i, unit - TURN_OUT[s]):
                        if s == TURN_OUT_LATE:
                            pe.wait_ge(max_copied, PRIME + u + 1 if exists(i, unit) else PRIME + u)
                        turn_out(u - TURN_OUT[s], TURN_OUT[s])
                    if s == TURN_MAX and exists(i, unit + 1):
                        turn_max(u + 1)

                TURN_OUT_LATE = 2
                pe.wait_ge(ones_set, PRIME + 2)
                for t in range(NTILE):
                    row_tile(0, 0, 0, t)
                turn_max(0)
                for s in range(FIRST_TILES, NS):
                    for t in tiles_beside(s)[1]:
                        row_tile(0, 1, 1, t)
                slots(pe, slot)

            @block.scalar
            def _(act):
                def copy_max(u):
                    act.wait_ge(max_turned, PRIME + u + 1)
                    nc.scalar.copy(maxturned[:, :], smallb[0:MAXROWS * 4 * QT, 0:P]).then_inc(max_copied, 1)

                def slot(i, k):
                    unit, s = k // NS, k % NS
                    u, row = i * QUADS + unit, i + unit // QUADS
                    qc, j = STEPS[s]
                    off = max(0, (j - qc * TPC) * P)
                    if s in COPY_OUT and exists(i, unit - COPY_OUT[s]):
                        half = COPY_OUT[s]
                        act.wait_ge(pv_done, PRIME + u * NS + (0 if half else TPC))
                        nc.scalar.copy(outT[half][:, :], outps[:, :]).then_inc(out_copied, 1)
                    if exists(i, unit):
                        act.wait_ge(pv_done, PRIME + u * NS + s - 2)
                        for h in range(4):
                            m = 4 * s + h
                            act.wait_ge(scoreT_done, PRIME + u * 4 * NS + m + 1)
                            nc.scalar.activation(probs[s % 3][:, h, off:BANK], scoreT[m % NTURNED][:, off:BANK],
                                                 ACT.Exp).then_inc(exp_done, 1)
                    if s == TURN_MAX and exists(i, unit + 1):
                        act.wait_ge(max_in[unit % QUADS], PRIME + 16 * MAXROWS * (row + 1))
                        copy_max(u + 1)
                    if isinstance(i, int) and i == B - 1 and k in PIECE_AT:
                        m, piece = PIECES[PIECE_AT.index(k)]
                        cols = slice(piece * BANK, (piece + 1) * BANK)
                        act.wait_ge(expert_in[m], 16)
                        nc.scalar.copy(g.parts(m)[0][:, cols], g.raw(m)[:, cols]).then_inc(expert_hi, 1)

                copy_max(0)
                slots(act, slot)

            @block.vector
            def _(dve):
                def row_tile(u, t):
                    h, qt, half = TILES[t]
                    dve.wait_ge(score_done, PRIME + u * NTILE + t + 1)
                    if t == 0:
                        dve.wait_ge(max_step, PRIME + u * MAXSTEPS)
                    width = min(BANK, (qt + 1) * P - half * BANK)
                    nc.vector.tensor_reduce(rowmax[:, half, h, qt:qt + 1], score[t % NSCORE][:, 0:width],
                                            AX.X, ALU.max).then_inc(max_done, 1)

                def split_max(u):
                    base = u * MAXSTEPS
                    dve.wait_ge(max_done, PRIME + (u + 1) * NTILE)
                    dve.wait_ge(max_turned, PRIME + u)
                    far = L // 2 // P
                    nc.vector.tensor_tensor(rowmax[:, 0, :, far:QT], rowmax[:, 0, :, far:QT], rowmax[:, 1, :, far:QT],
                                            ALU.max).then_inc(max_step, 1)
                    dve.wait_ge(max_step, PRIME + base + 1)
                    nc.vector.tensor_scalar(maxparts[:, 0, :, :], rowmax[:, 0, :, :], -1.0, None, ALU.mult).then_inc(max_step, 1)
                    dve.wait_ge(max_step, PRIME + base + 2)
                    nc.vector.scalar_tensor_tensor(out=maxrest[:, :, :], in0=rowmax[:, 0, :, :], scalar=-1.0,
                                                   in1=maxparts[:, 0, :, :], op0=ALU.mult,
                                                   op1=ALU.subtract).then_inc(max_step, 1)
                    dve.wait_ge(max_step, PRIME + base + 3)
                    nc.vector.tensor_copy(maxparts[:, 1, :, :], maxrest[:, :, :]).then_inc(max_step, 1)
                    dve.wait_ge(max_step, PRIME + base + 4)
                    nc.vector.tensor_tensor(maxrest[:, :, :], maxrest[:, :, :], maxparts[:, 1, :, :],
                                            ALU.subtract).then_inc(max_step, 1)
                    dve.wait_ge(max_step, PRIME + base + 5)
                    nc.vector.tensor_copy(maxparts[:, 2, :, :], maxrest[:, :, :]).then_inc(max_step, 1)

                def normalise(u, qc):
                    turned = small[:, :, :].rearrange("p t (h c) -> p (t h) c", h=4)
                    over = recip[:, :, :].rearrange("p t h -> p (t h)")
                    dve.wait_ge(out_turned, PRIME + 2 * u + qc + 1)
                    nc.vector.reciprocal(over, turned[:, :, DH]).then_inc(heads_step, 1)
                    dve.wait_ge(heads_step, PRIME + (2 * u + qc) * 2 + 1)
                    dve.wait_ge(heads_out[qc], PRIME + u * 16)
                    nc.vector.tensor_tensor(heads[qc][:, :, :].rearrange("p t (h c) -> p (t h) c", h=4),
                                            turned[:, :, 0:DH], over.unsqueeze(2).broadcast_to([P, TPC * 4, DH]),
                                            ALU.mult).then_inc(heads_step, 1)

                def slot(i, k):
                    unit, s = k // NS, k % NS
                    u = i * QUADS + unit
                    ahead, tiles = tiles_beside(s)
                    if s in NORMALISE and exists(i, unit - NORMALISE[s]):
                        normalise(u - NORMALISE[s], NORMALISE[s])
                    if exists(i, unit + ahead):
                        for t in tiles:
                            row_tile(u + ahead, t)
                    if s == FIRST_TILES - 1 and exists(i, unit + 1):
                        split_max(u + 1)

                nc.vector.memset(outps[:, :], 0.0).then_inc(ones_set, 1)
                for t in range(NTILE):
                    row_tile(0, t)
                split_max(0)
                for s in range(FIRST_TILES, NS):
                    for t in tiles_beside(s)[1]:
                        row_tile(1, t)
                slots(dve, slot)


HALF = CAP // 2
NHALF = 2
GU = FC * NHALF


HID = 768
HC = HID // P
SCALE = 1.0 / 127.0


def build_experts(nc, g, wg, wu, wd, squares, integers):
    with ExitStack() as ctx:
        def sb(name, shape, dt=F32):
            return ctx.enter_context(nc.sbuf_tensor(name, shape, dt))

        def psum(name, shape):
            return ctx.enter_context(nc.psum_tensor(name, shape, F32))

        primed = []

        def sem(name):
            primed.append(ctx.enter_context(nc.semaphore(name)))
            return primed[-1]

        raw = [g.raw(0), g.raw(1), sb("raw2", [P, WCOLS])]
        whi = [[g.parts(m)[0] for m in range(MATS)], [sb(f"whi{m}", [P, WCOLS], F32R) for m in range(MATS)]]
        wlo = [[g.parts(m)[1] for m in range(MATS)], [sb(f"wlo{m}", [P, WCOLS], F32R) for m in range(MATS)]]
        queue = sb("queue", [P, CT, D])
        qhi = sb("qhi", [P, KC, CAP], F32R)
        qlo = sb("qlo", [P, KC, CAP], F32R)
        act_out = [sb(f"act_out{n}", [P, HALF]) for n in range(2)]
        hidden = [sb(f"hidden{n}", [P, HALF]) for n in range(2)]
        hhi = sb("hhi", [P, FC, CAP], F32R)
        hlo = sb("hlo", [P, FC, CAP], F32R)
        rows = [sb(f"rows{n}", [P, D]) for n in range(2)]
        gps = [psum(f"gps{n}", [P, BANK]) for n in range(2)]
        ups = [psum(f"ups{n}", [P, BANK]) for n in range(2)]
        dps = [psum(f"dps{n}", [P, BANK]) for n in range(2)]
        tps = [psum(f"tps{n}", [P, KC, P]) for n in range(2)]

        raw_in = [sem(f"raw_in{m}") for m in range(MATS)]
        queue_in = sem("queue_in")
        whi_done = [sem(f"whi_done{m}") for m in range(MATS)]
        wlo_done = [sem(f"wlo_done{m}") for m in range(MATS)]
        queue_turned = sem("queue_turned")
        qhi_done = sem("qhi_done")
        qlo_done = sem("qlo_done")
        gate_done = sem("gate_done")
        up_done = sem("up_done")
        silu_done = sem("silu_done")
        hidden_done = sem("hidden_done")
        hhi_done = sem("hhi_done")
        hlo_done = sem("hlo_done")
        down_done = sem("down_done")
        rows_done = sem("rows_done")
        rows_out = [sem(f"rows_out{n}") for n in range(2)]
        scaled_done = sem("scaled_done")
        next_turned = sem("next_turned")
        next_hi = sem("next_hi")
        next_lo = sem("next_lo")
        weights = (wg, wu, wd)
        WHOLE = HC * D
        groups = []
        for m in range(2):
            for c in range(KC):
                for f in range(0, HC, 2):
                    groups.append((m, [(f + k) * D + c * P for k in range(2)], c * HID + f * P))
        for f in range(HC):
            groups.append((2, [k * HID + f * P for k in range(2)], f * D))

        def beside(n):
            return range(len(groups) * n // GU, len(groups) * (n + 1) // GU)

        def pairs(eng, first, body):
            first()
            with eng.Fori(0, E // 2 - 1) as i:
                for s in range(2):
                    body(i * 2 + s, s, i, True)
            for s in range(2):
                body(E - 2 + s, s, E // 2 - 1, s == 0)

        with nc.Block() as block:
            @block.sync
            def _(sp):
                def load_weights(e):
                    for m in range(MATS):
                        sp.wait_ge(wlo_done[m], PRIME + e)
                        sp.dma_start(raw[m][:, :].rearrange("p (c f) -> p c f", c=KC if m < 2 else FC),
                                     weights[m][bass.ds(e, 1), :, :].rearrange("o (c p) f -> p (o c) f", p=P)).then_inc(raw_in[m], 16)

                def load_queue(e):
                    sp.wait_ge(queue_turned, PRIME + e * CT)
                    sp.dma_start(queue[:, :, :], g.queues[bass.ds(e * CAP, CAP), :].rearrange(
                        "(t p) d -> p t d", p=P)).then_inc(queue_in, 16)

                def store(e, t, n):
                    sp.wait_ge(rows_done, PRIME + e * CT + t + 1)
                    sp.dma_start(g.answers[bass.ds(e * CAP + t * P, P), :], rows[n][:, :]).then_inc(rows_out[n], 16)

                def body(e, s, i, more):
                    if more:
                        load_queue(e + 1)
                        load_weights(e + 1)
                    else:
                        load_next()
                    for t in range(CT):
                        store(e, t, (s + t) % 2)

                def load_next():
                    for m, (whole, square) in enumerate(zip(integers, squares)):
                        sp.wait_ge(wlo_done[m], PRIME + E)
                        sp.dma_start(raw[m][:, 0:WHOLE].bitcast(I32).rearrange("p (c d) -> p c d", c=HC if m < 2 else KC),
                                     whole.rearrange("(c p) d -> p c d", p=P)).then_inc(raw_in[m], 16)
                        sp.dma_start(raw[m][:, WHOLE:WCOLS].rearrange("p (c d) -> p c d", c=KC),
                                     square.rearrange("(c p) d -> p c d", p=P)).then_inc(raw_in[m], 16)

                def first():
                    load_queue(0)
                    sp.dma_start(raw[2][:, :].rearrange("p (c f) -> p c f", c=FC),
                                 wd[0].rearrange("(c p) f -> p c f", p=P)).then_inc(raw_in[2], 16)

                pairs(sp, first, body)
                for n in range(2):
                    sp.wait_ge(rows_out[n], PRIME + 16 * E * CT // 2)

            @block.gpsimd
            def _(pool):
                prime(pool, primed)
                for m in range(2):
                    pool.sem_inc(raw_in[m], 16)
                    pool.sem_inc(whi_done[m], 1)
                    pool.sem_inc(wlo_done[m], 1)
                for m in range(MATS):
                    pool.wait_ge(raw_in[m], PRIME + 16 * (E + 2))
                    nc.gpsimd.tensor_scalar(raw[m][:, 0:WHOLE], raw[m][:, 0:WHOLE].bitcast(I32), SCALE, None,
                                            ALU.mult).then_inc(scaled_done, 1)

            @block.tensor
            def _(pe):
                def turn_next(n):
                    m, blocks, _ = groups[n]
                    pe.wait_ge(scaled_done, PRIME + m + 1)
                    pe.wait_ge(next_lo, PRIME + n - 1)
                    for k, col in enumerate(blocks):
                        mm = nc.tensor.transpose(tps[n % 2][:, k, :], raw[m][:, col:col + P], g.ident[:, :])
                    mm.then_inc(next_turned, 1)

                def turn_queue(e):
                    pe.wait_ge(queue_in, PRIME + 16 * (e + 1))
                    for t in range(CT):
                        pe.wait_ge(qlo_done, PRIME + e * CT + t - 1)
                        for c in range(KC):
                            mm = nc.tensor.transpose(tps[t % 2][:, c, :], queue[:, t, c * P:(c + 1) * P], g.ident[:, :])
                        mm.then_inc(queue_turned, 1)

                def gate_up(e, s, more):
                    for m in range(2):
                        pe.wait_ge(wlo_done[m], PRIME + e + 1)
                    pe.wait_ge(qlo_done, PRIME + (e + 1) * CT)
                    for n in range(GU):
                        f, half = n // NHALF, n % NHALF
                        cols = slice(half * HALF, (half + 1) * HALF)
                        pe.wait_ge(hidden_done, PRIME + e * GU + n - 1)
                        for m, (ps, done) in enumerate(((gps, gate_done), (ups, up_done))):
                            for c in range(KC):
                                w = slice(c * F + f * P, c * F + (f + 1) * P)
                                mm = split_product(nc, ps[n % 2][:, 0:HALF],
                                                   (whi[s][m][:, w], wlo[s][m][:, w]),
                                                   (qhi[:, c, cols], qlo[:, c, cols]), c == 0, c == KC - 1)
                            mm.then_inc(done, 1)
                        if not more:
                            for b in beside(n):
                                turn_next(b)

                def down(e, s):
                    pe.wait_ge(wlo_done[2], PRIME + e + 1)
                    pe.wait_ge(hlo_done, PRIME + (e + 1) * GU)
                    for t in range(CT):
                        pe.wait_ge(rows_done, PRIME + e * CT + t - 1)
                        for f in range(FC):
                            w, h = slice(f * D, (f + 1) * D), slice(t * P, (t + 1) * P)
                            mm = split_product(nc, dps[(s + t) % 2][:, 0:D], (hhi[:, f, h], hlo[:, f, h]),
                                               (whi[s][2][:, w], wlo[s][2][:, w]), f == 0, f == FC - 1)
                        mm.then_inc(down_done, 1)

                def body(e, s, i, more):
                    gate_up(e, s, more)
                    if more:
                        turn_queue(e + 1)
                    down(e, s)

                pairs(pe, lambda: turn_queue(0), body)

            @block.scalar
            def _(act):
                def split_weights(e, s):
                    for m in range(MATS):
                        act.wait_ge(raw_in[m], PRIME + 16 * (e + 1))
                        act.wait_ge(down_done, PRIME + (e - 1) * CT)
                        nc.scalar.copy(whi[s][m][:, :], raw[m][:, :]).then_inc(whi_done[m], 1)

                def split_queue(e):
                    for t in range(CT):
                        act.wait_ge(queue_turned, PRIME + e * CT + t + 1)
                        if t == 0:
                            act.wait_ge(up_done, PRIME + e * GU)
                        nc.scalar.copy(qhi[:, :, t * P:(t + 1) * P], tps[t % 2][:, :, :]).then_inc(qhi_done, 1)

                def body(e, s, i, more):
                    for n in range(GU):
                        f, half = n // NHALF, n % NHALF
                        cols = slice(half * HALF, (half + 1) * HALF)
                        act.wait_ge(gate_done, PRIME + e * GU + n + 1)
                        act.wait_ge(hidden_done, PRIME + e * GU + n - 1)
                        nc.scalar.activation(act_out[n % 2][:, :], gps[n % 2][:, 0:HALF], ACT.Silu).then_inc(silu_done, 1)
                        act.wait_ge(hidden_done, PRIME + e * GU + n + 1)
                        if n == 0:
                            act.wait_ge(down_done, PRIME + e * CT)
                        nc.scalar.copy(hhi[:, f, cols], hidden[n % 2][:, :]).then_inc(hhi_done, 1)
                        if not more:
                            for b in beside(n):
                                m, _, col = groups[b]
                                act.wait_ge(next_turned, PRIME + b + 1)
                                nc.scalar.copy(whi[0][m][:, col:col + D], tps[b % 2][:, :, :].rearrange(
                                    "p k c -> p (k c)")).then_inc(next_hi, 1)
                    if more:
                        split_queue(e + 1)
                        split_weights(e + 1, 1 - s)
                    else:
                        for m in range(MATS):
                            nc.scalar.copy(whi[0][m][:, WHOLE:WCOLS], raw[m][:, WHOLE:WCOLS]).then_inc(next_hi, 1)
                    for t in range(CT):
                        act.wait_ge(down_done, PRIME + e * CT + t + 1)
                        act.wait_ge(rows_out[(s + t) % 2], PRIME + 16 * ROWS_OUT(e, s, t, i))
                        nc.scalar.copy(rows[(s + t) % 2][:, :], dps[(s + t) % 2][:, 0:D]).then_inc(rows_done, 1)

                def ROWS_OUT(e, s, t, i):
                    n = (s + t) % 2
                    return i * CT + sum(1 for ss in range(s + 1) for tt in range(CT if ss < s else t) if (ss + tt) % 2 == n)

                def first():
                    split_queue(0)
                    act.wait_ge(raw_in[2], PRIME + 16)
                    nc.scalar.copy(whi[0][2][:, :], raw[2][:, :]).then_inc(whi_done[2], 1)

                pairs(act, first, body)

            @block.vector
            def _(dve):
                def split_weights(e, s):
                    for m in range(MATS):
                        dve.wait_ge(whi_done[m], PRIME + e + 1)
                        nc.vector.tensor_tensor(wlo[s][m][:, :], raw[m][:, :], whi[s][m][:, :].bitcast(F32),
                                                ALU.subtract).then_inc(wlo_done[m], 1)

                def split_queue(e):
                    for t in range(CT):
                        dve.wait_ge(qhi_done, PRIME + e * CT + t + 1)
                        nc.vector.tensor_tensor(qlo[:, :, t * P:(t + 1) * P], tps[t % 2][:, :, :],
                                                qhi[:, :, t * P:(t + 1) * P].bitcast(F32), ALU.subtract).then_inc(qlo_done, 1)

                def body(e, s, i, more):
                    for n in range(GU):
                        f, half = n // NHALF, n % NHALF
                        cols = slice(half * HALF, (half + 1) * HALF)
                        dve.wait_ge(silu_done, PRIME + e * GU + n + 1)
                        dve.wait_ge(up_done, PRIME + e * GU + n + 1)
                        dve.wait_ge(hlo_done, PRIME + e * GU + n - 1)
                        nc.vector.tensor_tensor(hidden[n % 2][:, :], act_out[n % 2][:, :], ups[n % 2][:, 0:HALF],
                                                ALU.mult).then_inc(hidden_done, 1)
                        dve.wait_ge(hidden_done, PRIME + e * GU + n + 1)
                        dve.wait_ge(hhi_done, PRIME + e * GU + n + 1)
                        nc.vector.tensor_tensor(hlo[:, f, cols], hidden[n % 2][:, :], hhi[:, f, cols].bitcast(F32),
                                                ALU.subtract).then_inc(hlo_done, 1)
                        if not more:
                            for b in beside(n):
                                m, _, col = groups[b]
                                dve.wait_ge(next_hi, PRIME + b + 1)
                                nc.vector.tensor_tensor(wlo[0][m][:, col:col + D], tps[b % 2][:, :, :].rearrange("p k c -> p (k c)"),
                                                        whi[0][m][:, col:col + D].bitcast(F32), ALU.subtract).then_inc(next_lo, 1)
                    if more:
                        split_queue(e + 1)
                        split_weights(e + 1, 1 - s)
                    else:
                        for m in range(MATS):
                            dve.wait_ge(next_hi, PRIME + len(groups) + m + 1)
                            nc.vector.tensor_tensor(wlo[0][m][:, WHOLE:WCOLS], raw[m][:, WHOLE:WCOLS],
                                                    whi[0][m][:, WHOLE:WCOLS].bitcast(F32), ALU.subtract).then_inc(next_lo, 1)

                def first():
                    split_queue(0)
                    dve.wait_ge(whi_done[2], PRIME + 1)
                    nc.vector.tensor_tensor(wlo[0][2][:, :], raw[2][:, :], whi[0][2][:, :].bitcast(F32),
                                            ALU.subtract).then_inc(wlo_done[2], 1)

                pairs(dve, first, body)


def build_finish(nc, g, x, b_in, log_A, B_vec, Dv, out):
    with ExitStack() as ctx:
        def sb(name, shape, dt=F32):
            return ctx.enter_context(nc.sbuf_tensor(name, shape, dt))

        def psum(name, shape):
            return ctx.enter_context(nc.psum_tensor(name, shape, F32))

        primed = []

        def sem(name):
            primed.append(ctx.enter_context(nc.semaphore(name)))
            return primed[-1]

        def two(name, shape, dt=F32):
            return [sb(f"{name}{s}", shape, dt) for s in range(2)]

        def matrix(m, first, chunks, cols):
            return [part[:, first:first + chunks * cols].rearrange("p (c d) -> p c d", c=chunks) for part in g.parts(m)]

        gateT, upT, downT = matrix(0, 0, KC, HID), matrix(1, 0, KC, HID), matrix(2, 0, HC, D)
        wout, win, cmat = [matrix(m, HC * D, KC, D) for m in range(3)]
        vecs = sb("vecs", [P, 3, KC])
        decay = sb("decay", [P, KC])
        dmat = sb("dmat", [P, 1, D])
        attn = two("attn", [P, TPC, D])
        x1 = two("x1", [P, TPC, D])
        answer = [two(f"answer{k}", [P, TPC, D]) for k in range(TOPK)]
        index = two("index", [P, TOPK, TPC], U32)
        share = two("share", [P, TOPK, TPC])
        gate1 = sb("gate1", [P, TPC, D])
        gate2 = sb("gate2", [P, TPC, D])
        stats = sb("fstats", [P, TPC, 6])
        mv = sb("fmv", [P, TPC, 2])
        var = sb("fvar", [P, TPC])
        power = sb("power", [P, TPC])
        rstd_power = sb("rstd_power", [P, TPC])
        rstd = sb("frstd", [P, TPC])
        newt = sb("fnewt", [P, TPC])
        xn = two("fxn", [P, TPC, D])
        side = two("side", [P, TPC, D])
        ahi, alo = sb("ahi", [P, KC, CHUNK], F32R), sb("alo", [P, KC, CHUNK], F32R)
        xhi, xlo = two("xhi", [P, KC, CHUNK], F32R), two("xlo", [P, KC, CHUNK], F32R)
        drive = sb("drive", [P, KC, CHUNK])
        state = two("state", [P, KC, CHUNK])
        shi, slo = sb("shi", [P, KC, CHUNK], F32R), sb("slo", [P, KC, CHUNK], F32R)
        act_out = two("fact_out", [P, CHUNK])
        hidden = two("fhidden", [P, CHUNK])
        hhi, hlo = sb("fhhi", [P, HC, CHUNK], F32R), sb("fhlo", [P, HC, CHUNK], F32R)
        tps = psum("ftps", [P, KC, CHUNK])
        yps = psum("yps", [P, TPC, D])
        gps = [psum(f"fgps{n}", [P, CHUNK]) for n in range(2)]
        ups = [psum(f"fups{n}", [P, CHUNK]) for n in range(2)]

        tally = sem("f_tally")
        vecs_in = sem("vecs_in")
        decay_step = sem("decay_step")
        attn_in = [sem(f"attn_in{s}") for s in range(2)]
        x_in = [sem(f"fx_in{s}") for s in range(2)]
        index_set = sem("index_set")
        index_tally = sem("index_tally")
        answers_in = [ctx.enter_context(nc.semaphore(f"answers_in{s}")) for s in range(2)]
        share_set = sem("share_set")
        mix_step = sem("mix_step")
        gate1_done = sem("gate1_done")
        attn_turned = sem("attn_turned")
        ahi_done = sem("ahi_done")
        alo_done = sem("alo_done")
        proj_done = sem("proj_done")
        x1_step = sem("x1_step")
        ln_step = sem("ln_step")
        power_set = sem("power_set")
        power_done = sem("power_done")
        xn_done = sem("fxn_done")
        xn_turned = sem("xn_turned")
        xhi_done = sem("xhi_done")
        xlo_done = sem("xlo_done")
        side_done = sem("side_done")
        drive_in = sem("drive_in")
        drive_done = sem("drive_done")
        state_done = sem("state_done")
        shi_done = sem("shi_done")
        slo_done = sem("slo_done")
        recur_done = sem("recur_done")
        recur_kept = sem("recur_kept")
        gate_done = sem("fgate_done")
        up_done = sem("fup_done")
        silu_done = sem("fsilu_done")
        hidden_done = sem("fhidden_done")
        hhi_done = sem("fhhi_done")
        hlo_done = sem("fhlo_done")
        ffn_done = sem("ffn_done")
        gate2_done = sem("gate2_done")
        out_step = sem("out_step")
        out_stored = [sem(f"out_stored{s}") for s in range(2)]
        LN = 7

        def steps(eng, first, body):
            first()
            with eng.Fori(0, B - 1) as i:
                for s in range(2):
                    body(i * 2 + s, s, i, True)
            for s in range(2):
                body((B - 1) * 2 + s, s, B - 1, s == 0)

        def turn(s, i):
            return i if s == 0 else i + 1

        def last_row(i):
            return isinstance(i, int) and i == B - 1

        with nc.Block() as block:
            @block.sync
            def _(sp):
                def rows_of(n):
                    return bass.ds(n * CHUNK, CHUNK)

                def load_attn(n, s):
                    sp.wait_ge(x1_step, PRIME + (n - 1) * 2)
                    sp.dma_start(attn[s][:, :, :], g.attn_rows[rows_of(n), :].rearrange("(t p) d -> p t d", p=P)).then_inc(attn_in[s], 16)

                def load_x(n, s):
                    sp.wait_ge(out_step, PRIME + (n - 1) * 2)
                    sp.dma_start(x1[s][:, :, :], x[rows_of(n), :].rearrange("(t p) d -> p t d", p=P)).then_inc(x_in[s], 16)

                def body(n, s, i, more):
                    if not last_row(i):
                        load_attn(n + 2, s)
                        load_x(n + 2, s)
                    sp.wait_ge(out_step, PRIME + (n + 1) * 2)
                    sp.dma_start(out[rows_of(n), :].rearrange("(t p) d -> p t d", p=P), side[s][:, :, :]).then_inc(out_stored[s], 16)

                def first():
                    load_attn(0, 0)
                    load_x(0, 0)
                    for n, v in enumerate((b_in, B_vec, log_A)):
                        sp.dma_start(vecs[:, n, :], v.rearrange("(c p) -> p c", p=P),
                                     allow_slow_non_contiguous=True).then_inc(vecs_in, 16)
                    sp.dma_start(dmat[:, 0, :], Dv.unsqueeze(0).broadcast_to([P, D])).then_inc(vecs_in, 16)
                    load_attn(1, 1)
                    load_x(1, 1)

                steps(sp, first, body)
                for s in range(2):
                    sp.wait_ge(out_stored[s], PRIME + 16 * B)

            @block.gpsimd
            def _(pool):
                prime(pool, primed)

                def gather(n, s, i):
                    pool.wait_ge(gate1_done, PRIME + n - 1)
                    if not (isinstance(i, int) and i == 0):
                        pool.wait_ge(answers_in[s], 16 * TOPK * TPC * i)
                    nc.gpsimd.tensor_copy(index[s][:, :, :], g.slots[:, :, bass.ds(n * TPC, TPC)]).then_inc(index_set, 1)
                    pool.wait_ge(index_set, PRIME + n + 1)
                    pool.sem_inc(index_tally, 1)
                    for k in range(TOPK):
                        for t in range(TPC):
                            nc.gpsimd.indirect_dma_start(
                                answer[k][s][:, t, :], None, g.answers,
                                bass.IndirectOffsetOnAxis(ap=index[s][:, k, t:t + 1], axis=0)).then_inc(answers_in[s], 16)

                def front(n, s, i):
                    pool.wait_ge(ln_step, PRIME + n * LN + 3)
                    nc.gpsimd.tensor_tensor(power[:, :], var[:, :], rstd_power[:, :], ALU.pow).then_inc(power_done, 1)
                    pool.wait_ge(xn_done, PRIME + (n + 1) * TPC)
                    pool.wait_ge(out_stored[s], PRIME + 16 * i)
                    nc.gpsimd.tensor_tensor(side[s][:, :, :], xn[s][:, :, :], dmat[:, :, :].broadcast_to([P, TPC, D]),
                                            ALU.mult).then_inc(side_done, 1)

                def body(n, s, i, more):
                    if not last_row(i):
                        gather(n + 2, s, i + 1)
                    if more:
                        front(n + 1, 1 - s, turn(s, i))

                def first():
                    gather(0, 0, 0)
                    nc.gpsimd.memset(rstd_power[:, :], -0.5).then_inc(power_set, 1)
                    pool.wait_ge(power_set, PRIME + 1)
                    pool.wait_ge(vecs_in, PRIME + 64)
                    front(0, 0, 0)
                    gather(1, 1, 0)

                steps(pool, first, body)

            @block.tensor
            def _(pe):
                def turn_attn(n, s, i):
                    pe.wait_ge(attn_in[s], PRIME + 16 * (i + 1))
                    pe.wait_ge(drive_done, PRIME + n * KC)
                    for t in range(TPC):
                        for c in range(KC):
                            mm = nc.tensor.transpose(tps[:, c, t * P:(t + 1) * P], attn[s][:, t, c * P:(c + 1) * P], g.ident[:, :])
                    mm.then_inc(attn_turned, 1)

                def rows_product(hi, lo, w, chunks):
                    for t in range(TPC):
                        for c in range(chunks):
                            cols = slice(t * P, (t + 1) * P)
                            mm = split_product(nc, yps[:, t, :], (hi[:, c, cols], lo[:, c, cols]),
                                               (w[0][:, c, :], w[1][:, c, :]), c == 0, c == chunks - 1)
                    return mm

                def project(n):
                    pe.wait_ge(alo_done, PRIME + n + 1)
                    pe.wait_ge(gate2_done, PRIME + n - 1)
                    rows_product(ahi, alo, wout, KC).then_inc(proj_done, 1)

                def turn_xn(n, s):
                    pe.wait_ge(xn_done, PRIME + (n + 1) * TPC)
                    pe.wait_ge(alo_done, PRIME + n + 1)
                    for t in range(TPC):
                        for c in range(KC):
                            mm = nc.tensor.transpose(tps[:, c, t * P:(t + 1) * P], xn[s][:, t, c * P:(c + 1) * P], g.ident[:, :])
                    mm.then_inc(xn_turned, 1)

                def recurrence_input(n, s):
                    pe.wait_ge(xlo_done, PRIME + n + 1)
                    for e in range(KC):
                        for c in range(KC):
                            mm = split_product(nc, tps[:, e, :], (win[0][:, c, e * P:(e + 1) * P], win[1][:, c, e * P:(e + 1) * P]),
                                               (xhi[s][:, c, :], xlo[s][:, c, :]), c == 0, c == KC - 1)
                    mm.then_inc(drive_in, 1)

                def recurrence_output(n, more):
                    pe.wait_ge(slo_done, PRIME + n + 1)
                    if more:
                        pe.wait_ge(x1_step, PRIME + 2 * n + 3)
                    else:
                        pe.wait_ge(gate2_done, PRIME + n)
                    rows_product(shi, slo, cmat, KC).then_inc(recur_done, 1)

                def gate_up(n, s, f):
                    pe.wait_ge(hidden_done, PRIME + n * HC + f - 1)
                    for ps, w, done in ((gps, gateT, gate_done), (ups, upT, up_done)):
                        for c in range(KC):
                            cols = slice(f * P, (f + 1) * P)
                            mm = split_product(nc, ps[f % 2][:, :], (w[0][:, c, cols], w[1][:, c, cols]),
                                               (xhi[s][:, c, :], xlo[s][:, c, :]), c == 0, c == KC - 1)
                        mm.then_inc(done, 1)

                def down(n):
                    pe.wait_ge(hlo_done, PRIME + (n + 1) * HC)
                    pe.wait_ge(recur_kept, PRIME + n + 1)
                    rows_product(hhi, hlo, downT, HC).then_inc(ffn_done, 1)

                def body(n, s, i, more):
                    if more:
                        turn_attn(n + 1, 1 - s, turn(s, i))
                    gate_up(n, s, 0)
                    gate_up(n, s, 1)
                    if more:
                        project(n + 1)
                    gate_up(n, s, 2)
                    recurrence_output(n, more)
                    gate_up(n, s, 3)
                    gate_up(n, s, 4)
                    if more:
                        turn_xn(n + 1, 1 - s)
                    gate_up(n, s, 5)
                    if more:
                        recurrence_input(n + 1, 1 - s)
                    down(n)

                def first():
                    turn_attn(0, 0, 0)
                    project(0)
                    turn_xn(0, 0)
                    recurrence_input(0, 0)

                steps(pe, first, body)

            @block.scalar
            def _(act):
                def gate_first(n, s):
                    act.wait_ge(mix_step, PRIME + (n + 1) * 2 * TPC)
                    act.wait_ge(x1_step, PRIME + n * 2)
                    nc.scalar.activation(gate1[:, :, :], answer[0][s][:, :, :], ACT.Silu).then_inc(gate1_done, 1)

                def attn_hi(n):
                    act.wait_ge(attn_turned, PRIME + n + 1)
                    act.wait_ge(proj_done, PRIME + n)
                    nc.scalar.copy(ahi[:, :, :], tps[:, :, :]).then_inc(ahi_done, 1)

                def xn_hi(n, s):
                    act.wait_ge(xn_turned, PRIME + n + 1)
                    act.wait_ge(up_done, PRIME + (n - 1) * HC)
                    nc.scalar.copy(xhi[s][:, :, :], tps[:, :, :]).then_inc(xhi_done, 1)

                def state_hi(n, s):
                    act.wait_ge(state_done, PRIME + (n + 1) * KC)
                    act.wait_ge(recur_done, PRIME + n)
                    nc.scalar.copy(shi[:, :, :], state[s][:, :, :]).then_inc(shi_done, 1)

                def silu(n, f):
                    act.wait_ge(gate_done, PRIME + n * HC + f + 1)
                    act.wait_ge(hidden_done, PRIME + n * HC + f - 1)
                    nc.scalar.activation(act_out[f % 2][:, :], gps[f % 2][:, :], ACT.Silu).then_inc(silu_done, 1)
                    act.wait_ge(hidden_done, PRIME + n * HC + f + 1)
                    if f == 0:
                        act.wait_ge(ffn_done, PRIME + n)
                    nc.scalar.copy(hhi[:, f, :], hidden[f % 2][:, :]).then_inc(hhi_done, 1)

                def gate_second(n):
                    act.wait_ge(ffn_done, PRIME + n + 1)
                    act.wait_ge(out_step, PRIME + n * 2)
                    nc.scalar.activation(gate2[:, :, :], yps[:, :, :], ACT.Silu).then_inc(gate2_done, 1)

                def body(n, s, i, more):
                    if more:
                        attn_hi(n + 1)
                    silu(n, 0)
                    if more:
                        gate_first(n + 1, 1 - s)
                    for f in range(1, HC - 1):
                        silu(n, f)
                    if more:
                        xn_hi(n + 1, 1 - s)
                    silu(n, HC - 1)
                    if more:
                        state_hi(n + 1, 1 - s)
                    gate_second(n)

                def first():
                    act.wait_ge(vecs_in, PRIME + 64)
                    nc.scalar.activation(decay[:, :], vecs[:, 2, :], ACT.Exp).then_inc(decay_step, 1)
                    attn_hi(0)
                    gate_first(0, 0)
                    xn_hi(0, 0)
                    state_hi(0, 0)

                steps(act, first, body)

            @block.vector
            def _(dve):
                def mix(n, s, i):
                    nc.vector.tensor_copy(share[s][:, :, :], g.weights[:, :, bass.ds(n * TPC, TPC)]).then_inc(share_set, 1)
                    dve.wait_ge(share_set, PRIME + n + 1)
                    dve.wait_ge(answers_in[s], 16 * TOPK * TPC * (i + 1))
                    for t in range(TPC):
                        nc.vector.tensor_scalar(answer[0][s][:, t, :], answer[0][s][:, t, :], share[s][:, 0, t:t + 1], None,
                                                ALU.mult).then_inc(mix_step, 1)
                    for t in range(TPC):
                        dve.wait_ge(mix_step, PRIME + n * 2 * TPC + TPC + t)
                        nc.vector.scalar_tensor_tensor(out=answer[0][s][:, t, :], in0=answer[1][s][:, t, :],
                                                       scalar=share[s][:, 1, t:t + 1], in1=answer[0][s][:, t, :],
                                                       op0=ALU.mult, op1=ALU.add).then_inc(mix_step, 1)

                def attn_lo(n):
                    dve.wait_ge(ahi_done, PRIME + n + 1)
                    nc.vector.tensor_tensor(alo[:, :, :], tps[:, :, :], ahi[:, :, :].bitcast(F32), ALU.subtract).then_inc(alo_done, 1)

                def add_first(n, s, i):
                    dve.wait_ge(proj_done, PRIME + n + 1)
                    dve.wait_ge(gate1_done, PRIME + n + 1)
                    dve.wait_ge(x_in[s], PRIME + 16 * (i + 1))
                    nc.vector.tensor_tensor(attn[s][:, :, :], yps[:, :, :], gate1[:, :, :], ALU.mult).then_inc(x1_step, 1)
                    dve.wait_ge(x1_step, PRIME + 2 * n + 1)
                    nc.vector.tensor_tensor(x1[s][:, :, :], x1[s][:, :, :], attn[s][:, :, :], ALU.add).then_inc(x1_step, 1)

                def layernorm(n, s):
                    base = n * LN
                    dve.wait_ge(x1_step, PRIME + 2 * n + 2)
                    for t in range(TPC):
                        last = nc.vector.bn_stats(stats[:, t, :], x1[s][:, t, :])
                    last.then_inc(ln_step, 1)
                    dve.wait_ge(ln_step, PRIME + base + 1)
                    dve.sem_inc(tally, 1)
                    for t in range(TPC):
                        last = nc.vector.bn_aggr(mv[:, t, :], stats[:, t, :])
                    last.then_inc(ln_step, 1)
                    dve.wait_ge(ln_step, PRIME + base + 2)
                    nc.vector.tensor_scalar(var[:, :], mv[:, :, 1], EPS, None, ALU.add).then_inc(ln_step, 1)
                    dve.wait_ge(power_done, PRIME + n + 1)
                    nc.vector.tensor_tensor(newt[:, :], power[:, :], power[:, :], ALU.mult).then_inc(ln_step, 1)
                    dve.wait_ge(ln_step, PRIME + base + 4)
                    nc.vector.tensor_tensor(newt[:, :], newt[:, :], var[:, :], ALU.mult).then_inc(ln_step, 1)
                    dve.wait_ge(ln_step, PRIME + base + 5)
                    nc.vector.tensor_scalar(newt[:, :], newt[:, :], -0.5, 1.5, ALU.mult, ALU.add).then_inc(ln_step, 1)
                    dve.wait_ge(ln_step, PRIME + base + 6)
                    nc.vector.tensor_tensor(rstd[:, :], power[:, :], newt[:, :], ALU.mult).then_inc(ln_step, 1)
                    dve.wait_ge(ln_step, PRIME + base + 7)
                    dve.wait_ge(xn_turned, PRIME + n - 1)
                    dve.wait_ge(side_done, PRIME + n - 1)
                    for t in range(TPC):
                        nc.vector.tensor_scalar(xn[s][:, t, :], x1[s][:, t, :], mv[:, t, 0:1], rstd[:, t:t + 1],
                                                ALU.subtract, ALU.mult).then_inc(xn_done, 1)

                def xn_lo(n, s):
                    dve.wait_ge(xhi_done, PRIME + n + 1)
                    nc.vector.tensor_tensor(xlo[s][:, :, :], tps[:, :, :], xhi[s][:, :, :].bitcast(F32), ALU.subtract).then_inc(xlo_done, 1)

                def recur(n, s):
                    dve.wait_ge(drive_in, PRIME + n + 1)
                    for e in range(KC):
                        nc.vector.tensor_scalar(drive[:, e, :], tps[:, e, :], vecs[:, 0, e:e + 1], vecs[:, 1, e:e + 1],
                                                ALU.add, ALU.mult).then_inc(drive_done, 1)
                    for e in range(KC):
                        dve.wait_ge(drive_done, PRIME + n * KC + e + 1)
                        nc.vector.tensor_tensor_scan(state[s][:, e, :], decay[:, e:e + 1].broadcast_to([P, CHUNK]), drive[:, e, :],
                                                     0.0 if s == 0 else state[0][:, e, CHUNK - 1:CHUNK],
                                                     ALU.mult, ALU.add).then_inc(state_done, 1)
                    dve.wait_ge(shi_done, PRIME + n + 1)
                    nc.vector.tensor_tensor(slo[:, :, :], state[s][:, :, :], shi[:, :, :].bitcast(F32), ALU.subtract).then_inc(slo_done, 1)

                def keep_recurrence(n, s):
                    dve.wait_ge(recur_done, PRIME + n + 1)
                    dve.wait_ge(side_done, PRIME + n + 1)
                    nc.vector.tensor_tensor(side[s][:, :, :], yps[:, :, :], side[s][:, :, :], ALU.add).then_inc(recur_kept, 1)

                def multiply(n, f):
                    dve.wait_ge(silu_done, PRIME + n * HC + f + 1)
                    dve.wait_ge(up_done, PRIME + n * HC + f + 1)
                    dve.wait_ge(hlo_done, PRIME + n * HC + f - 1)
                    nc.vector.tensor_tensor(hidden[f % 2][:, :], act_out[f % 2][:, :], ups[f % 2][:, :], ALU.mult).then_inc(hidden_done, 1)
                    dve.wait_ge(hidden_done, PRIME + n * HC + f + 1)
                    dve.wait_ge(hhi_done, PRIME + n * HC + f + 1)
                    nc.vector.tensor_tensor(hlo[:, f, :], hidden[f % 2][:, :], hhi[:, f, :].bitcast(F32), ALU.subtract).then_inc(hlo_done, 1)

                def add_second(n, s):
                    dve.wait_ge(gate2_done, PRIME + n + 1)
                    dve.wait_ge(recur_kept, PRIME + n + 1)
                    nc.vector.tensor_tensor(side[s][:, :, :], side[s][:, :, :], gate2[:, :, :], ALU.mult).then_inc(out_step, 1)
                    dve.wait_ge(out_step, PRIME + 2 * n + 1)
                    nc.vector.tensor_tensor(side[s][:, :, :], side[s][:, :, :], x1[s][:, :, :], ALU.add).then_inc(out_step, 1)

                def body(n, s, i, more):
                    if more:
                        attn_lo(n + 1)
                    multiply(n, 0)
                    multiply(n, 1)
                    if more:
                        add_first(n + 1, 1 - s, turn(s, i))
                    multiply(n, 2)
                    if more:
                        layernorm(n + 1, 1 - s)
                    multiply(n, 3)
                    multiply(n, 4)
                    if more:
                        xn_lo(n + 1, 1 - s)
                    keep_recurrence(n, s)
                    multiply(n, 5)
                    if more:
                        recur(n + 1, 1 - s)
                    if not last_row(i):
                        mix(n + 2, s, i + 1)
                    add_second(n, s)

                def first():
                    dve.wait_ge(decay_step, PRIME + 1)
                    nc.vector.tensor_scalar(decay[:, :], decay[:, :], -1.0, None, ALU.mult).then_inc(decay_step, 1)
                    dve.wait_ge(decay_step, PRIME + 2)
                    attn_lo(0)
                    mix(0, 0, 0)
                    add_first(0, 0, 0)
                    layernorm(0, 0)
                    xn_lo(0, 0)
                    recur(0, 0)
                    mix(1, 1, 0)

                steps(dve, first, body)


def build(nc, ins, out):
    g = Shared()
    (x, Wq, Wk, Wv, Wout, router_w, wg, wu, wd, W_in, b_in, log_A, B_vec, C, Dv, w_gate, w_up, w_down) = ins
    x = x.rearrange("b l d -> (b l) d")
    out = out.rearrange("b l d -> (b l) d")
    g.qk_parts = nc.dram_tensor("qk_parts", [2, PARTS, H * DH, N], BF16, kind="Internal").ap()
    g.v_rows = nc.dram_tensor("v_rows", [B * QUADS, P, QT, 4 * VW], F32, kind="Internal").ap()
    g.queues = nc.dram_tensor("queues", [E * CAP, D], F32, kind="Internal").ap()
    g.answers = nc.dram_tensor("answers", [E * CAP + P, D], F32, kind="Internal").ap()
    g.attn_rows = nc.dram_tensor("attn_rows", [N, D], F32, kind="Internal").ap()
    with ExitStack() as ctx:
        g.weights = ctx.enter_context(nc.sbuf_tensor("weights", [P, TOPK, NT], F32))
        g.slots = ctx.enter_context(nc.sbuf_tensor("slots", [P, TOPK, NT], U32))
        build_constants(nc, ctx, g)
        g.fresh = ctx.enter_context(nc.sbuf_tensor("fresh", [P, 2, WCOLS], F32))
        g.split = ctx.enter_context(nc.sbuf_tensor("split", [P, 2 * MATS, WCOLS], F32R))
        with nc.sbuf_tensor("xn_all", [P, NT, D], F32) as g.xn_all:
            build_project(nc, g, x, Wq, Wk, Wv, router_w)
            build_attend(nc, g, wg, wu)
        build_experts(nc, g, wg, wu, wd, (Wout.rearrange("h e d -> (h e) d"), W_in, C), (w_gate, w_up, w_down))
        build_finish(nc, g, x, b_in, log_A, B_vec, Dv, out)
    return g


_INS = ["L0_attn_x", "L0_attn_Wq", "L0_attn_Wk", "L0_attn_Wv", "L0_attn_Wout", "L0_ffn_router_w", "L0_ffn_wg",
        "L0_ffn_wu", "L0_ffn_wd", "L1_attn_W_in", "L1_attn_b_in", "L1_attn_log_A", "L1_attn_B_vec", "L1_attn_C",
        "L1_attn_D", "L1_ffn_w_gate", "L1_ffn_w_up", "L1_ffn_w_down"]


def kernel(**inputs):
    import numpy as _np
    import concourse.bacc as _bacc
    from concourse import mybir as _mybir
    from concourse.bass_utils import run_bass_kernel_spmd as _run

    nc = _bacc.Bacc("TRN2", target_bir_lowering=False, num_devices=1)
    arrays, args = {}, []
    for name in _INS:
        a = _np.ascontiguousarray(inputs[name])
        arrays[f"in_{name}"] = a
        args.append(nc.dram_tensor(f"in_{name}", a.shape, _mybir.dt.from_np(a.dtype), kind="ExternalInput").ap())
    out = nc.dram_tensor("out", (B, L, D), F32, kind="ExternalOutput").ap()
    build(nc, args, out)
    r = _run(nc, [arrays], core_ids=[0])
    return r.results[0]["out"]
```

```python
from contextlib import ExitStack

import concourse.bass as bass
from concourse import mybir

F32 = mybir.dt.float32
F32R = mybir.dt.float32r
BF16 = mybir.dt.bfloat16
I32 = mybir.dt.int32
U32 = mybir.dt.uint32
ALU = mybir.AluOpType
ACT = mybir.ActivationFunctionType
AX = mybir.AxisListType

P = 128
BANK = 512
B, L, D = 4, 1024, 256
H, DH = 16, 16
N = B * L
NT = N // P
KC = D // P
CHUNK = 512
TPC = CHUNK // P
QUADS = H // 4
QT = L // P
PARTS = 3
VW = DH + 1
E, F = 8, 1024
FC = F // P
TOPK = 2
CAP = int(1.25 * N / E)
CT = CAP // P
EPS = 1e-5
MASKED = -1e38
TERMS = [(0, 0), (0, 1), (1, 0), (1, 1), (0, 2), (2, 0)]
WCOLS = KC * F
MATS = 3
STACK = len(TERMS) * DH
MAXROWS = PARTS


PRIME = 16


def prime(engine, semaphores):
    for s in semaphores:
        engine.sem_inc(s, PRIME)


class Shared:

    def raw(g, m):
        return g.fresh[:, m, :]

    def parts(g, m):
        return g.split[:, m, :], g.split[:, MATS + m, :]


def build_constants(nc, ctx, g):
    def sb(name, shape, dt):
        return ctx.enter_context(nc.sbuf_tensor(name, shape, dt))

    g.ident = sb("ident", [P, P], F32)
    g.identb = sb("identb", [P, P], BF16)
    g.maskneg = sb("maskneg", [P, P], BF16)
    filled = ctx.enter_context(nc.semaphore("filled"))
    cut = ctx.enter_context(nc.semaphore("cut"))
    with nc.Block() as block:
        @block.gpsimd
        def _(pool):
            nc.gpsimd.memset(g.ident[:, :], 0.0).then_inc(filled, 1)
            nc.gpsimd.memset(g.identb[:, :], 0.0).then_inc(filled, 1)
            nc.gpsimd.memset(g.maskneg[:, :], 0.0).then_inc(filled, 1)
            pool.wait_ge(filled, 3)
            for t in (g.ident, g.identb):
                nc.gpsimd.affine_select(out=t[:, :], in_=t[:, :], compare_op=ALU.not_equal, fill=1.0,
                                        base=0, pattern=[[-1, P]], channel_multiplier=1).then_inc(cut, 1)
            nc.gpsimd.affine_select(out=g.maskneg[:, :], in_=g.maskneg[:, :], compare_op=ALU.is_ge,
                                    fill=MASKED, base=0, pattern=[[-1, P]],
                                    channel_multiplier=1).then_inc(cut, 1)
            pool.wait_ge(cut, 3)


BITS = 30


def split_product(nc, out, left, right, first, last):
    nc.tensor.matmul(out, left[0], right[0], start=first, stop=False)
    nc.tensor.matmul(out, left[1], right[0], start=False, stop=False)
    return nc.tensor.matmul(out, left[0], right[1], start=False, stop=last)


def build_project(nc, g, x, Wq, Wk, Wv, router_w):
    MC = 2 * KC
    with ExitStack() as ctx:
        def sb(name, shape, dt=F32):
            return ctx.enter_context(nc.sbuf_tensor(name, shape, dt))

        def psum(name, shape):
            return ctx.enter_context(nc.psum_tensor(name, shape, F32))

        primed = []

        def sem(name):
            primed.append(ctx.enter_context(nc.semaphore(name)))
            return primed[-1]

        def two(name, shape, dt=F32):
            return [sb(f"{name}{s}", shape, dt) for s in range(2)]

        wqkv = sb("wqkv", [P, 3, KC, D])
        whi, wlo = [g.split[:, n, 0:3 * KC * D].rearrange("p (m c d) -> p m c d", m=3, c=KC) for n in range(2)]
        rw = sb("rw", [E, D])
        rwT = sb("rwT", [P, KC, E])
        eps = sb("eps", [P, 1])
        zeros = sb("zeros", [P, 4 * D])
        stats = two("stats", [P, TPC, 6])
        mv = two("mv", [P, TPC, 2])
        std = two("std", [P, TPC])
        rstd = two("rstd", [P, TPC])
        newt = two("newt", [P, TPC])
        xn = [g.fresh[:, 1, s * TPC * D:(s + 1) * TPC * D].rearrange("p (t d) -> p t d", t=TPC) for s in range(2)]
        xnT = two("xnT", [P, KC, CHUNK])
        turned_all = sb("turned_all", [P, KC, N])
        xhi, xlo = [[g.split[:, n, s * KC * CHUNK:(s + 1) * KC * CHUNK].rearrange("p (c t) -> p c t", c=KC)
                     for s in range(2)] for n in (2, 3)]
        rest = two("rest", [P, CHUNK])
        parts = two("parts", [P, MC, PARTS, CHUNK], BF16)
        vrow = two("vrow", [P, TPC, H, VW])
        logits = sb("logits", [P, NT, E])
        prob = sb("prob", [P, NT, E])
        left = sb("left", [P, NT, E])
        pick = sb("pick", [P, NT, E])
        hot = two("hot", [P, NT, E])
        gate = sb("gate", [P, NT, E])
        back = sb("back", [P, 1, E])
        row = sb("row", [P, NT])
        top = two("top", [P, NT])
        total = sb("total", [P, NT])
        limit = sb("limit", [P, E], I32)
        trial = sb("trial", [P, E], I32)
        bit = sb("bit", [P, E], I32)
        grow = sb("grow", [P, E], I32)
        over = sb("over", [P, E, NT], BF16)
        count = sb("count", [P, E], BF16)
        above = sb("above", [P, E, NT])
        ties = sb("ties", [P, E, NT], BF16)
        need = sb("need", [P, E])
        kept = sb("kept", [P, E, NT], BF16)
        start = sb("start", [P, E, NT])
        resets = sb("resets", [P, E, NT])
        slot = sb("slot", [P, E, NT])
        base = sb("base", [P, E, 1])
        ones = sb("ones", [P, P], BF16)
        before = sb("before", [P, P], BF16)
        qk = [psum(f"qk{m}", [P, CHUNK]) for m in range(2)]
        vps = psum("vps", [P, TPC, D])
        turned = [psum("turned", [P, KC, CHUNK]), vps[:, :, :].rearrange("p (c a) d -> p c (a d)", c=KC)]
        lps = psum("lps", [P, NT, E])
        counted = psum("counted", [P, E])
        ranked, tiles = qk[0][:, 0:E * NT], qk[1][:, 0:E * NT]

        router_in = sem("router_in")
        weights_in = sem("weights_in")
        x_in = [sem(f"x_in{s}") for s in range(2)]
        tally = sem("p_tally")
        stats_done = sem("stats_done")
        var_done = sem("var_done")
        std_done = sem("std_done")
        rstd_step = sem("rstd_step")
        xn_done = sem("xn_done")
        xn_kept = sem("xn_kept")
        turned_done = sem("turned_done")
        xnT_done = sem("xnT_done")
        turned_kept = sem("turned_kept")
        logits_done = sem("logits_done")
        logits_kept = sem("logits_kept")
        whi_done = sem("pwhi_done")
        wlo_done = sem("pwlo_done")
        xhi_done = sem("pxhi_done")
        xlo_done = sem("pxlo_done")
        qk_done = sem("qk_done")
        hi_done = sem("hi_done")
        rest_done = sem("rest_done")
        mid_done = sem("mid_done")
        lo_done = sem("lo_done")
        v_done = sem("v_done")
        v_kept = sem("v_kept")
        stored = [sem(f"stored{s}") for s in range(2)]
        filled = sem("p_filled")
        cut = sem("p_cut")
        rw_turned = sem("rw_turned")
        rw_done = sem("rw_done")
        zeroed = sem("zeroed")
        zeros_out = sem("zeros_out")
        shifted = sem("shifted")
        exp_done = sem("r_exp_done")
        step = sem("r_step")
        trial_done = sem("trial_done")
        trial_step = sem("trial_step")
        count_done = sem("count_done")
        prefix_in = sem("prefix_in")
        prefix_done = sem("prefix_done")
        NEWTON = 4
        VALUES = [[0, 1], [2], [3], []]
        FILLS = 3 + 4 + 2 * E
        TRIALSTEPS = 5
        TRIALS = 2 * B * MC
        assert TRIALS >= BITS

        def chunk(i, s):
            return bass.ds(i * L + s * CHUNK, CHUNK)

        def tiles_of(i, s):
            return bass.ds(i * QT + s * TPC, TPC)

        def rows(eng, body):
            with eng.Fori(0, B - 1) as i:
                for s in range(2):
                    body(i, s, True)
            for s in range(2):
                body(B - 1, s, s == 0)

        with nc.Block() as block:
            @block.sync
            def _(sp):
                def load(i, s):
                    sp.dma_start(g.xn_all[:, tiles_of(i, s), :], x[chunk(i, s), :].rearrange("(t p) d -> p t d", p=P)).then_inc(x_in[s], 16)

                load(0, 0)
                load(0, 1)
                sp.dma_start(rw[:, :], router_w).then_inc(router_in, 16)
                for n, w in enumerate((Wq, Wk, Wv)):
                    sp.dma_start(wqkv[:, n, :, :], w.rearrange("(c p) h e -> p c (h e)", p=P)).then_inc(weights_in, 16)
                with sp.Fori(0, B - 1) as i:
                    for s in range(2):
                        sp.wait_ge(x_in[s], PRIME + 16 * (i + 1))
                        load(i + 1, s)
                sp.wait_ge(zeroed, PRIME + 1)
                for r in range(0, E * CAP, 4 * P):
                    sp.dma_start(g.queues[r:r + 4 * P, :].rearrange("(p c) d -> p (c d)", c=4), zeros[:, :]).then_inc(zeros_out, 16)
                sp.dma_start(g.answers[E * CAP:E * CAP + P, :], zeros[:, 0:D]).then_inc(zeros_out, 16)
                with sp.Fori(0, B) as i:
                    for s in range(2):
                        n = i * 2 + s
                        for m in range(MC):
                            sp.wait_ge(lo_done, PRIME + n * MC + m + 1)
                            sp.dma_start(g.qk_parts[m // KC, :, (m % KC) * P:(m % KC + 1) * P, chunk(i, s)].rearrange(
                                "r p t -> p r t"), parts[s][:, m, :, :]).then_inc(stored[s], 16)
                        sp.wait_ge(v_kept, PRIME + n + 1)
                        for q in range(QUADS):
                            sp.dma_start(g.v_rows[bass.ds(i * QUADS + q, 1), :, s * TPC:(s + 1) * TPC, :].rearrange(
                                "o p t c -> p (o t) c"),
                                vrow[s][:, :, 4 * q:4 * q + 4, :].rearrange("p t h c -> p t (h c)")).then_inc(stored[s], 16)
                for s in range(2):
                    sp.wait_ge(stored[s], PRIME + 16 * B * (MC + QUADS))
                sp.wait_ge(zeros_out, PRIME + 16 * (E * CT // 4 + 1))

            @block.gpsimd
            def _(pool):
                prime(pool, primed)
                nc.gpsimd.memset(zeros[:, :], 0.0).then_inc(zeroed, 1)
                nc.gpsimd.memset(eps[:, :], EPS).then_inc(filled, 1)
                for s in range(2):
                    nc.gpsimd.memset(vrow[s][:, :, :, DH:VW], 1.0).then_inc(filled, 1)
                nc.gpsimd.memset(ones[:, :], 1.0).then_inc(filled, 1)
                nc.gpsimd.memset(limit[:, :], 0).then_inc(filled, 1)
                nc.gpsimd.memset(bit[:, :], 1 << (BITS - 1)).then_inc(filled, 1)
                nc.gpsimd.memset(resets[:, :, :], 1.0).then_inc(filled, 1)
                pool.wait_ge(filled, PRIME + 7)
                nc.gpsimd.affine_select(out=before[:, :], in_=ones[:, :], compare_op=ALU.is_gt, fill=0.0,
                                        base=0, pattern=[[1, P]], channel_multiplier=-1).then_inc(cut, 1)
                nc.gpsimd.memset(resets[:, :, 0:1], 0.0).then_inc(cut, 1)
                for e in range(E):
                    nc.gpsimd.memset(back[:, 0, e:e + 1], float(E - e)).then_inc(filled, 1)
                    nc.gpsimd.memset(base[:, e, :], float(e * CAP - E * CAP)).then_inc(filled, 1)

                def low_rows(n, i, s, c):
                    pool.wait_ge(xhi_done, PRIME + n + 1)
                    nc.gpsimd.tensor_tensor(xlo[s][:, c, :], turned_all[:, c, chunk(i, s)], xhi[s][:, c, :].bitcast(F32),
                                            ALU.subtract).then_inc(xlo_done, 1)

                def body(i, s, more):
                    n = i * 2 + s
                    for m in range(MC):
                        if 1 <= m <= KC and more:
                            low_rows(n + 1, i + s, 1 - s, m - 1)
                        pool.wait_ge(mid_done, PRIME + n * MC + m + 1)
                        nc.gpsimd.tensor_tensor(parts[s][:, m, 2, :], rest[m % 2][:, :], parts[s][:, m, 1, :],
                                                ALU.subtract).then_inc(lo_done, 1)

                for c in range(KC):
                    low_rows(0, 0, 0, c)
                rows(pool, body)

            @block.tensor
            def _(pe):
                pe.wait_ge(router_in, PRIME + 16)
                for c in range(KC):
                    nc.tensor.transpose(turned[0][:, 0, c * E:(c + 1) * E], rw[:, c * P:(c + 1) * P],
                                        g.ident[0:E, 0:E]).then_inc(rw_turned, 1)
                pe.wait_ge(rw_done, PRIME + 1)

                def turn(n, s):
                    pe.wait_ge(xn_done, PRIME + (n + 1) * TPC)
                    pe.wait_ge(xnT_done, PRIME + n - 1)
                    for t in range(TPC):
                        for c in range(KC):
                            mm = nc.tensor.transpose(turned[s][:, c, t * P:(t + 1) * P],
                                                     xn[s][:, t, c * P:(c + 1) * P], g.ident[:, :])
                    mm.then_inc(turned_done, 1)

                def route(n, i, s):
                    pe.wait_ge(xnT_done, PRIME + n + 1)
                    for t in range(TPC):
                        for c in range(KC):
                            mm = nc.tensor.matmul(lps[:, bass.ds(i * QT + s * TPC + t, 1), :].rearrange("p o e -> p (o e)"),
                                                  xnT[s][:, c, t * P:(t + 1) * P],
                                                  rwT[:, c, :], start=c == 0, stop=c == KC - 1)
                    mm.then_inc(logits_done, 1)

                turn(0, 0)
                with pe.Fori(0, B - 1) as i:
                    for s in range(2):
                        turn(i * 2 + s + 1, 1 - s)
                        route(i * 2 + s, i, s)
                turn(2 * B - 1, 1)
                for s in range(2):
                    route(2 * B - 2 + s, B - 1, s)

                def query_key(n, s, m):
                    pe.wait_ge(rest_done, PRIME + n * MC + m - 1)
                    cols = slice((m % KC) * P, (m % KC + 1) * P)
                    for c in range(KC):
                        mm = split_product(nc, qk[m % 2][:, :], (whi[:, m // KC, c, cols], wlo[:, m // KC, c, cols]),
                                           (xhi[s][:, c, :], xlo[s][:, c, :]), c == 0, c == KC - 1)
                    mm.then_inc(qk_done, 1)

                def body(i, s, more):
                    n = i * 2 + s
                    pe.wait_ge(xlo_done, PRIME + (n + 1) * KC)
                    query_key(n, s, 0)
                    for m in range(MC):
                        pe.wait_ge(trial_done, PRIME + n * MC + m + 1)
                        nc.tensor.matmul(counted[:, :], ones[:, :], count[:, :], start=True, stop=True).then_inc(count_done, 1)
                        if m < MC - 1:
                            query_key(n, s, m + 1)
                        if m == 0:
                            pe.wait_ge(v_kept, PRIME + n)
                        for t in VALUES[m]:
                            for c in range(KC):
                                cols = slice(t * P, (t + 1) * P)
                                mm = split_product(nc, vps[:, t, :], (xhi[s][:, c, cols], xlo[s][:, c, cols]),
                                                   (whi[:, 2, c, :], wlo[:, 2, c, :]), c == 0, c == KC - 1)
                            if t == TPC - 1:
                                mm.then_inc(v_done, 1)

                pe.wait_ge(wlo_done, PRIME + 3)
                pe.wait_ge(filled, PRIME + FILLS)
                pe.wait_ge(cut, PRIME + 2)
                rows(pe, body)
                pe.wait_ge(trial_done, PRIME + TRIALS + 1)
                nc.tensor.matmul(counted[:, :], ones[:, :], count[:, :], start=True, stop=True).then_inc(count_done, 1)
                pe.wait_ge(rest_done, PRIME + 2 * B * MC)
                for n, marks in enumerate((ties, kept)):
                    pe.wait_ge(prefix_in, PRIME + n + 1)
                    flat = marks[:, :, :].rearrange("p e t -> p (e t)")
                    nc.tensor.matmul(ranked, before[:, :], flat, start=True, stop=True)
                    nc.tensor.matmul(tiles, ones[:, :], flat, start=True, stop=True).then_inc(prefix_done, 1)

            @block.scalar
            def _(act):
                act.wait_ge(filled, PRIME + 3)

                def root(n, s):
                    act.wait_ge(var_done, PRIME + (n + 1) * TPC)
                    nc.scalar.activation(std[s][:, :], mv[s][:, :, 1], ACT.Sqrt, bias=eps[:, 0:1]).then_inc(std_done, 1)

                def copy_rows(n, i, s):
                    act.wait_ge(turned_done, PRIME + n + 1)
                    act.wait_ge(logits_done, PRIME + n - 1)
                    act.wait_ge(turned_kept, PRIME + n - 1)
                    nc.scalar.copy(xnT[s][:, :, :], turned[s][:, :, :]).then_inc(xnT_done, 1)
                    nc.scalar.copy(g.xn_all[:, tiles_of(i, s), :], xn[s][:, :, :]).then_inc(xn_kept, 1)

                root(0, 0)
                root(1, 1)
                with act.Fori(0, B - 1) as i:
                    for s in range(2):
                        copy_rows(i * 2 + s, i, s)
                        root(i * 2 + s + 2, s)
                for s in range(2):
                    copy_rows(2 * B - 2 + s, B - 1, s)
                act.wait_ge(weights_in, PRIME + 48)
                for m in range(3):
                    nc.scalar.copy(whi[:, m, :, :], wqkv[:, m, :, :]).then_inc(whi_done, 1)

                def high_rows(n, i, s):
                    act.wait_ge(turned_kept, PRIME + n + 1)
                    act.wait_ge(v_done, PRIME + n - 1)
                    nc.scalar.copy(xhi[s][:, :, :], turned_all[:, :, chunk(i, s)]).then_inc(xhi_done, 1)

                def mid(n, s, m):
                    act.wait_ge(rest_done, PRIME + n * MC + m + 1)
                    nc.scalar.copy(parts[s][:, m, 1, :], rest[m % 2][:, :]).then_inc(mid_done, 1)

                def body(i, s, more):
                    n = i * 2 + s
                    act.wait_ge(stored[s], PRIME + i * (16 * (MC + QUADS)))
                    for m in range(MC):
                        act.wait_ge(qk_done, PRIME + n * MC + m + 1)
                        nc.scalar.mul(parts[s][:, m, 0, :], qk[m % 2][:, :], DH ** -0.5 if m < KC else 1.0).then_inc(hi_done, 1)
                        if m:
                            mid(n, s, m - 1)
                        if m == 1 and more:
                            high_rows(n + 1, i + s, 1 - s)
                    act.wait_ge(v_done, PRIME + n + 1)
                    nc.scalar.copy(vrow[s][:, :, :, 0:DH], vps[:, :, :].rearrange("p t (h e) -> p t h e", e=DH)).then_inc(v_kept, 1)
                    mid(n, s, MC - 1)

                high_rows(0, 0, 0)
                act.wait_ge(shifted, PRIME + 1)
                nc.scalar.activation(prob[:, :, :], left[:, :, :], ACT.Exp).then_inc(exp_done, 1)
                rows(act, body)

            @block.vector
            def _(dve):
                def variance(n, i, s):
                    dve.wait_ge(x_in[s], PRIME + i * 16 + 16)
                    for t in range(TPC):
                        nc.vector.bn_stats(stats[s][:, t, :], g.xn_all[:, bass.ds(i * QT + s * TPC + t, 1), :].rearrange(
                            "p o d -> p (o d)")).then_inc(stats_done, 1)
                    dve.wait_ge(stats_done, PRIME + (n + 1) * TPC)
                    dve.sem_inc(tally, 1)
                    for t in range(TPC):
                        nc.vector.bn_aggr(mv[s][:, t, :], stats[s][:, t, :]).then_inc(var_done, 1)

                def normalise(n, i, s):
                    dve.wait_ge(std_done, PRIME + n + 1)
                    nc.vector.reciprocal(rstd[s][:, :], std[s][:, :]).then_inc(rstd_step, 1)
                    first = n * (NEWTON + 1)
                    dve.wait_ge(rstd_step, PRIME + first + 1)
                    nc.vector.tensor_tensor(newt[s][:, :], rstd[s][:, :], rstd[s][:, :], ALU.mult).then_inc(rstd_step, 1)
                    dve.wait_ge(rstd_step, PRIME + first + 2)
                    nc.vector.scalar_tensor_tensor(out=newt[s][:, :], in0=mv[s][:, :, 1], scalar=EPS, in1=newt[s][:, :],
                                                   op0=ALU.add, op1=ALU.mult).then_inc(rstd_step, 1)
                    dve.wait_ge(rstd_step, PRIME + first + 3)
                    nc.vector.tensor_scalar(newt[s][:, :], newt[s][:, :], -0.5, 1.5, ALU.mult, ALU.add).then_inc(rstd_step, 1)
                    dve.wait_ge(rstd_step, PRIME + first + 4)
                    nc.vector.tensor_tensor(rstd[s][:, :], rstd[s][:, :], newt[s][:, :], ALU.mult).then_inc(rstd_step, 1)
                    dve.wait_ge(rstd_step, PRIME + first + 5)
                    dve.wait_ge(xn_kept, PRIME + n - 1)
                    dve.wait_ge(turned_done, PRIME + n - 1)
                    for t in range(TPC):
                        nc.vector.tensor_scalar(xn[s][:, t, :], g.xn_all[:, bass.ds(i * QT + s * TPC + t, 1), :].rearrange(
                            "p o d -> p (o d)"), mv[s][:, t, 0:1], rstd[s][:, t:t + 1],
                            ALU.subtract, ALU.mult).then_inc(xn_done, 1)

                def keep(n, i, s):
                    dve.wait_ge(xnT_done, PRIME + n + 1)
                    nc.vector.tensor_copy(turned_all[:, :, chunk(i, s)], xnT[s][:, :, :]).then_inc(turned_kept, 1)

                variance(0, 0, 0)
                dve.wait_ge(rw_turned, PRIME + KC)
                nc.vector.tensor_copy(rwT[:, :, :], turned[0][:, 0, 0:KC * E].rearrange("p (c e) -> p c e", c=KC)).then_inc(rw_done, 1)
                variance(1, 0, 1)
                normalise(0, 0, 0)
                with dve.Fori(0, B - 1) as i:
                    for s in range(2):
                        n = i * 2 + s
                        normalise(n + 1, i + s, 1 - s)
                        variance(n + 2, i + 1, s)
                        keep(n, i, s)
                normalise(2 * B - 1, B - 1, 1)
                for s in range(2):
                    keep(2 * B - 2 + s, B - 1, s)
                for m in range(3):
                    dve.wait_ge(whi_done, PRIME + m + 1)
                    nc.vector.tensor_tensor(wlo[:, m, :, :], wqkv[:, m, :, :], whi[:, m, :, :].bitcast(F32),
                                            ALU.subtract).then_inc(wlo_done, 1)
                dve.wait_ge(logits_done, PRIME + 2 * B)
                nc.vector.tensor_copy(logits[:, :, :], lps[:, :, :]).then_inc(logits_kept, 1)

                chain = [PRIME]

                def link(ins):
                    chain[0] += 1
                    ins.then_inc(step, 1)
                    dve.wait_ge(step, chain[0])

                def by_expert(t):
                    return t[:, :, :].rearrange("p t e -> p e t")

                def over_experts(t):
                    return t[:, :].unsqueeze(2).broadcast_to([P, NT, E])

                def over_tiles(t):
                    return t[:, :].unsqueeze(2).broadcast_to([P, E, NT])

                dve.wait_ge(logits_kept, PRIME + 1)
                link(nc.vector.tensor_reduce(row[:, :], logits[:, :, :], AX.X, ALU.max))
                nc.vector.tensor_tensor(left[:, :, :], logits[:, :, :], over_experts(row), ALU.subtract).then_inc(shifted, 1)
                dve.wait_ge(exp_done, PRIME + 1)
                link(nc.vector.tensor_reduce(total[:, :], prob[:, :, :], AX.X, ALU.add))
                link(nc.vector.reciprocal(row[:, :], total[:, :]))
                link(nc.vector.tensor_tensor(prob[:, :, :], prob[:, :, :], over_experts(row), ALU.mult))
                dve.wait_ge(filled, PRIME + FILLS)
                dve.wait_ge(cut, PRIME + 2)
                backwards = back[:, :, :].broadcast_to([P, NT, E])
                now = prob
                for k in range(TOPK):
                    link(nc.vector.tensor_reduce(top[k][:, :], now[:, :, :], AX.X, ALU.max))
                    link(nc.vector.tensor_tensor(pick[:, :, :], now[:, :, :], over_experts(top[k]), ALU.is_equal))
                    link(nc.vector.tensor_tensor(pick[:, :, :], pick[:, :, :], backwards, ALU.mult))
                    link(nc.vector.tensor_reduce(row[:, :], pick[:, :, :], AX.X, ALU.max))
                    link(nc.vector.tensor_tensor(hot[k][:, :, :], backwards, over_experts(row), ALU.is_equal))
                    if k == 0:
                        link(nc.vector.scalar_tensor_tensor(out=left[:, :, :], in0=hot[0][:, :, :], scalar=-2.0,
                                                            in1=prob[:, :, :], op0=ALU.mult, op1=ALU.add))
                        now = left
                link(nc.vector.tensor_tensor(total[:, :], top[0][:, :], top[1][:, :], ALU.add))
                link(nc.vector.tensor_scalar(total[:, :], total[:, :], 1e-6, None, ALU.add))
                link(nc.vector.reciprocal(row[:, :], total[:, :]))
                for k in range(TOPK):
                    link(nc.vector.tensor_tensor(g.weights[:, k, :], top[k][:, :], row[:, :], ALU.mult))
                link(nc.vector.tensor_tensor(gate[:, :, :], hot[0][:, :, :], over_experts(g.weights[:, 0, :]), ALU.mult))
                link(nc.vector.tensor_tensor(pick[:, :, :], hot[1][:, :, :], over_experts(g.weights[:, 1, :]), ALU.mult))
                link(nc.vector.tensor_tensor(gate[:, :, :], gate[:, :, :], pick[:, :, :], ALU.add))
                link(nc.vector.scalar_tensor_tensor(out=pick[:, :, :], in0=hot[0][:, :, :], scalar=-1.0,
                                                    in1=hot[1][:, :, :], op0=ALU.add, op1=ALU.add))
                link(nc.vector.tensor_tensor(gate[:, :, :], gate[:, :, :], pick[:, :, :], ALU.add))

                def count_trial(done):
                    dve.wait_ge(trial_step, PRIME + done)
                    nc.vector.tensor_tensor(trial[:, :], limit[:, :], bit[:, :], ALU.bitwise_or).then_inc(trial_step, 1)
                    dve.wait_ge(trial_step, PRIME + done + 1)
                    nc.vector.tensor_tensor(over[:, :, :], by_expert(gate), over_tiles(trial[:, :].bitcast(F32)),
                                            ALU.is_ge).then_inc(trial_step, 1)
                    dve.wait_ge(trial_step, PRIME + done + 2)
                    with nc.allow_low_precision("counts of at most NT are exact in bfloat16"):
                        nc.vector.tensor_reduce(count[:, :], over[:, :, :], AX.X, ALU.add).then_inc(trial_done, 1)

                def body(i, s, more):
                    n = i * 2 + s
                    for m in range(MC):
                        done = 2 + (n * MC + m) * TRIALSTEPS
                        dve.wait_ge(hi_done, PRIME + n * MC + m + 1)
                        dve.wait_ge(lo_done, PRIME + n * MC + m - 1)
                        nc.vector.scalar_tensor_tensor(out=rest[m % 2][:, :], in0=qk[m % 2][:, :],
                                                       scalar=DH ** -0.5 if m < KC else 1.0,
                                                       in1=parts[s][:, m, 0, :], op0=ALU.mult,
                                                       op1=ALU.subtract).then_inc(rest_done, 1)
                        dve.wait_ge(count_done, PRIME + n * MC + m + 1)
                        nc.vector.scalar_tensor_tensor(out=grow[:, :], in0=counted[:, :], scalar=float(CAP), in1=bit[:, :],
                                                       op0=ALU.is_ge, op1=ALU.mult).then_inc(trial_step, 1)
                        nc.vector.tensor_scalar(bit[:, :], bit[:, :], 1, None, ALU.logical_shift_right).then_inc(trial_step, 1)
                        dve.wait_ge(trial_step, PRIME + done + 1)
                        nc.vector.tensor_tensor(limit[:, :], limit[:, :], grow[:, :], ALU.bitwise_or).then_inc(trial_step, 1)
                        if more or m < MC - 1:
                            count_trial(done + 3)

                count_trial(0)
                rows(dve, body)
                dve.wait_ge(trial_step, PRIME + TRIALS * TRIALSTEPS)
                bound = over_tiles(limit[:, :].bitcast(F32))
                link(nc.vector.tensor_tensor(above[:, :, :], by_expert(gate), bound, ALU.is_gt))
                with nc.allow_low_precision("counts of at most NT are exact in bfloat16"):
                    nc.vector.tensor_reduce(count[:, :], above[:, :, :], AX.X, ALU.add).then_inc(trial_done, 1)
                nc.vector.tensor_tensor(ties[:, :, :], by_expert(gate), bound, ALU.is_equal).then_inc(prefix_in, 1)
                dve.wait_ge(count_done, PRIME + TRIALS + 1)
                link(nc.vector.tensor_scalar(need[:, :], counted[:, :], -1.0, float(CAP), ALU.mult, ALU.add))

                def ranks(n):
                    dve.wait_ge(prefix_done, PRIME + n + 1)
                    link(nc.vector.tensor_copy(slot[:, :, :].rearrange("p e t -> p (e t)"), tiles))
                    link(nc.vector.tensor_tensor_scan(
                        start[:, :, :].rearrange("p e t -> p (e t)"), resets[:, :, :].rearrange("p e t -> p (e t)"),
                        slot[:, :, :].rearrange("p e t -> p (e t)"), 0.0, ALU.mult, ALU.add))
                    link(nc.vector.tensor_tensor(start[:, :, :], start[:, :, :], slot[:, :, :], ALU.subtract))
                    link(nc.vector.tensor_tensor(slot[:, :, :], ranked.rearrange("p (e t) -> p e t", e=E), start[:, :, :], ALU.add))

                ranks(0)
                link(nc.vector.tensor_tensor(slot[:, :, :], slot[:, :, :], over_tiles(need), ALU.is_lt))
                link(nc.vector.tensor_tensor(slot[:, :, :], slot[:, :, :], ties[:, :, :], ALU.mult))
                nc.vector.tensor_tensor(kept[:, :, :], above[:, :, :], slot[:, :, :], ALU.add).then_inc(prefix_in, 1)
                ranks(1)
                link(nc.vector.tensor_tensor(slot[:, :, :], slot[:, :, :], base[:, :, :].broadcast_to([P, E, NT]), ALU.add))
                link(nc.vector.tensor_tensor(slot[:, :, :], slot[:, :, :], kept[:, :, :], ALU.mult))
                for k in range(TOPK):
                    link(nc.vector.tensor_tensor(pick[:, :, :], hot[k][:, :, :], slot[:, :, :].rearrange("p e t -> p t e"), ALU.mult))
                    link(nc.vector.tensor_reduce(row[:, :], pick[:, :, :], AX.X, ALU.add))
                    link(nc.vector.tensor_scalar(g.slots[:, k, :], row[:, :], float(E * CAP), None, ALU.add))


STEPS = [(qc, j) for qc in range(L // BANK) for j in range((qc + 1) * TPC)]
NS = len(STEPS)
MASKED_STEPS = [s for s, (qc, j) in enumerate(STEPS) if j >= qc * TPC]
HALVES = [(3, 0), (0, 0), (7, 0), (6, 1), (4, 0), (1, 0), (5, 0), (5, 1), (7, 1), (2, 0), (6, 0), (4, 1)]
TILES = [(h, qt, half) for h in range(4) for qt, half in HALVES]
NTILE = len(TILES)
NSCORE = 3
NTURNED = 3
LAG = 2
FIRST_TILES = 8
TURN_MAX = 9
COPY_OUT = {TPC + LAG: 0, LAG: 1}
TURN_OUT = {TPC + LAG + 1: 0, LAG + 1: 1}
NORMALISE = {TPC + LAG + 2: 0, LAG + 2: 1}
LOAD_NEXT = LAG
TAIL = LAG + 3


def tiles_beside(s):
    ahead, n = (2, s - FIRST_TILES) if s >= FIRST_TILES else (1, s - FIRST_TILES + NS)
    return ahead, range(NTILE * n // NS, NTILE * (n + 1) // NS)


def exists(i, unit):
    return unit < 2 * QUADS if not isinstance(i, int) else 0 <= i * QUADS + unit < B * QUADS


PIECES = [(m, n) for m in range(2) for n in range(WCOLS // BANK)]
PIECE_AT = [TAIL + 1 + 2 * n for n in range(len(PIECES))]
EARLY = 20


def build_attend(nc, g, wg, wu):
    with ExitStack() as ctx:
        def sb(name, shape, dt):
            return ctx.enter_context(nc.sbuf_tensor(name, shape, dt))

        def psum(name, shape):
            return ctx.enter_context(nc.psum_tensor(name, shape, F32))

        primed = []

        def sem(name):
            primed.append(ctx.enter_context(nc.semaphore(name)))
            return primed[-1]

        qst = [sb(f"qst{q}", [STACK + MAXROWS, 4, L], BF16) for q in range(QUADS)]
        kst = [sb(f"kst{q}", [STACK + MAXROWS, 4, L], BF16) for q in range(QUADS)]
        vst = [sb(f"vst{q}", [P, QT, 4 * VW], F32) for q in range(QUADS)]
        probs = [sb(f"probs{n}", [P, 4, BANK], F32) for n in range(3)]
        rowmax = [sb(f"rowmax{n}", [P, 2, 4, QT], F32) for n in range(2)]
        maxrest = sb("maxrest", [P, 4, QT], F32)
        maxparts = sb("maxparts", [P, MAXROWS, 4, QT], BF16)
        maxturned = sb("maxturned", [MAXROWS * 4 * QT, P], BF16)
        outT = [sb(f"outT{n}", [P, BANK], F32) for n in range(2)]
        recip = sb("recip", [P, TPC, 4], F32)
        heads = [sb(f"heads{n}", [P, TPC, 4 * DH], F32) for n in range(2)]
        score = [psum(f"score{n}", [P, BANK]) for n in range(NSCORE)]
        scoreT = [psum(f"scoreT{n}", [P, BANK]) for n in range(NTURNED)]
        outps = psum("outps", [P, BANK])
        small = psum("small", [P, TPC, P])
        smallb = small[:, 0, :].bitcast(BF16)

        sent = ctx.enter_context(nc.semaphore("sent"))
        tally = sem("a_tally")
        expert_in = [ctx.enter_context(nc.semaphore(f"expert_in{m}")) for m in range(2)]
        first_queue_in = ctx.enter_context(nc.semaphore("first_queue_in"))
        expert_hi = ctx.enter_context(nc.semaphore("expert_hi"))
        expert_lo = ctx.enter_context(nc.semaphore("expert_lo"))
        ones_set = sem("ones_set")
        stack_in = [sem(f"stack_in{q}") for q in range(QUADS)]
        max_in = [sem(f"max_in{q}") for q in range(QUADS)]
        score_done = sem("score_done")
        max_done = sem("max_done")
        max_step = sem("max_step")
        max_turned = sem("max_turned")
        max_copied = sem("max_copied")
        scoreT_done = sem("scoreT_done")
        exp_done = sem("exp_done")
        mask_done = sem("mask_done")
        pv_done = sem("pv_done")
        out_copied = sem("out_copied")
        out_turned = sem("out_turned")
        heads_step = sem("heads_step")
        heads_out = [sem(f"heads_out{n}") for n in range(2)]
        LOADS = 2 * len(TERMS) + 1
        MAXSTEPS = 6

        def slots(eng, slot):
            for k in range(TAIL):
                slot(0, k)
            with eng.Fori(0, B - 1) as i:
                for k in range(TAIL, QUADS * NS + TAIL):
                    slot(i, k)
            for k in range(TAIL, QUADS * NS + TAIL):
                slot(B - 1, k)

        def load_term(eng, i, q, side, n):
            st, part = (qst, kst)[side], TERMS[n][side]
            eng.dma_start(st[q][n * DH:(n + 1) * DH, :, :],
                          g.qk_parts[side, part, 4 * DH * q:4 * DH * (q + 1), bass.ds(i * L, L)].rearrange(
                              "(h d) t -> d h t", d=DH)).then_inc(stack_in[q], 16)

        with nc.Block() as block:
            @block.sync
            def _(sp):
                def load(i, q, keys=True):
                    for n in range(len(TERMS)):
                        for side in range(1 + keys):
                            load_term(sp, i, q, side, n)
                    sp.dma_start(vst[q][:, :, :], g.v_rows[bass.ds(i * QUADS + q, 1), :, :, :].rearrange(
                        "o p t c -> p (o t) c")).then_inc(stack_in[q], 16)

                def max_rows(u, q):
                    sp.wait_ge(max_copied, PRIME + u + 1)
                    for r in range(MAXROWS):
                        sp.dma_start(qst[q][STACK + r:STACK + r + 1, :, :].rearrange("o h t -> o (h t)"),
                                     maxturned[r * 4 * QT:(r + 1) * 4 * QT, :]).then_inc(max_in[q], 16)

                def slot(i, k):
                    unit, s = k // NS, k % NS
                    u = i * QUADS + unit
                    if s == LOAD_NEXT and exists(i, unit - 1) and exists(i, unit + 3):
                        sp.wait_ge(scoreT_done, PRIME + u * 4 * NS)
                        sp.wait_ge(pv_done, PRIME + u * NS)
                        load(i + (unit + 3) // QUADS, (unit + 3) % QUADS)
                    if s in NORMALISE:
                        qc = NORMALISE[s]
                        if exists(i, unit - qc):
                            done = unit - qc
                            sp.wait_ge(heads_step, PRIME + ((i * QUADS + done) * 2 + qc + 1) * 2)
                            row, q = i + done // QUADS, done % QUADS
                            sp.dma_start(g.attn_rows[bass.ds(row * L + qc * BANK, BANK), 4 * DH * q:4 * DH * (q + 1)].rearrange(
                                "(t p) c -> p t c", p=P), heads[qc][:, :, :]).then_inc(heads_out[qc], 16)
                    if s == TURN_MAX and exists(i, unit + 1):
                        max_rows(u + 1, (unit + 1) % QUADS)
                    if isinstance(i, int) and i == B - 1 and k == QUADS * NS - 1:
                        sp.wait_ge(sent, 16 * NT * TOPK)
                        sp.dma_start(g.queue[:, :, :], g.queues[0:CAP, :].rearrange("(t p) d -> p t d", p=P)).then_inc(first_queue_in, 16)

                for q in range(QUADS):
                    load(0, q, keys=q > 0)
                max_rows(0, 0)
                for m, w in enumerate((wg, wu)):
                    sp.dma_start(g.raw(m).rearrange("p (c f) -> p c f", c=KC),
                                 w[0].rearrange("(c p) f -> p c f", p=P)).then_inc(expert_in[m], 16)
                slots(sp, slot)
                for qc in range(2):
                    sp.wait_ge(heads_out[qc], PRIME + 16 * B * QUADS)
                sp.wait_ge(first_queue_in, 16)

            @block.gpsimd
            def _(pool):
                prime(pool, primed)

                def send(n):
                    t, choice = n // TOPK, n % TOPK
                    nc.gpsimd.indirect_dma_start(
                        g.queues, bass.IndirectOffsetOnAxis(ap=g.slots[:, choice, t:t + 1], axis=0),
                        g.xn_all[:, t, :], None, bounds_check=E * CAP - 1, oob_is_err=False).then_inc(sent, 16)

                def slot(i, k):
                    unit, s = k // NS, k % NS
                    u = i * QUADS + unit
                    qc, j = STEPS[s]
                    last = isinstance(i, int) and i == B - 1
                    if last:
                        late, span = NT * TOPK - EARLY, (QUADS - 1) * NS
                        for n in range(late * (k - TAIL) // span, min(late, late * (k - TAIL + 1) // span)):
                            send(EARLY + n)
                    if s in MASKED_STEPS and exists(i, unit):
                        off = (j - qc * TPC) * P
                        pool.wait_ge(exp_done, PRIME + u * 4 * NS + 4 * (s + 1))
                        pool.sem_inc(tally, 1)
                        tile = probs[s % 3][:, :, off:off + P]
                        nc.gpsimd.affine_select(out=tile, in_=tile, compare_op=ALU.is_ge, fill=0.0, base=0,
                                                pattern=[[0, 4], [1, P]], channel_multiplier=-1).then_inc(mask_done, 1)
                    if last and k - 1 in PIECE_AT:
                        n = PIECE_AT.index(k - 1)
                        m, piece = PIECES[n]
                        cols = slice(piece * BANK, (piece + 1) * BANK)
                        pool.wait_ge(expert_hi, n + 1)
                        nc.gpsimd.tensor_tensor(g.parts(m)[1][:, cols], g.raw(m)[:, cols], g.parts(m)[0][:, cols].bitcast(F32),
                                                ALU.subtract).then_inc(expert_lo, 1)

                for q in range(QUADS // 2, QUADS):
                    nc.gpsimd.memset(kst[q][STACK:STACK + MAXROWS, :, :], 1.0).then_inc(ones_set, 1)
                for n in range(EARLY):
                    send(n)
                slots(pool, slot)
                pool.wait_ge(expert_lo, len(PIECES))
                pool.wait_ge(sent, 16 * NT * TOPK)

            @block.tensor
            def _(pe):
                def row_tile(row, u, q, t):
                    h, qt, half = TILES[t]
                    if t == 0:
                        pe.wait_ge(stack_in[q], PRIME + 16 * LOADS * (row + 1))
                    pe.wait_ge(max_done, PRIME + u * NTILE + t - NSCORE + 1)
                    k0 = half * BANK
                    width = min(BANK, (qt + 1) * P - k0)
                    diagonal = k0 + width == (qt + 1) * P
                    bank = score[t % NSCORE]
                    mm = nc.tensor.matmul(bank[:, 0:width], qst[q][0:STACK, h, qt * P:(qt + 1) * P],
                                          kst[q][0:STACK, h, k0:k0 + width], start=True, stop=not diagonal)
                    if diagonal:
                        mm = nc.tensor.matmul(bank[:, width - P:width], g.identb[:, :], g.maskneg[:, :],
                                              start=False, stop=True)
                    mm.then_inc(score_done, 1)

                def turn_max(u):
                    pe.wait_ge(max_step, PRIME + (u + 1) * MAXSTEPS)
                    pe.wait_ge(heads_step, PRIME + (2 * u - 1) * 2)
                    nc.tensor.transpose(smallb[0:MAXROWS * 4 * QT, 0:P],
                                        maxparts[:, :, :, :].rearrange("p r h t -> p (r h t)"),
                                        g.identb[:, :]).then_inc(max_turned, 1)

                def turn_out(u, qc):
                    pe.wait_ge(out_copied, PRIME + 2 * u + qc + 1)
                    pe.wait_ge(heads_step, PRIME + (2 * u + qc) * 2)
                    for t in range(TPC):
                        mm = nc.tensor.transpose(small[:, t, :], outT[qc][:, t * P:(t + 1) * P], g.ident[:, :])
                    mm.then_inc(out_turned, 1)

                def values(u, q, s):
                    qc, j = STEPS[s]
                    off = max(0, (j - qc * TPC) * P)
                    pe.wait_ge(exp_done, PRIME + u * 4 * NS + 4 * (s + 1))
                    if s in MASKED_STEPS:
                        pe.wait_ge(mask_done, PRIME + u * len(MASKED_STEPS) + MASKED_STEPS.index(s) + 1)
                    if j == 0:
                        pe.wait_ge(out_copied, PRIME + 2 * u + qc)
                    for h in range(4):
                        mm = nc.tensor.matmul(outps[32 * h:32 * h + VW, off:BANK], vst[q][:, j, h * VW:(h + 1) * VW],
                                              probs[s % 3][:, h, off:BANK], start=j == 0,
                                              stop=j == (qc + 1) * TPC - 1)
                    mm.then_inc(pv_done, 1)

                def slot(i, k):
                    unit, s = k // NS, k % NS
                    u, q, row = i * QUADS + unit, unit % QUADS, i + unit // QUADS
                    qc, j = STEPS[s]
                    off = max(0, (j - qc * TPC) * P)
                    ahead, tiles = tiles_beside(s)
                    tiles = list(tiles) if exists(i, unit + ahead) else []
                    ahead += unit
                    if s == 0 and exists(i, unit):
                        pe.wait_ge(max_in[q], PRIME + 16 * MAXROWS * (row + 1))
                    for h in range(4):
                        m = 4 * s + h
                        if exists(i, unit):
                            pe.wait_ge(exp_done, PRIME + u * 4 * NS + m - NTURNED + 1)
                            nc.tensor.matmul(scoreT[m % NTURNED][:, off:BANK], kst[q][:, h, j * P:(j + 1) * P],
                                             qst[q][:, h, qc * BANK + off:(qc + 1) * BANK],
                                             start=True, stop=True).then_inc(scoreT_done, 1)
                        if tiles:
                            row_tile(i + ahead // QUADS, i * QUADS + ahead, ahead % QUADS, tiles.pop(0))
                        if s == TURN_MAX and h == 0 and exists(i, unit + 1):
                            turn_max(u + 1)
                        if h == 2 and s >= LAG and exists(i, unit):
                            values(u, q, s - LAG)
                        if h == 2 and s < LAG and exists(i, unit - 1):
                            values(u - 1, (unit - 1) % QUADS, NS + s - LAG)
                    assert not tiles
                    if s in TURN_OUT and exists(i, unit - TURN_OUT[s]):
                        if s == LAG + 1:
                            pe.wait_ge(max_copied, PRIME + u + (1 if exists(i, unit) else 0))
                        turn_out(u - TURN_OUT[s], TURN_OUT[s])

                for t in range(NTILE):
                    row_tile(0, 0, 0, t)
                turn_max(0)
                for s in range(FIRST_TILES, NS):
                    for t in tiles_beside(s)[1]:
                        row_tile(0, 1, 1, t)
                pe.wait_ge(ones_set, PRIME + QUADS + 1)
                slots(pe, slot)

            @block.scalar
            def _(act):
                def copy_max(u):
                    act.wait_ge(max_turned, PRIME + u + 1)
                    nc.scalar.copy(maxturned[:, :], smallb[0:MAXROWS * 4 * QT, 0:P]).then_inc(max_copied, 1)

                def slot(i, k):
                    unit, s = k // NS, k % NS
                    u, row = i * QUADS + unit, i + unit // QUADS
                    qc, j = STEPS[s]
                    off = max(0, (j - qc * TPC) * P)
                    if s in COPY_OUT and exists(i, unit - COPY_OUT[s]):
                        half = COPY_OUT[s]
                        act.wait_ge(pv_done, PRIME + u * NS + (0 if half else TPC))
                        nc.scalar.copy(outT[half][:, :], outps[:, :]).then_inc(out_copied, 1)
                    if exists(i, unit):
                        act.wait_ge(pv_done, PRIME + u * NS + s - 2)
                        for h in range(4):
                            m = 4 * s + h
                            act.wait_ge(scoreT_done, PRIME + u * 4 * NS + m + 1)
                            nc.scalar.activation(probs[s % 3][:, h, off:BANK], scoreT[m % NTURNED][:, off:BANK],
                                                 ACT.Exp).then_inc(exp_done, 1)
                            if s == TURN_MAX and h == 1 and exists(i, unit + 1):
                                act.wait_ge(max_in[unit % QUADS], PRIME + 16 * MAXROWS * (row + 1))
                                copy_max(u + 1)
                    if isinstance(i, int) and i == B - 1 and k in PIECE_AT:
                        m, piece = PIECES[PIECE_AT.index(k)]
                        cols = slice(piece * BANK, (piece + 1) * BANK)
                        act.wait_ge(expert_in[m], 16)
                        nc.scalar.copy(g.parts(m)[0][:, cols], g.raw(m)[:, cols]).then_inc(expert_hi, 1)

                for n in range(len(TERMS)):
                    load_term(act, 0, 0, 1, n)
                copy_max(0)
                slots(act, slot)

            @block.vector
            def _(dve):
                def row_tile(u, unit, t):
                    h, qt, half = TILES[t]
                    dve.wait_ge(score_done, PRIME + u * NTILE + t + 1)
                    width = min(BANK, (qt + 1) * P - half * BANK)
                    nc.vector.tensor_reduce(rowmax[unit % 2][:, half, h, qt:qt + 1], score[t % NSCORE][:, 0:width],
                                            AX.X, ALU.max).then_inc(max_done, 1)

                def split_max(u, unit, step):
                    top = rowmax[unit % 2]
                    if step == 0:
                        dve.wait_ge(max_done, PRIME + (u + 1) * NTILE)
                    else:
                        dve.wait_ge(max_step, PRIME + u * MAXSTEPS + step)
                    if step == 0:
                        far = L // 2 // P
                        nc.vector.tensor_tensor(top[:, 0, :, far:QT], top[:, 0, :, far:QT], top[:, 1, :, far:QT],
                                                ALU.max).then_inc(max_step, 1)
                    if step == 1:
                        dve.wait_ge(max_turned, PRIME + u)
                        nc.vector.tensor_scalar(maxparts[:, 0, :, :], top[:, 0, :, :], -1.0, None, ALU.mult).then_inc(max_step, 1)
                    if step == 2:
                        nc.vector.scalar_tensor_tensor(out=maxrest[:, :, :], in0=top[:, 0, :, :], scalar=-1.0,
                                                       in1=maxparts[:, 0, :, :], op0=ALU.mult,
                                                       op1=ALU.subtract).then_inc(max_step, 1)
                    if step == 3:
                        nc.vector.tensor_copy(maxparts[:, 1, :, :], maxrest[:, :, :]).then_inc(max_step, 1)
                    if step == 4:
                        nc.vector.tensor_tensor(maxrest[:, :, :], maxrest[:, :, :], maxparts[:, 1, :, :],
                                                ALU.subtract).then_inc(max_step, 1)
                    if step == 5:
                        nc.vector.tensor_copy(maxparts[:, 2, :, :], maxrest[:, :, :]).then_inc(max_step, 1)

                def normalise(u, qc):
                    turned = small[:, :, :].rearrange("p t (h c) -> p (t h) c", h=4)
                    over = recip[:, :, :].rearrange("p t h -> p (t h)")
                    dve.wait_ge(out_turned, PRIME + 2 * u + qc + 1)
                    nc.vector.reciprocal(over, turned[:, :, DH]).then_inc(heads_step, 1)
                    dve.wait_ge(heads_step, PRIME + (2 * u + qc) * 2 + 1)
                    dve.wait_ge(heads_out[qc], PRIME + u * 16)
                    nc.vector.tensor_tensor(heads[qc][:, :, :].rearrange("p t (h c) -> p (t h) c", h=4),
                                            turned[:, :, 0:DH], over.unsqueeze(2).broadcast_to([P, TPC * 4, DH]),
                                            ALU.mult).then_inc(heads_step, 1)

                def slot(i, k):
                    unit, s = k // NS, k % NS
                    u = i * QUADS + unit
                    ahead, tiles = tiles_beside(s)
                    if s in NORMALISE and exists(i, unit - NORMALISE[s]):
                        normalise(u - NORMALISE[s], NORMALISE[s])
                    split = {FIRST_TILES - 1: [[], [], [], [0]], FIRST_TILES: [[1], [2], [3, 4, 5], []]}.get(s)
                    for n, t in enumerate(tiles):
                        if exists(i, unit + ahead):
                            row_tile(u + ahead, unit + ahead, t)
                        if split and exists(i, unit + 1):
                            for step in split[n]:
                                split_max(u + 1, unit + 1, step)

                for q in range(QUADS // 2):
                    nc.vector.memset(kst[q][STACK:STACK + MAXROWS, :, :], 1.0).then_inc(ones_set, 1)
                nc.vector.memset(outps[:, :], 0.0).then_inc(ones_set, 1)
                for t in range(NTILE):
                    row_tile(0, 0, t)
                for step in range(MAXSTEPS):
                    split_max(0, 0, step)
                for s in range(FIRST_TILES, NS):
                    for t in tiles_beside(s)[1]:
                        row_tile(1, 1, t)
                slots(dve, slot)


HALF = CAP // 2
NHALF = 2
GU = FC * NHALF


HID = 768
HC = HID // P
SCALE = 1.0 / 127.0


def build_experts(nc, g, wg, wu, wd, squares, integers):
    with ExitStack() as ctx:
        def sb(name, shape, dt=F32):
            return ctx.enter_context(nc.sbuf_tensor(name, shape, dt))

        def psum(name, shape):
            return ctx.enter_context(nc.psum_tensor(name, shape, F32))

        primed = []

        def sem(name):
            primed.append(ctx.enter_context(nc.semaphore(name)))
            return primed[-1]

        raw = [g.raw(0), g.raw(1), sb("raw2", [P, WCOLS])]
        whi = [[g.parts(m)[0] for m in range(MATS)], [sb(f"whi{m}", [P, WCOLS], F32R) for m in range(MATS)]]
        wlo = [[g.parts(m)[1] for m in range(MATS)], [sb(f"wlo{m}", [P, WCOLS], F32R) for m in range(MATS)]]
        queue = g.queue
        qhi = sb("qhi", [P, KC, CAP], F32R)
        qlo = sb("qlo", [P, KC, CAP], F32R)
        act_out = [sb(f"act_out{n}", [P, HALF]) for n in range(2)]
        hidden = [sb(f"hidden{n}", [P, HALF]) for n in range(2)]
        hhi = sb("hhi", [P, FC, CAP], F32R)
        hlo = sb("hlo", [P, FC, CAP], F32R)
        rows = [sb(f"rows{n}", [P, D]) for n in range(2)]
        gps = [psum(f"gps{n}", [P, BANK]) for n in range(2)]
        ups = [psum(f"ups{n}", [P, BANK]) for n in range(2)]
        dps = [psum(f"dps{n}", [P, BANK]) for n in range(2)]
        tps = [psum(f"tps{n}", [P, KC, P]) for n in range(2)]

        raw_in = [sem(f"raw_in{m}") for m in range(MATS)]
        queue_in = sem("queue_in")
        whi_done = [sem(f"whi_done{m}") for m in range(MATS)]
        wlo_done = [sem(f"wlo_done{m}") for m in range(MATS)]
        queue_turned = sem("queue_turned")
        qhi_done = sem("qhi_done")
        qlo_done = sem("qlo_done")
        gate_done = sem("gate_done")
        up_done = sem("up_done")
        silu_done = sem("silu_done")
        hidden_done = sem("hidden_done")
        hhi_done = sem("hhi_done")
        hlo_done = sem("hlo_done")
        down_done = sem("down_done")
        rows_done = sem("rows_done")
        rows_out = [sem(f"rows_out{n}") for n in range(2)]
        scaled_done = sem("scaled_done")
        next_turned = sem("next_turned")
        next_hi = sem("next_hi")
        next_lo = sem("next_lo")
        weights = (wg, wu, wd)
        WHOLE = HC * D
        groups = []
        for m in range(2):
            for c in range(KC):
                for f in range(0, HC, 2):
                    groups.append((m, [(f + k) * D + c * P for k in range(2)], c * HID + f * P))
        for f in range(HC):
            groups.append((2, [k * HID + f * P for k in range(2)], f * D))

        def beside(n):
            return range(len(groups) * n // GU, len(groups) * (n + 1) // GU)

        def pairs(eng, first, body):
            first()
            with eng.Fori(0, E // 2 - 1) as i:
                for s in range(2):
                    body(i * 2 + s, s, i, True)
            for s in range(2):
                body(E - 2 + s, s, E // 2 - 1, s == 0)

        with nc.Block() as block:
            @block.sync
            def _(sp):
                def load_weights(e):
                    for m in range(MATS):
                        sp.wait_ge(wlo_done[m], PRIME + e)
                        sp.dma_start(raw[m][:, :].rearrange("p (c f) -> p c f", c=KC if m < 2 else FC),
                                     weights[m][bass.ds(e, 1), :, :].rearrange("o (c p) f -> p (o c) f", p=P)).then_inc(raw_in[m], 16)

                def load_queue(e):
                    sp.wait_ge(queue_turned, PRIME + e * CT)
                    sp.dma_start(queue[:, :, :], g.queues[bass.ds(e * CAP, CAP), :].rearrange(
                        "(t p) d -> p t d", p=P)).then_inc(queue_in, 16)

                def store(e, t, n):
                    sp.wait_ge(rows_done, PRIME + e * CT + t + 1)
                    sp.dma_start(g.answers[bass.ds(e * CAP + t * P, P), :], rows[n][:, :]).then_inc(rows_out[n], 16)

                def body(e, s, i, more):
                    if more:
                        load_queue(e + 1)
                        load_weights(e + 1)
                    else:
                        load_next()
                    for t in range(CT):
                        store(e, t, (s + t) % 2)

                def load_next():
                    for m, (whole, square) in enumerate(zip(integers, squares)):
                        sp.wait_ge(wlo_done[m], PRIME + E)
                        sp.dma_start(raw[m][:, 0:WHOLE].bitcast(I32).rearrange("p (c d) -> p c d", c=HC if m < 2 else KC),
                                     whole.rearrange("(c p) d -> p c d", p=P)).then_inc(raw_in[m], 16)
                        sp.dma_start(raw[m][:, WHOLE:WCOLS].rearrange("p (c d) -> p c d", c=KC),
                                     square.rearrange("(c p) d -> p c d", p=P)).then_inc(raw_in[m], 16)

                def first():
                    sp.dma_start(raw[2][:, :].rearrange("p (c f) -> p c f", c=FC),
                                 wd[0].rearrange("(c p) f -> p c f", p=P)).then_inc(raw_in[2], 16)

                pairs(sp, first, body)
                for n in range(2):
                    sp.wait_ge(rows_out[n], PRIME + 16 * E * CT // 2)

            @block.gpsimd
            def _(pool):
                prime(pool, primed)
                pool.sem_inc(queue_in, 16)
                for m in range(2):
                    pool.sem_inc(raw_in[m], 16)
                    pool.sem_inc(whi_done[m], 1)
                    pool.sem_inc(wlo_done[m], 1)
                for m in range(MATS):
                    pool.wait_ge(raw_in[m], PRIME + 16 * (E + 2))
                    nc.gpsimd.tensor_scalar(raw[m][:, 0:WHOLE], raw[m][:, 0:WHOLE].bitcast(I32), SCALE, None,
                                            ALU.mult).then_inc(scaled_done, 1)

            @block.tensor
            def _(pe):
                def turn_next(n):
                    m, blocks, _ = groups[n]
                    pe.wait_ge(scaled_done, PRIME + m + 1)
                    pe.wait_ge(next_lo, PRIME + n - 1)
                    for k, col in enumerate(blocks):
                        mm = nc.tensor.transpose(tps[n % 2][:, k, :], raw[m][:, col:col + P], g.ident[:, :])
                    mm.then_inc(next_turned, 1)

                def turn_queue(e, t):
                    if t == 0:
                        pe.wait_ge(queue_in, PRIME + 16 * (e + 1))
                    pe.wait_ge(qlo_done, PRIME + e * CT + t - 1)
                    for c in range(KC):
                        mm = nc.tensor.transpose(tps[t % 2][:, c, :], queue[:, t, c * P:(c + 1) * P], g.ident[:, :])
                    mm.then_inc(queue_turned, 1)

                def gate_up(e, s, more):
                    for m in range(2):
                        pe.wait_ge(wlo_done[m], PRIME + e + 1)
                    pe.wait_ge(qlo_done, PRIME + (e + 1) * CT)
                    for n in range(GU):
                        f, half = n // NHALF, n % NHALF
                        cols = slice(half * HALF, (half + 1) * HALF)
                        pe.wait_ge(hidden_done, PRIME + e * GU + n - 1)
                        for m, (ps, done) in enumerate(((gps, gate_done), (ups, up_done))):
                            for c in range(KC):
                                w = slice(c * F + f * P, c * F + (f + 1) * P)
                                mm = split_product(nc, ps[n % 2][:, 0:HALF],
                                                   (whi[s][m][:, w], wlo[s][m][:, w]),
                                                   (qhi[:, c, cols], qlo[:, c, cols]), c == 0, c == KC - 1)
                            mm.then_inc(done, 1)
                        if not more:
                            for b in beside(n):
                                turn_next(b)

                def down(e, s, t):
                    if t == 0:
                        pe.wait_ge(wlo_done[2], PRIME + e + 1)
                        pe.wait_ge(hlo_done, PRIME + (e + 1) * GU - NHALF)
                    pe.wait_ge(rows_done, PRIME + e * CT + t - 1)
                    for f in range(FC):
                        if f == FC - 1 and t == 0:
                            pe.wait_ge(hlo_done, PRIME + (e + 1) * GU - 1)
                        if f == FC - 1 and t == HALF // P:
                            pe.wait_ge(hlo_done, PRIME + (e + 1) * GU)
                        w, h = slice(f * D, (f + 1) * D), slice(t * P, (t + 1) * P)
                        mm = split_product(nc, dps[(s + t) % 2][:, 0:D], (hhi[:, f, h], hlo[:, f, h]),
                                           (whi[s][2][:, w], wlo[s][2][:, w]), f == 0, f == FC - 1)
                    mm.then_inc(down_done, 1)

                def body(e, s, i, more):
                    gate_up(e, s, more)
                    if more:
                        turn_queue(e + 1, 0)
                    for t in range(CT):
                        if more and t + 1 < CT:
                            turn_queue(e + 1, t + 1)
                        down(e, s, t)

                def first():
                    for t in range(CT):
                        turn_queue(0, t)

                pairs(pe, first, body)

            @block.scalar
            def _(act):
                def split_weights(e, s, m):
                    act.wait_ge(raw_in[m], PRIME + 16 * (e + 1))
                    act.wait_ge(down_done, PRIME + (e - 1) * CT)
                    nc.scalar.copy(whi[s][m][:, :], raw[m][:, :]).then_inc(whi_done[m], 1)

                def split_queue(e, t):
                    act.wait_ge(queue_turned, PRIME + e * CT + t + 1)
                    if t == 0:
                        act.wait_ge(up_done, PRIME + e * GU)
                    nc.scalar.copy(qhi[:, :, t * P:(t + 1) * P], tps[t % 2][:, :, :]).then_inc(qhi_done, 1)

                def body(e, s, i, more):
                    for n in range(GU):
                        f, half = n // NHALF, n % NHALF
                        cols = slice(half * HALF, (half + 1) * HALF)
                        act.wait_ge(gate_done, PRIME + e * GU + n + 1)
                        act.wait_ge(hidden_done, PRIME + e * GU + n - 1)
                        nc.scalar.activation(act_out[n % 2][:, :], gps[n % 2][:, 0:HALF], ACT.Silu).then_inc(silu_done, 1)
                        act.wait_ge(hidden_done, PRIME + e * GU + n + 1)
                        if n == 0:
                            act.wait_ge(down_done, PRIME + e * CT)
                        nc.scalar.copy(hhi[:, f, cols], hidden[n % 2][:, :]).then_inc(hhi_done, 1)
                        if not more:
                            for b in beside(n):
                                m, _, col = groups[b]
                                act.wait_ge(next_turned, PRIME + b + 1)
                                nc.scalar.copy(whi[0][m][:, col:col + D], tps[b % 2][:, :, :].rearrange(
                                    "p k c -> p (k c)")).then_inc(next_hi, 1)
                    if more:
                        split_queue(e + 1, 0)
                    else:
                        for m in range(MATS):
                            nc.scalar.copy(whi[0][m][:, WHOLE:WCOLS], raw[m][:, WHOLE:WCOLS]).then_inc(next_hi, 1)
                    for t in range(CT):
                        if more and t + 1 < CT:
                            split_queue(e + 1, t + 1)
                        if more and t < MATS:
                            split_weights(e + 1, 1 - s, t)
                        act.wait_ge(down_done, PRIME + e * CT + t + 1)
                        act.wait_ge(rows_out[(s + t) % 2], PRIME + 16 * ROWS_OUT(e, s, t, i))
                        nc.scalar.copy(rows[(s + t) % 2][:, :], dps[(s + t) % 2][:, 0:D]).then_inc(rows_done, 1)

                def ROWS_OUT(e, s, t, i):
                    n = (s + t) % 2
                    return i * CT + sum(1 for ss in range(s + 1) for tt in range(CT if ss < s else t) if (ss + tt) % 2 == n)

                def first():
                    for t in range(CT):
                        split_queue(0, t)
                    act.wait_ge(raw_in[2], PRIME + 16)
                    nc.scalar.copy(whi[0][2][:, :], raw[2][:, :]).then_inc(whi_done[2], 1)

                pairs(act, first, body)

            @block.vector
            def _(dve):
                def split_weights(e, s, m):
                    dve.wait_ge(whi_done[m], PRIME + e + 1)
                    nc.vector.tensor_tensor(wlo[s][m][:, :], raw[m][:, :], whi[s][m][:, :].bitcast(F32),
                                            ALU.subtract).then_inc(wlo_done[m], 1)

                def split_queue(e, t):
                    dve.wait_ge(qhi_done, PRIME + e * CT + t + 1)
                    nc.vector.tensor_tensor(qlo[:, :, t * P:(t + 1) * P], tps[t % 2][:, :, :],
                                            qhi[:, :, t * P:(t + 1) * P].bitcast(F32), ALU.subtract).then_inc(qlo_done, 1)

                def body(e, s, i, more):
                    for n in range(GU):
                        f, half = n // NHALF, n % NHALF
                        cols = slice(half * HALF, (half + 1) * HALF)
                        dve.wait_ge(silu_done, PRIME + e * GU + n + 1)
                        dve.wait_ge(up_done, PRIME + e * GU + n + 1)
                        dve.wait_ge(hlo_done, PRIME + e * GU + n - 1)
                        nc.vector.tensor_tensor(hidden[n % 2][:, :], act_out[n % 2][:, :], ups[n % 2][:, 0:HALF],
                                                ALU.mult).then_inc(hidden_done, 1)
                        dve.wait_ge(hidden_done, PRIME + e * GU + n + 1)
                        dve.wait_ge(hhi_done, PRIME + e * GU + n + 1)
                        nc.vector.tensor_tensor(hlo[:, f, cols], hidden[n % 2][:, :], hhi[:, f, cols].bitcast(F32),
                                                ALU.subtract).then_inc(hlo_done, 1)
                        if not more:
                            for b in beside(n):
                                m, _, col = groups[b]
                                dve.wait_ge(next_hi, PRIME + b + 1)
                                nc.vector.tensor_tensor(wlo[0][m][:, col:col + D], tps[b % 2][:, :, :].rearrange("p k c -> p (k c)"),
                                                        whi[0][m][:, col:col + D].bitcast(F32), ALU.subtract).then_inc(next_lo, 1)
                    if more:
                        split_queue(e + 1, 0)
                        for t in range(1, CT):
                            split_queue(e + 1, t)
                            if t <= MATS:
                                split_weights(e + 1, 1 - s, t - 1)
                    else:
                        for m in range(MATS):
                            dve.wait_ge(next_hi, PRIME + len(groups) + m + 1)
                            nc.vector.tensor_tensor(wlo[0][m][:, WHOLE:WCOLS], raw[m][:, WHOLE:WCOLS],
                                                    whi[0][m][:, WHOLE:WCOLS].bitcast(F32), ALU.subtract).then_inc(next_lo, 1)

                def first():
                    for t in range(CT):
                        split_queue(0, t)
                    dve.wait_ge(whi_done[2], PRIME + 1)
                    nc.vector.tensor_tensor(wlo[0][2][:, :], raw[2][:, :], whi[0][2][:, :].bitcast(F32),
                                            ALU.subtract).then_inc(wlo_done[2], 1)

                pairs(dve, first, body)


def build_finish(nc, g, x, b_in, log_A, B_vec, Dv, out):
    with ExitStack() as ctx:
        def sb(name, shape, dt=F32):
            return ctx.enter_context(nc.sbuf_tensor(name, shape, dt))

        def psum(name, shape):
            return ctx.enter_context(nc.psum_tensor(name, shape, F32))

        primed = []

        def sem(name):
            primed.append(ctx.enter_context(nc.semaphore(name)))
            return primed[-1]

        def two(name, shape, dt=F32):
            return [sb(f"{name}{s}", shape, dt) for s in range(2)]

        def matrix(m, first, chunks, cols):
            return [part[:, first:first + chunks * cols].rearrange("p (c d) -> p c d", c=chunks) for part in g.parts(m)]

        gateT, upT, downT = matrix(0, 0, KC, HID), matrix(1, 0, KC, HID), matrix(2, 0, HC, D)
        wout, win, cmat = [matrix(m, HC * D, KC, D) for m in range(3)]
        vecs = sb("vecs", [P, 3, KC])
        decay = sb("decay", [P, KC])
        dmat = sb("dmat", [P, 1, D])
        projected = sb("projected", [P, NT, D])
        xrow = [g.fresh[:, 0, s * TPC * D:(s + 1) * TPC * D].rearrange("p (t d) -> p t d", d=D) for s in range(2)]
        answer = [two(f"answer{k}", [P, TPC, D]) for k in range(TOPK)]
        index = two("index", [P, TOPK, TPC], U32)
        share = two("share", [P, TOPK, TPC])
        gate1, gate2 = [g.fresh[:, 1, n * TPC * D:(n + 1) * TPC * D].rearrange("p (t d) -> p t d", d=D) for n in range(2)]
        stats = sb("fstats", [P, TPC, 6])
        mv = sb("fmv", [P, TPC, 2])
        var = sb("fvar", [P, TPC])
        power = sb("power", [P, TPC])
        rstd_power = sb("rstd_power", [P, TPC])
        rstd = sb("frstd", [P, TPC])
        newt = sb("fnewt", [P, TPC])
        xn = two("fxn", [P, TPC, D])
        side = two("side", [P, TPC, D])
        xhi, xlo = two("xhi", [P, KC, CHUNK], F32R), two("xlo", [P, KC, CHUNK], F32R)
        drive = sb("drive", [P, KC, CHUNK])
        state = two("state", [P, KC, CHUNK])
        shi, slo = sb("shi", [P, KC, CHUNK], F32R), sb("slo", [P, KC, CHUNK], F32R)
        act_out = two("fact_out", [P, CHUNK])
        hidden = two("fhidden", [P, CHUNK])
        hhi, hlo = sb("fhhi", [P, HC, CHUNK], F32R), sb("fhlo", [P, HC, CHUNK], F32R)
        tps = psum("ftps", [P, KC, CHUNK])
        yps = psum("yps", [P, TPC, D])
        gate_bank, up_bank = psum("gate_bank", [P, 2, CHUNK]), psum("up_bank", [P, 2, CHUNK])
        gps, ups = [[bank[:, n, :] for n in range(2)] for bank in (gate_bank, up_bank)]
        attn = [state[s][:, :, :].rearrange("p c (a d) -> p (c a) d", d=D) for s in range(2)]
        ahi, alo = [[part[:, s * KC:(s + 1) * KC, :] for s in range(2)] for part in (hhi, hlo)]
        attn_ps = [tps, gate_bank]
        proj_ps = [yps, up_bank[:, :, :].rearrange("p b (a d) -> p (b a) d", d=D)]

        tally = sem("f_tally")
        vecs_in = sem("vecs_in")
        decay_step = sem("decay_step")
        attn_in = [sem(f"attn_in{s}") for s in range(2)]
        x_in = [sem(f"fx_in{s}") for s in range(2)]
        index_set = sem("index_set")
        index_tally = sem("index_tally")
        answers_in = [ctx.enter_context(nc.semaphore(f"answers_in{s}")) for s in range(2)]
        share_set = sem("share_set")
        mix_step = sem("mix_step")
        gate1_done = sem("gate1_done")
        attn_turned = sem("attn_turned")
        ahi_done = sem("ahi_done")
        alo_done = sem("alo_done")
        proj_done = sem("proj_done")
        proj_kept = sem("proj_kept")
        x1_step = sem("x1_step")
        ln_step = sem("ln_step")
        power_set = sem("power_set")
        power_done = sem("power_done")
        xn_done = sem("fxn_done")
        xn_turned = sem("xn_turned")
        xhi_done = sem("xhi_done")
        xlo_done = sem("xlo_done")
        side_done = sem("side_done")
        drive_in = sem("drive_in")
        drive_done = sem("drive_done")
        state_done = sem("state_done")
        shi_done = sem("shi_done")
        slo_done = sem("slo_done")
        recur_done = sem("recur_done")
        recur_kept = sem("recur_kept")
        gate_done = sem("fgate_done")
        up_done = sem("fup_done")
        silu_done = sem("fsilu_done")
        hidden_done = sem("fhidden_done")
        hhi_done = sem("fhhi_done")
        hlo_done = sem("fhlo_done")
        ffn_done = sem("ffn_done")
        gate2_done = sem("gate2_done")
        out_step = sem("out_step")
        out_stored = [sem(f"out_stored{s}") for s in range(2)]
        LN = 7

        def steps(eng, first, body):
            first()
            with eng.Fori(0, B - 1) as i:
                for s in range(2):
                    body(i * 2 + s, s, i, True)
            for s in range(2):
                body((B - 1) * 2 + s, s, B - 1, s == 0)

        def turn(s, i):
            return i if s == 0 else i + 1

        def portions(more):
            return [slice(0, TPC)] if more else [slice(0, TPC // 2), slice(TPC // 2, TPC)]

        def last_row(i):
            return isinstance(i, int) and i == B - 1

        with nc.Block() as block:
            @block.sync
            def _(sp):
                def rows_of(n):
                    return bass.ds(n * CHUNK, CHUNK)

                def load_attn(n, s):
                    sp.wait_ge(attn_turned, PRIME + n - 1)
                    sp.dma_start(attn[s][:, :, :], g.attn_rows[rows_of(n), :].rearrange("(t p) d -> p t d", p=P)).then_inc(attn_in[s], 16)

                def load_x(n, s):
                    sp.wait_ge(x1_step, PRIME + (n - 1) * 2)
                    sp.dma_start(xrow[s][:, :, :], x[rows_of(n), :].rearrange("(t p) d -> p t d", p=P)).then_inc(x_in[s], 16)

                def body(n, s, i, more):
                    if not last_row(i):
                        load_x(n + 2, s)
                    for k, tiles in enumerate(portions(more)):
                        sp.wait_ge(out_step, PRIME + (n + 1 + k) * 2)
                        sp.dma_start(out[rows_of(n), :].rearrange("(t p) d -> p t d", p=P)[:, tiles, :],
                                     side[s][:, tiles, :]).then_inc(out_stored[s], 16)

                def first():
                    load_attn(0, 0)
                    load_attn(1, 1)
                    load_x(0, 0)
                    for n, v in enumerate((b_in, B_vec, log_A)):
                        sp.dma_start(vecs[:, n, :], v.rearrange("(c p) -> p c", p=P),
                                     allow_slow_non_contiguous=True).then_inc(vecs_in, 16)
                    sp.dma_start(dmat[:, 0, :], Dv.unsqueeze(0).broadcast_to([P, D])).then_inc(vecs_in, 16)
                    load_x(1, 1)
                    with sp.Fori(1, B) as i:
                        for s in range(2):
                            load_attn(i * 2 + s, s)

                steps(sp, first, body)
                for s in range(2):
                    sp.wait_ge(out_stored[s], PRIME + 16 * (B + s))

            @block.gpsimd
            def _(pool):
                prime(pool, primed)

                def gather(n, s, i):
                    pool.wait_ge(gate1_done, PRIME + n - 1)
                    if not (isinstance(i, int) and i == 0):
                        pool.wait_ge(answers_in[s], 16 * TOPK * TPC * i)
                    nc.gpsimd.tensor_copy(index[s][:, :, :], g.slots[:, :, bass.ds(n * TPC, TPC)]).then_inc(index_set, 1)
                    pool.wait_ge(index_set, PRIME + n + 1)
                    pool.sem_inc(index_tally, 1)
                    for k in range(TOPK):
                        for t in range(TPC):
                            nc.gpsimd.indirect_dma_start(
                                answer[k][s][:, t, :], None, g.answers,
                                bass.IndirectOffsetOnAxis(ap=index[s][:, k, t:t + 1], axis=0)).then_inc(answers_in[s], 16)

                def front(n, s, i):
                    pool.wait_ge(ln_step, PRIME + n * LN + 3)
                    nc.gpsimd.tensor_tensor(power[:, :], var[:, :], rstd_power[:, :], ALU.pow).then_inc(power_done, 1)
                    pool.wait_ge(xn_done, PRIME + (n + 1) * TPC)
                    pool.wait_ge(out_stored[s], PRIME + 16 * i)
                    nc.gpsimd.tensor_tensor(side[s][:, :, :], xn[s][:, :, :], dmat[:, :, :].broadcast_to([P, TPC, D]),
                                            ALU.mult).then_inc(side_done, 1)

                def body(n, s, i, more):
                    if not last_row(i):
                        gather(n + 2, s, i + 1)
                    if more:
                        front(n + 1, 1 - s, turn(s, i))

                def first():
                    gather(0, 0, 0)
                    nc.gpsimd.memset(rstd_power[:, :], -0.5).then_inc(power_set, 1)
                    pool.wait_ge(power_set, PRIME + 1)
                    gather(1, 1, 0)
                    pool.wait_ge(vecs_in, PRIME + 64)
                    front(0, 0, 0)

                steps(pool, first, body)

            @block.tensor
            def _(pe):
                def turn_attn(n, s, i):
                    pe.wait_ge(attn_in[s], PRIME + 16 * (i + 1))
                    pe.wait_ge(alo_done, PRIME + n - 1)
                    for t in range(TPC):
                        for c in range(KC):
                            mm = nc.tensor.transpose(attn_ps[s][:, c, t * P:(t + 1) * P], attn[s][:, t, c * P:(c + 1) * P], g.ident[:, :])
                    mm.then_inc(attn_turned, 1)

                def rows_product(out_ps, hi, lo, w, chunks, tiles=range(TPC)):
                    for t in tiles:
                        for c in range(chunks):
                            cols = slice(t * P, (t + 1) * P)
                            mm = split_product(nc, out_ps[:, t, :], (hi[:, c, cols], lo[:, c, cols]),
                                               (w[0][:, c, :], w[1][:, c, :]), c == 0, c == chunks - 1)
                    return mm

                def project(n, s):
                    pe.wait_ge(alo_done, PRIME + n + 1)
                    pe.wait_ge(proj_kept, PRIME + n - 1)
                    rows_product(proj_ps[s], ahi[s], alo[s], wout, KC).then_inc(proj_done, 1)

                def turn_xn(n, s):
                    pe.wait_ge(xn_done, PRIME + (n + 1) * TPC)
                    pe.wait_ge(drive_done, PRIME + n * KC)
                    for t in range(TPC):
                        for c in range(KC):
                            mm = nc.tensor.transpose(tps[:, c, t * P:(t + 1) * P], xn[s][:, t, c * P:(c + 1) * P], g.ident[:, :])
                    mm.then_inc(xn_turned, 1)

                def recurrence_input(n, s):
                    pe.wait_ge(xlo_done, PRIME + n + 1)
                    for e in range(KC):
                        for c in range(KC):
                            mm = split_product(nc, tps[:, e, :], (win[0][:, c, e * P:(e + 1) * P], win[1][:, c, e * P:(e + 1) * P]),
                                               (xhi[s][:, c, :], xlo[s][:, c, :]), c == 0, c == KC - 1)
                    mm.then_inc(drive_in, 1)

                def recurrence_output(n):
                    pe.wait_ge(slo_done, PRIME + n + 1)
                    pe.wait_ge(gate2_done, PRIME + n)
                    rows_product(yps, shi, slo, cmat, KC).then_inc(recur_done, 1)

                def gate_up(n, s, f):
                    pe.wait_ge(hidden_done, PRIME + n * HC + f - 1)
                    for ps, w, done in ((gps, gateT, gate_done), (ups, upT, up_done)):
                        for c in range(KC):
                            cols = slice(f * P, (f + 1) * P)
                            mm = split_product(nc, ps[f % 2][:, :], (w[0][:, c, cols], w[1][:, c, cols]),
                                               (xhi[s][:, c, :], xlo[s][:, c, :]), c == 0, c == KC - 1)
                        mm.then_inc(done, 1)

                def down(n, more):
                    pe.wait_ge(hlo_done, PRIME + (n + 1) * HC)
                    pe.wait_ge(recur_kept, PRIME + n + 1)
                    for tiles in portions(more):
                        rows_product(yps, hhi, hlo, downT, HC, range(TPC)[tiles]).then_inc(ffn_done, 1)

                def body(n, s, i, more):
                    for f in range(3):
                        gate_up(n, s, f)
                    recurrence_output(n)
                    gate_up(n, s, 3)
                    if more:
                        turn_xn(n + 1, 1 - s)
                    gate_up(n, s, 4)
                    gate_up(n, s, 5)
                    if more:
                        recurrence_input(n + 1, 1 - s)
                    down(n, more)

                def first():
                    turn_attn(0, 0, 0)
                    with pe.Fori(0, B - 1) as i:
                        for s in range(2):
                            turn_attn(i * 2 + s + 1, 1 - s, turn(s, i))
                            project(i * 2 + s, s)
                    turn_attn(2 * B - 1, 1, B - 1)
                    for s in range(2):
                        project(2 * B - 2 + s, s)
                    pe.wait_ge(proj_kept, PRIME + 2 * B)
                    turn_xn(0, 0)
                    recurrence_input(0, 0)

                steps(pe, first, body)

            @block.scalar
            def _(act):
                def gate_first(n, s):
                    act.wait_ge(mix_step, PRIME + (n + 1) * 2 * TPC)
                    act.wait_ge(x1_step, PRIME + n * 2)
                    nc.scalar.activation(gate1[:, :, :], answer[0][s][:, :, :], ACT.Silu).then_inc(gate1_done, 1)

                def attn_hi(n, s):
                    act.wait_ge(attn_turned, PRIME + n + 1)
                    act.wait_ge(proj_done, PRIME + n - 1)
                    nc.scalar.copy(ahi[s], attn_ps[s][:, :, :]).then_inc(ahi_done, 1)

                def keep_projection(n, s):
                    act.wait_ge(proj_done, PRIME + n + 1)
                    nc.scalar.copy(projected[:, bass.ds(n * TPC, TPC), :], proj_ps[s][:, :, :]).then_inc(proj_kept, 1)

                def projections(first, last):
                    with act.Fori(first, last) as i:
                        for s in range(2):
                            attn_hi(i * 2 + s + 1, 1 - s)
                            keep_projection(i * 2 + s, s)

                def xn_hi(n, s):
                    act.wait_ge(xn_turned, PRIME + n + 1)
                    act.wait_ge(up_done, PRIME + (n - 1) * HC)
                    nc.scalar.copy(xhi[s][:, :, :], tps[:, :, :]).then_inc(xhi_done, 1)

                def state_hi(n, s):
                    act.wait_ge(state_done, PRIME + (n + 1) * KC)
                    act.wait_ge(recur_done, PRIME + n)
                    nc.scalar.copy(shi[:, :, :], state[s][:, :, :]).then_inc(shi_done, 1)

                def silu(n, f):
                    act.wait_ge(gate_done, PRIME + n * HC + f + 1)
                    act.wait_ge(hidden_done, PRIME + n * HC + f - 1)
                    nc.scalar.activation(act_out[f % 2][:, :], gps[f % 2][:, :], ACT.Silu).then_inc(silu_done, 1)
                    act.wait_ge(hidden_done, PRIME + n * HC + f + 1)
                    if f == 0:
                        act.wait_ge(ffn_done, PRIME + n)
                    nc.scalar.copy(hhi[:, f, :], hidden[f % 2][:, :]).then_inc(hhi_done, 1)

                def gate_second(n, more):
                    for k, tiles in enumerate(portions(more)):
                        act.wait_ge(ffn_done, PRIME + n + 1 + k)
                        act.wait_ge(out_step, PRIME + n * 2)
                        nc.scalar.activation(gate2[:, tiles, :], yps[:, tiles, :], ACT.Silu).then_inc(gate2_done, 1)

                def body(n, s, i, more):
                    if more:
                        gate_first(n + 1, 1 - s)
                    for f in range(4):
                        silu(n, f)
                    if more:
                        xn_hi(n + 1, 1 - s)
                    for f in range(4, HC):
                        silu(n, f)
                    if more:
                        state_hi(n + 1, 1 - s)
                    gate_second(n, more)

                def first():
                    act.wait_ge(vecs_in, PRIME + 64)
                    nc.scalar.activation(decay[:, :], vecs[:, 2, :], ACT.Exp).then_inc(decay_step, 1)
                    attn_hi(0, 0)
                    projections(0, B // 2)
                    gate_first(0, 0)
                    projections(B // 2, B - 1)
                    attn_hi(2 * B - 1, 1)
                    for s in range(2):
                        keep_projection(2 * B - 2 + s, s)
                    xn_hi(0, 0)
                    state_hi(0, 0)

                steps(act, first, body)

            @block.vector
            def _(dve):
                def mix(n, s, i):
                    nc.vector.tensor_copy(share[s][:, :, :], g.weights[:, :, bass.ds(n * TPC, TPC)]).then_inc(share_set, 1)
                    dve.wait_ge(share_set, PRIME + n + 1)
                    dve.wait_ge(answers_in[s], 16 * TOPK * TPC * (i + 1))
                    for t in range(TPC):
                        nc.vector.tensor_scalar(answer[0][s][:, t, :], answer[0][s][:, t, :], share[s][:, 0, t:t + 1], None,
                                                ALU.mult).then_inc(mix_step, 1)
                    for t in range(TPC):
                        dve.wait_ge(mix_step, PRIME + n * 2 * TPC + TPC + t)
                        nc.vector.scalar_tensor_tensor(out=answer[0][s][:, t, :], in0=answer[1][s][:, t, :],
                                                       scalar=share[s][:, 1, t:t + 1], in1=answer[0][s][:, t, :],
                                                       op0=ALU.mult, op1=ALU.add).then_inc(mix_step, 1)

                def attn_lo(n, s):
                    dve.wait_ge(ahi_done, PRIME + n + 1)
                    nc.vector.tensor_tensor(alo[s], attn_ps[s][:, :, :], ahi[s].bitcast(F32), ALU.subtract).then_inc(alo_done, 1)

                def add_first(n, s, i):
                    dve.wait_ge(proj_kept, PRIME + n + 1)
                    dve.wait_ge(gate1_done, PRIME + n + 1)
                    dve.wait_ge(x_in[s], PRIME + 16 * (i + 1))
                    nc.vector.tensor_tensor(gate1[:, :, :], projected[:, bass.ds(n * TPC, TPC), :], gate1[:, :, :],
                                            ALU.mult).then_inc(x1_step, 1)
                    dve.wait_ge(x1_step, PRIME + 2 * n + 1)
                    nc.vector.tensor_tensor(projected[:, bass.ds(n * TPC, TPC), :], xrow[s][:, :, :], gate1[:, :, :],
                                            ALU.add).then_inc(x1_step, 1)

                def x1_tile(n, t):
                    return projected[:, bass.ds(n * TPC + t, 1), :].rearrange("p o d -> p (o d)")

                def variance(n, s):
                    base = n * LN
                    dve.wait_ge(x1_step, PRIME + 2 * n + 2)
                    dve.sem_inc(tally, 1)
                    for t in range(TPC):
                        last = nc.vector.bn_stats(stats[:, t, :], x1_tile(n, t))
                    last.then_inc(ln_step, 1)
                    dve.wait_ge(ln_step, PRIME + base + 1)
                    dve.sem_inc(tally, 1)
                    for t in range(TPC):
                        last = nc.vector.bn_aggr(mv[:, t, :], stats[:, t, :])
                    last.then_inc(ln_step, 1)
                    dve.wait_ge(ln_step, PRIME + base + 2)
                    nc.vector.tensor_scalar(var[:, :], mv[:, :, 1], EPS, None, ALU.add).then_inc(ln_step, 1)

                def root(n, s):
                    base = n * LN
                    dve.wait_ge(power_done, PRIME + n + 1)
                    nc.vector.tensor_tensor(newt[:, :], power[:, :], power[:, :], ALU.mult).then_inc(ln_step, 1)
                    dve.wait_ge(ln_step, PRIME + base + 4)
                    nc.vector.tensor_tensor(newt[:, :], newt[:, :], var[:, :], ALU.mult).then_inc(ln_step, 1)
                    dve.wait_ge(ln_step, PRIME + base + 5)
                    nc.vector.tensor_scalar(newt[:, :], newt[:, :], -0.5, 1.5, ALU.mult, ALU.add).then_inc(ln_step, 1)
                    dve.wait_ge(ln_step, PRIME + base + 6)
                    nc.vector.tensor_tensor(rstd[:, :], power[:, :], newt[:, :], ALU.mult).then_inc(ln_step, 1)

                def scale_rows(n, s):
                    dve.wait_ge(ln_step, PRIME + n * LN + 7)
                    dve.wait_ge(xn_turned, PRIME + n - 1)
                    dve.wait_ge(side_done, PRIME + n - 1)
                    for t in range(TPC):
                        nc.vector.tensor_scalar(xn[s][:, t, :], x1_tile(n, t), mv[:, t, 0:1], rstd[:, t:t + 1],
                                                ALU.subtract, ALU.mult).then_inc(xn_done, 1)

                def xn_lo(n, s):
                    dve.wait_ge(xhi_done, PRIME + n + 1)
                    nc.vector.tensor_tensor(xlo[s][:, :, :], tps[:, :, :], xhi[s][:, :, :].bitcast(F32), ALU.subtract).then_inc(xlo_done, 1)

                def recur(n, s):
                    dve.wait_ge(drive_in, PRIME + n + 1)
                    for e in range(KC):
                        nc.vector.tensor_scalar(drive[:, e, :], tps[:, e, :], vecs[:, 0, e:e + 1], vecs[:, 1, e:e + 1],
                                                ALU.add, ALU.mult).then_inc(drive_done, 1)
                    for e in range(KC):
                        dve.wait_ge(drive_done, PRIME + n * KC + e + 1)
                        nc.vector.tensor_tensor_scan(state[s][:, e, :], decay[:, e:e + 1].broadcast_to([P, CHUNK]), drive[:, e, :],
                                                     0.0 if s == 0 else state[0][:, e, CHUNK - 1:CHUNK],
                                                     ALU.mult, ALU.add).then_inc(state_done, 1)
                    dve.wait_ge(shi_done, PRIME + n + 1)
                    nc.vector.tensor_tensor(slo[:, :, :], state[s][:, :, :], shi[:, :, :].bitcast(F32), ALU.subtract).then_inc(slo_done, 1)

                def keep_recurrence(n, s):
                    dve.wait_ge(recur_done, PRIME + n + 1)
                    dve.wait_ge(side_done, PRIME + n + 1)
                    nc.vector.tensor_tensor(side[s][:, :, :], yps[:, :, :], side[s][:, :, :], ALU.add).then_inc(recur_kept, 1)

                def hidden_row(n, f):
                    dve.wait_ge(silu_done, PRIME + n * HC + f + 1)
                    dve.wait_ge(up_done, PRIME + n * HC + f + 1)
                    dve.wait_ge(hlo_done, PRIME + n * HC + f - 1)
                    nc.vector.tensor_tensor(hidden[f % 2][:, :], act_out[f % 2][:, :], ups[f % 2][:, :], ALU.mult).then_inc(hidden_done, 1)

                def hidden_lo(n, f):
                    dve.wait_ge(hidden_done, PRIME + n * HC + f + 1)
                    dve.wait_ge(hhi_done, PRIME + n * HC + f + 1)
                    nc.vector.tensor_tensor(hlo[:, f, :], hidden[f % 2][:, :], hhi[:, f, :].bitcast(F32), ALU.subtract).then_inc(hlo_done, 1)

                def add_second(n, s, more):
                    dve.wait_ge(recur_kept, PRIME + n + 1)
                    for k, tiles in enumerate(portions(more)):
                        dve.wait_ge(gate2_done, PRIME + n + 1 + k)
                        nc.vector.tensor_tensor(side[s][:, tiles, :], side[s][:, tiles, :], gate2[:, tiles, :],
                                                ALU.mult).then_inc(out_step, 1)
                        dve.wait_ge(out_step, PRIME + 2 * (n + k) + 1)
                        nc.vector.tensor_tensor(side[s][:, tiles, :], side[s][:, tiles, :],
                                                projected[:, bass.ds(n * TPC + tiles.start, tiles.stop - tiles.start), :],
                                                ALU.add).then_inc(out_step, 1)

                def body(n, s, i, more):
                    for f in range(HC):
                        hidden_row(n, f)
                        if f == 0 and more:
                            add_first(n + 1, 1 - s, turn(s, i))
                        if f == 1 and more:
                            variance(n + 1, 1 - s)
                        if f == 2 and more:
                            root(n + 1, 1 - s)
                            scale_rows(n + 1, 1 - s)
                        if f == 3:
                            keep_recurrence(n, s)
                        if f == 4 and more:
                            xn_lo(n + 1, 1 - s)
                        hidden_lo(n, f)
                    if more:
                        recur(n + 1, 1 - s)
                    if not last_row(i):
                        mix(n + 2, s, i + 1)
                    add_second(n, s, more)

                def first():
                    dve.wait_ge(decay_step, PRIME + 1)
                    nc.vector.tensor_scalar(decay[:, :], decay[:, :], -1.0, None, ALU.mult).then_inc(decay_step, 1)
                    dve.wait_ge(decay_step, PRIME + 2)
                    for n in range(2 * B):
                        attn_lo(n, n % 2)
                        if n == 1:
                            mix(0, 0, 0)
                        if n == B:
                            add_first(0, 0, 0)
                        if n == B + 1:
                            variance(0, 0)
                        if n == B + 2:
                            root(0, 0)
                            scale_rows(0, 0)
                        if n == B + 3:
                            mix(1, 1, 0)
                    xn_lo(0, 0)
                    recur(0, 0)

                steps(dve, first, body)


def build(nc, ins, out):
    g = Shared()
    (x, Wq, Wk, Wv, Wout, router_w, wg, wu, wd, W_in, b_in, log_A, B_vec, C, Dv, w_gate, w_up, w_down) = ins
    x = x.rearrange("b l d -> (b l) d")
    out = out.rearrange("b l d -> (b l) d")
    g.qk_parts = nc.dram_tensor("qk_parts", [2, PARTS, H * DH, N], BF16, kind="Internal").ap()
    g.v_rows = nc.dram_tensor("v_rows", [B * QUADS, P, QT, 4 * VW], F32, kind="Internal").ap()
    g.queues = nc.dram_tensor("queues", [E * CAP, D], F32, kind="Internal").ap()
    g.answers = nc.dram_tensor("answers", [E * CAP + P, D], F32, kind="Internal").ap()
    g.attn_rows = nc.dram_tensor("attn_rows", [N, D], F32, kind="Internal").ap()
    with ExitStack() as ctx:
        g.weights = ctx.enter_context(nc.sbuf_tensor("weights", [P, TOPK, NT], F32))
        g.slots = ctx.enter_context(nc.sbuf_tensor("slots", [P, TOPK, NT], U32))
        build_constants(nc, ctx, g)
        g.fresh = ctx.enter_context(nc.sbuf_tensor("fresh", [P, 2, WCOLS], F32))
        g.split = ctx.enter_context(nc.sbuf_tensor("split", [P, 2 * MATS, WCOLS], F32R))
        with nc.sbuf_tensor("queue", [P, CT, D], F32) as g.queue:
            with nc.sbuf_tensor("xn_all", [P, NT, D], F32) as g.xn_all:
                build_project(nc, g, x, Wq, Wk, Wv, router_w)
                build_attend(nc, g, wg, wu)
            build_experts(nc, g, wg, wu, wd, (Wout.rearrange("h e d -> (h e) d"), W_in, C), (w_gate, w_up, w_down))
        build_finish(nc, g, x, b_in, log_A, B_vec, Dv, out)
    return g


_INS = ["L0_attn_x", "L0_attn_Wq", "L0_attn_Wk", "L0_attn_Wv", "L0_attn_Wout", "L0_ffn_router_w", "L0_ffn_wg",
        "L0_ffn_wu", "L0_ffn_wd", "L1_attn_W_in", "L1_attn_b_in", "L1_attn_log_A", "L1_attn_B_vec", "L1_attn_C",
        "L1_attn_D", "L1_ffn_w_gate", "L1_ffn_w_up", "L1_ffn_w_down"]


def kernel(**inputs):
    import numpy as _np
    import concourse.bacc as _bacc
    from concourse import mybir as _mybir
    from concourse.bass_utils import run_bass_kernel_spmd as _run

    nc = _bacc.Bacc("TRN2", target_bir_lowering=False, num_devices=1)
    arrays, args = {}, []
    for name in _INS:
        a = _np.ascontiguousarray(inputs[name])
        arrays[f"in_{name}"] = a
        args.append(nc.dram_tensor(f"in_{name}", a.shape, _mybir.dt.from_np(a.dtype), kind="ExternalInput").ap())
    out = nc.dram_tensor("out", (B, L, D), F32, kind="ExternalOutput").ap()
    build(nc, args, out)
    r = _run(nc, [arrays], core_ids=[0])
    return r.results[0]["out"]
```
